# Optimizing a Trainium2 kernel written in Bass

```python
import numpy as np
import jax
import jax.numpy as jnp

def _softmax(x, axis=-1):
    return jax.nn.softmax(x, axis=axis)

def _gelu(x):
    return jax.nn.gelu(x, approximate=True)

def _silu(x):
    return jax.nn.silu(x)

def _sigmoid(x):
    return jax.nn.sigmoid(x)

def _layernorm(x, axis=-1, eps=1e-05):
    m = jnp.mean(x, axis=axis, keepdims=True)
    v = jnp.var(x, axis=axis, keepdims=True)
    return (x - m) / jnp.sqrt(v + eps)

def _scatter_add(tgt, idx, src, axis=0):
    return tgt.at[idx].add(src)

def _segment_sum(src, seg, n):
    return jax.ops.segment_sum(src, seg, n)
kernel_name = 'mk_decoder_postln_d4_seqx_r8_121335'

def setup_inputs(seed: int=0):
    np.random.seed(seed)
    _w = jnp.asarray

    def _rec_inputs():
        import jax
        import jax.numpy as jnp
        _rk = jax.random.key(seed)
        x = -0.0003929 + 0.9999 * jax.random.normal(jax.random.fold_in(_rk, 1), (32, 100, 128), jnp.float32)
        _lenS = 100 - jax.random.randint(jax.random.fold_in(_rk, 7), (32,), 0, max(1, 100 // 4) + 1, jnp.int32)
        _lenS2 = 1444 - jax.random.randint(jax.random.fold_in(_rk, 8), (32,), 0, max(1, 1444 // 4) + 1, jnp.int32)
        _ctx_2048P = jax.random.normal(jax.random.fold_in(_rk, 11), (32, 16, 256), jnp.float32)
        _ctx_2048c = jax.random.dirichlet(jax.random.fold_in(_rk, 511), 0.3 * jnp.ones((16,), jnp.float32), (32, 1444))
        _ctx_2048t = jnp.einsum('bsk,bkd->bsd', _ctx_2048c, _ctx_2048P)
        _ctx_2048t = _ctx_2048t * jax.lax.rsqrt(jnp.mean(jnp.square(_ctx_2048t)) + 1e-12) * 0.953939
        ctx_2048 = 4.13588e-05 + 0.999923 * (_ctx_2048t + 0.3 * jax.random.normal(jax.random.fold_in(_rk, 611), (32, 1444, 256), jnp.float32))
        _validS = jnp.arange(100)[None, :] < _lenS[:, None]
        _validS2 = jnp.arange(1444)[None, :] < _lenS2[:, None]
        _causal = jnp.tril(jnp.ones((100, 100), dtype=bool))
        mask_BxS2_if0 = jnp.where(jnp.ones((32, 1444), dtype=bool), 4, 0).astype(jnp.int32)
        mask_BxS2_ik0 = jnp.where(jnp.broadcast_to(_validS2[:, :], (32, 1444)), 0, 1).astype(jnp.int32)
        return (x, ctx_2048, mask_BxS2_if0, mask_BxS2_ik0)
    x, ctx_2048, mask_BxS2_if0, mask_BxS2_ik0 = _rec_inputs()

    def _L0_attn_setup():
        import jax, jax.numpy as jnp
        import numpy as np
        D_MODEL = 128
        H = 16
        DH = D_MODEL // H
        WIN = 7
        PAD = WIN // 2
        B, L = (2, 512)
        key = jax.random.key(seed)
        ks = jax.random.split(key, 12)
        s = lambda k, shape: jax.random.normal(k, shape, dtype=jnp.float32) * 0.02
        return {'x': jax.random.normal(ks[0], (B, L, D_MODEL), dtype=jnp.float32), 'wq': s(ks[1], (D_MODEL, D_MODEL)), 'wk': s(ks[2], (D_MODEL, D_MODEL)), 'wv': s(ks[3], (D_MODEL, D_MODEL)), 'wo': s(ks[4], (D_MODEL, D_MODEL)), 'bo': s(ks[5], (D_MODEL,)), 'cw1': s(ks[6], (H, 32, 1)), 'cb1': s(ks[7], (H, 32)), 'cw2': s(ks[8], (H, 32, 32)), 'cb2': s(ks[9], (H, 32)), 'cw3': s(ks[10], (H, 1, 32)), 'cb3': s(ks[11], (H, 1))}
    _L0_attn_all = _L0_attn_setup()
    _L0_attn_in = {k: v for k, v in _L0_attn_all.items() if k in ('wq', 'wk', 'wv', 'wo', 'bo', 'cw1', 'cb1', 'cw2', 'cb2', 'cw3', 'cb3')}
    del _L0_attn_all

    def _L0_xattn_setup():
        import jax, jax.numpy as jnp
        import numpy as np
        B, L, P = (4, 512, 128)
        D_MODEL = 128
        D_GLOBAL = 256
        HEADDIM = 32
        EPSILON = 0.001
        RMS_EPS = 1e-05

        def rmsnorm(x, g, eps=RMS_EPS):
            var = jnp.mean(jnp.square(x), axis=-1, keepdims=True)
            return x * jax.lax.rsqrt(var + eps) * g

        def _hnet_depool(h, h_patch_full, patch_lens):
            h_patch = h_patch_full[..., :D_MODEL]
            bsz, plen = (h_patch.shape[0], h_patch.shape[1])
            seqlen = h.shape[1]
            logp = jnp.full((bsz, plen), -EPSILON, dtype=jnp.float32)
            bidx = jnp.cumsum(patch_lens, axis=1) - 1
            boundary_mask = jnp.zeros((bsz, seqlen), dtype=jnp.int32)
            boundary_mask = boundary_mask.at[jnp.arange(bsz)[:, None], bidx].set(1)
            dt = (-jnp.log(-jnp.expm1(logp))).astype(h_patch.dtype)
            x = h_patch / dt[..., None]
            n_heads = D_MODEL // HEADDIM
            A = -jnp.ones((n_heads,), dtype=jnp.float32)
            bcoef = jnp.exp(logp).astype(h_patch.dtype)
            x4 = x.reshape(bsz, plen, n_heads, HEADDIM)
            a = jnp.exp(dt[:, :, None] * A[None, None, :])
            u = (dt * bcoef)[:, :, None, None] * x4
            a_b = jnp.broadcast_to(a[..., None], u.shape)

            def comb(lft, rgt):
                aL, uL = lft
                aR, uR = rgt
                return (aL * aR, uL * aR + uR)
            _, s = jax.lax.associative_scan(comb, (a_b, u), axis=1)
            depool = s.reshape(bsz, plen, D_MODEL)
            plug = jnp.clip(jnp.cumsum(boundary_mask, axis=1) - 1, 0, plen - 1)
            depool_out = depool[jnp.arange(bsz)[:, None], plug]
            return depool_out + h
        key = jax.random.key(seed)
        k1, k2, k3, k4 = jax.random.split(key, 4)
        embeds = jax.random.normal(k1, (B, L, D_MODEL), dtype=jnp.float32)
        patch_embeds = jax.random.normal(k2, (B, P, D_GLOBAL), dtype=jnp.float32)
        patch_lens = jnp.full((B, P), L // P, dtype=jnp.int64)
        W_in = jax.random.normal(k3, (D_MODEL, D_MODEL), dtype=jnp.float32) * 0.02
        b_in = jnp.zeros((D_MODEL,), dtype=jnp.float32)
        g_res = jnp.ones((D_MODEL,), dtype=jnp.float32)
        g_init = jnp.ones((D_GLOBAL,), dtype=jnp.float32)
        return {'embeds': embeds, 'patch_embeds': patch_embeds, 'patch_lens': patch_lens, 'W_in': W_in, 'b_in': b_in, 'g_res': g_res, 'g_init': g_init}
    _L0_xattn_all = _L0_xattn_setup()
    _L0_xattn_in = {k: v for k, v in _L0_xattn_all.items() if k in ('W_in', 'b_in', 'g_res', 'g_init')}
    del _L0_xattn_all

    def _L0_ffn_setup():
        import jax, jax.numpy as jnp
        import numpy as np
        B, S, D = (4, 512, 128)
        E, F_EXP = (16, 256)
        F_C = 2.0
        F_SH = 256
        key = jax.random.key(seed)
        ks = jax.random.split(key, 8)
        s = 0.02
        return {'hidden_states': jax.random.normal(ks[0], (B, S, D), jnp.float32), 'gate_w': jax.random.normal(ks[1], (E, D), jnp.float32) * s, 'Wg': jax.random.normal(ks[2], (E, F_EXP, D), jnp.float32) * s, 'Wu': jax.random.normal(ks[3], (E, F_EXP, D), jnp.float32) * s, 'Wd': jax.random.normal(ks[4], (E, D, F_EXP), jnp.float32) * s, 'Ws_g': jax.random.normal(ks[5], (F_SH, D), jnp.float32) * s, 'Ws_u': jax.random.normal(ks[6], (F_SH, D), jnp.float32) * s, 'Ws_d': jax.random.normal(ks[7], (D, F_SH), jnp.float32) * s}
    _L0_ffn_all = _L0_ffn_setup()
    _L0_ffn_in = {k: v for k, v in _L0_ffn_all.items() if k in ('gate_w', 'Wg', 'Wu', 'Wd', 'Ws_g', 'Ws_u', 'Ws_d')}
    del _L0_ffn_all

    def _L1_attn_setup():
        import jax, jax.numpy as jnp
        import numpy as np
        import math
        B, L, HID = (2, 512, 128)
        NH, DK, DV = (12, 64, 128)
        KD, VD, CS = (NH * DK, NH * DV, 4)
        SCALE = DK ** (-0.5)

        def _causal_depthwise_conv(x, w):
            c, k = w.shape
            xt = jnp.transpose(x, (0, 2, 1))
            out = jax.lax.conv_general_dilated(xt, w[:, None, :], window_strides=(1,), padding=[(k - 1, 0)], feature_group_count=c, dimension_numbers=('NCH', 'OIH', 'NCH'))
            return jnp.transpose(out, (0, 2, 1))

        def _l2norm(x, eps=1e-06):
            return x * jax.lax.rsqrt(jnp.sum(x * x, axis=-1, keepdims=True) + eps)

        def _gated_delta_net(hidden_states, Wq, Wk, Wv, Wg, Wo, conv_q, conv_k, conv_v, Wgk, Wb, b_b, A_log, dt_bias, g_norm_weight):
            b, l, _ = hidden_states.shape
            q = jax.nn.silu(_causal_depthwise_conv(hidden_states @ Wq, conv_q))
            k = jax.nn.silu(_causal_depthwise_conv(hidden_states @ Wk, conv_k))
            v = jax.nn.silu(_causal_depthwise_conv(hidden_states @ Wv, conv_v))
            gk = -jnp.exp(A_log) * jax.nn.softplus(hidden_states @ Wgk + dt_bias)
            beta = jax.nn.sigmoid(hidden_states @ Wb + b_b)
            q = jnp.transpose(q.reshape(b, l, NH, DK), (0, 2, 1, 3))
            k = jnp.transpose(k.reshape(b, l, NH, DK), (0, 2, 1, 3))
            v = jnp.transpose(v.reshape(b, l, NH, DV), (0, 2, 1, 3))
            q = _l2norm(q) * SCALE
            k = _l2norm(k)
            qs = jnp.moveaxis(q, 2, 0)
            ks_ = jnp.moveaxis(k, 2, 0)
            vs = jnp.moveaxis(v, 2, 0)
            bs = jnp.moveaxis(beta, 1, 0)
            gs = jnp.moveaxis(gk, 1, 0)

            def step(S, inp):
                qt, kt, vt, bt, gt = inp
                S = S * jnp.exp(gt)[..., None, None]
                kv = jnp.einsum('bhk,bhkv->bhv', kt, S)
                delta = (vt - kv) * bt[..., None]
                S = S + jnp.einsum('bhk,bhv->bhkv', kt, delta)
                ot = jnp.einsum('bhk,bhkv->bhv', qt, S)
                return (S, ot)
            S0 = jnp.zeros((b, NH, DK, DV), hidden_states.dtype)
            _, os_ = jax.lax.scan(step, S0, (qs, ks_, vs, bs, gs))
            o = jnp.moveaxis(os_, 0, 1)
            g = (hidden_states @ Wg).reshape(b, l, NH, DV)
            var = jnp.mean(o * o, axis=-1, keepdims=True)
            o = o * jax.lax.rsqrt(var + 1e-05) * g_norm_weight
            o = o * g * jax.nn.sigmoid(g)
            return o.reshape(b, l, VD) @ Wo
        key = jax.random.key(seed)
        ks = jax.random.split(key, 16)
        rn = lambda i, shape, s: jax.random.normal(ks[i], shape, jnp.float32) * s
        hidden_states = rn(0, (B, L, HID), 1.0)
        Wq = rn(1, (HID, KD), HID ** (-0.5))
        Wk = rn(2, (HID, KD), HID ** (-0.5))
        Wv = rn(3, (HID, VD), HID ** (-0.5))
        Wg = rn(4, (HID, VD), HID ** (-0.5))
        Wo = rn(5, (VD, HID), VD ** (-0.5))
        conv_q = rn(6, (KD, CS), 0.5)
        conv_k = rn(7, (KD, CS), 0.5)
        conv_v = rn(8, (VD, CS), 0.5)
        Wgk = rn(9, (HID, NH), HID ** (-0.5))
        Wb = rn(10, (HID, NH), HID ** (-0.5))
        b_b = rn(11, (NH,), 0.1)
        A = jax.random.uniform(ks[12], (NH,), jnp.float32, 0.5, 16.0)
        A_log = jnp.log(A)
        dt = jnp.exp(jax.random.uniform(ks[13], (NH,), jnp.float32) * (math.log(0.1) - math.log(0.001)) + math.log(0.001))
        dt = jnp.clip(dt, 0.0001, None)
        dt_bias = dt + jnp.log(-jnp.expm1(-dt))
        g_norm_weight = jnp.ones((DV,), jnp.float32)
        return dict(hidden_states=hidden_states, Wq=Wq, Wk=Wk, Wv=Wv, Wg=Wg, Wo=Wo, conv_q=conv_q, conv_k=conv_k, conv_v=conv_v, Wgk=Wgk, Wb=Wb, b_b=b_b, A_log=A_log, dt_bias=dt_bias, g_norm_weight=g_norm_weight)
    _L1_attn_all = _L1_attn_setup()
    _L1_attn_in = {k: v for k, v in _L1_attn_all.items() if k in ('Wq', 'Wk', 'Wv', 'Wg', 'Wo', 'conv_q', 'conv_k', 'conv_v', 'Wgk', 'Wb', 'b_b', 'A_log', 'dt_bias', 'g_norm_weight')}
    del _L1_attn_all

    def _L1_xattn_setup():
        import jax, jax.numpy as jnp
        import numpy as np
        NUM_HEADS = 16
        key = jax.random.key(seed)
        ks = jax.random.split(key, 5)
        dim = 128
        B, N, N_c = (4, 128, 32)
        x = jax.random.normal(ks[0], (B, N, dim), dtype=jnp.float32)
        context = jax.random.normal(ks[1], (B, N_c, 2 * dim), dtype=jnp.float32)
        w_qkv = jax.random.normal(ks[2], (3 * dim, dim), dtype=jnp.float32) * 0.02
        w_proj = jax.random.normal(ks[3], (dim, dim), dtype=jnp.float32) * 0.02
        b_proj = jax.random.normal(ks[4], (dim,), dtype=jnp.float32) * 0.02
        return {'x': x, 'context': context, 'w_qkv': w_qkv, 'w_proj': w_proj, 'b_proj': b_proj}
    _L1_xattn_all = _L1_xattn_setup()
    _L1_xattn_in = {k: v for k, v in _L1_xattn_all.items() if k in ('w_qkv', 'w_proj', 'b_proj')}
    del _L1_xattn_all

    def _L1_ffn_setup():
        import jax, jax.numpy as jnp
        import numpy as np
        NUM_EXPERTS = 8
        HIDDEN = 128
        FFN = 512
        BATCH = 2
        SEQ = 256
        key = jax.random.key(seed)
        k_x, k_g, k_u, k_d = jax.random.split(key, 4)
        scale_in = 1.0 / np.sqrt(HIDDEN)
        scale_mid = 1.0 / np.sqrt(FFN)
        return {'hidden_states': jax.random.normal(k_x, (BATCH, SEQ, HIDDEN), dtype=jnp.float32), 'Wg': jax.random.normal(k_g, (NUM_EXPERTS, HIDDEN, FFN), dtype=jnp.float32) * scale_in, 'Wu': jax.random.normal(k_u, (NUM_EXPERTS, HIDDEN, FFN), dtype=jnp.float32) * scale_in, 'Wd': jax.random.normal(k_d, (NUM_EXPERTS, FFN, HIDDEN), dtype=jnp.float32) * scale_mid}
    _L1_ffn_all = _L1_ffn_setup()
    _L1_ffn_in = {k: v for k, v in _L1_ffn_all.items() if k in ('Wg', 'Wu', 'Wd')}
    del _L1_ffn_all

    def _L2_attn_setup():
        import jax, jax.numpy as jnp
        import numpy as np
        B, N, D = (8, 512, 128)
        key = jax.random.key(seed)
        k1, k2 = jax.random.split(key)
        x = jax.random.normal(k1, (B, N, D), dtype=jnp.float32)
        t = jax.random.normal(k2, (N, D), dtype=jnp.float32)
        return {'x': x, 't': t}
    _L2_attn_all = _L2_attn_setup()
    _L2_attn_in = {k: v for k, v in _L2_attn_all.items() if k in ('t',)}
    del _L2_attn_all

    def _L2_xattn_setup():
        import jax, jax.numpy as jnp
        import numpy as np
        NUM_HEADS = 16
        key = jax.random.key(seed)
        ks = jax.random.split(key, 5)
        dim = 128
        B, N, N_c = (4, 128, 32)
        x = jax.random.normal(ks[0], (B, N, dim), dtype=jnp.float32)
        context = jax.random.normal(ks[1], (B, N_c, 2 * dim), dtype=jnp.float32)
        w_qkv = jax.random.normal(ks[2], (3 * dim, dim), dtype=jnp.float32) * 0.02
        w_proj = jax.random.normal(ks[3], (dim, dim), dtype=jnp.float32) * 0.02
        b_proj = jax.random.normal(ks[4], (dim,), dtype=jnp.float32) * 0.02
        return {'x': x, 'context': context, 'w_qkv': w_qkv, 'w_proj': w_proj, 'b_proj': b_proj}
    _L2_xattn_all = _L2_xattn_setup()
    _L2_xattn_in = {k: v for k, v in _L2_xattn_all.items() if k in ('w_qkv', 'w_proj', 'b_proj')}
    del _L2_xattn_all

    def _L2_ffn_setup():
        import jax, jax.numpy as jnp
        import numpy as np
        EPS = 1e-08

        def _ste(x, q):
            return x + jax.lax.stop_gradient(q - x)

        def quant_act_uint8(x):
            s = jax.lax.stop_gradient(jnp.maximum(jnp.max(x), EPS)) / 255.0
            q = jnp.clip(jnp.round(x / s), 0.0, 255.0) * s
            return (_ste(x, q), s)

        def quant_weight_int8_perchannel(w):
            s = jax.lax.stop_gradient(jnp.maximum(jnp.max(jnp.abs(w), axis=1, keepdims=True), EPS)) / 127.0
            q = jnp.clip(jnp.round(w / s), -128.0, 127.0) * s
            return (_ste(w, q), s[:, 0])

        def quant_bias_int32(b, s_in, s_w):
            s = jax.lax.stop_gradient(s_in * s_w)
            q = jnp.round(b / s) * s
            return _ste(b, q)

        def quant_linear(x, w, b):
            xq, s_in = quant_act_uint8(x)
            wq, s_w = quant_weight_int8_perchannel(w)
            bq = quant_bias_int32(b, s_in, s_w)
            return jnp.einsum('btd,fd->btf', xq, wq) + bq
        key = jax.random.key(seed)
        k1, k2, k3, k4, k5 = jax.random.split(key, 5)
        B, S, D, F = (4, 256, 128, 512)
        return {'x': jax.random.normal(k1, (B, S, D), dtype=jnp.float32), 'w1': jax.random.normal(k2, (F, D), dtype=jnp.float32) * (1.0 / np.sqrt(D)), 'b1': jax.random.normal(k3, (F,), dtype=jnp.float32) * 0.01, 'w2': jax.random.normal(k4, (D, F), dtype=jnp.float32) * (1.0 / np.sqrt(F)), 'b2': jax.random.normal(k5, (D,), dtype=jnp.float32) * 0.01}
    _L2_ffn_all = _L2_ffn_setup()
    _L2_ffn_in = {k: v for k, v in _L2_ffn_all.items() if k in ('w1', 'b1', 'w2', 'b2')}
    del _L2_ffn_all

    def _L3_attn_setup():
        import jax, jax.numpy as jnp
        import numpy as np
        D_MODEL = 128
        D_STATE = 16
        EXPANSION = 2
        GROUPS = 16
        D_INNER = EXPANSION * D_MODEL
        GROUP_SIZE = D_INNER // GROUPS
        B, T = (2, 128)

        def _rmsnorm(x, g, eps=1e-06):
            return x * jax.lax.rsqrt(jnp.mean(x * x, axis=-1, keepdims=True) + eps) * g

        def _ssm(u, delta, b, c, A_log):
            A = -jnp.exp(A_log)
            deltaA = jnp.clip(delta[..., None] * A, -10.0, 10.0)
            expA = jnp.exp(deltaA)
            frac_exact = (expA - 1.0) / (A + 1e-12)
            frac = jnp.where(jnp.abs(deltaA) < 0.0001, delta[..., None], frac_exact)
            Bu = frac * (b * u[..., None])

            def step(h, inp):
                Ah_t, Bu_t, c_t = inp
                h = Ah_t * h + Bu_t
                return (h, jnp.sum(h * c_t, axis=-1))
            tm = lambda a: jnp.moveaxis(a, 1, 0)
            h0 = jnp.zeros(u.shape[:1] + u.shape[2:] + (A.shape[0],), u.dtype)
            _, ys = jax.lax.scan(step, h0, (tm(expA), tm(Bu), tm(c)))
            return jnp.moveaxis(ys, 0, 1)
        key = jax.random.key(seed)
        ks = jax.random.split(key, 8)
        s_in = 1.0 / np.sqrt(D_MODEL)
        s_inner = 1.0 / np.sqrt(D_INNER)
        s_ff = 1.0 / np.sqrt(4 * D_MODEL)
        return {'x': jax.random.normal(ks[0], (B, T, D_MODEL), dtype=jnp.float32), 'A_log': jnp.log(jnp.linspace(1.0, float(D_STATE), D_STATE)).astype(jnp.float32), 'g1': jnp.ones((D_MODEL,), jnp.float32), 'g2': jnp.ones((D_MODEL,), jnp.float32), 'W_in': jax.random.normal(ks[1], (2 * D_INNER, D_MODEL), jnp.float32) * s_in, 'W_param': jax.random.normal(ks[2], (GROUPS * (1 + 2 * D_STATE), D_INNER), jnp.float32) * s_inner, 'W_out': jax.random.normal(ks[3], (D_MODEL, D_INNER), jnp.float32) * s_inner, 'W_ffn1': jax.random.normal(ks[4], (4 * D_MODEL, D_MODEL), jnp.float32) * s_in, 'b_ffn1': jnp.zeros((4 * D_MODEL,), jnp.float32), 'W_ffn2': jax.random.normal(ks[5], (D_MODEL, 4 * D_MODEL), jnp.float32) * s_ff, 'b_ffn2': jnp.zeros((D_MODEL,), jnp.float32)}
    _L3_attn_all = _L3_attn_setup()
    _L3_attn_in = {k: v for k, v in _L3_attn_all.items() if k in ('A_log', 'g1', 'g2', 'W_in', 'W_param', 'W_out', 'W_ffn1', 'b_ffn1', 'W_ffn2', 'b_ffn2')}
    del _L3_attn_all

    def _L3_xattn_setup():
        import jax, jax.numpy as jnp
        import numpy as np
        UNITS = 128
        NUM_HEADS = 8

        def _split_heads(x, n):
            B, S, D = x.shape
            return x.reshape(B, S, n, D // n).transpose(0, 2, 1, 3)
        key = jax.random.key(seed)
        k1, k2, k3 = jax.random.split(key, 3)
        B, S = (8, 128)
        memory = jax.random.normal(k1, (B, S, 2 * UNITS), dtype=jnp.float32)
        query = jax.random.normal(k2, (B, S, UNITS), dtype=jnp.float32)
        seq_mask = jax.random.randint(k3, (B, S), 0, 2, dtype=jnp.int32)
        b = jnp.zeros((1,), dtype=jnp.float32)
        return {'memory': memory, 'query': query, 'seq_mask': seq_mask, 'b': b}
    _L3_xattn_all = _L3_xattn_setup()
    _L3_xattn_in = {k: v for k, v in _L3_xattn_all.items() if k in ('b',)}
    del _L3_xattn_all

    def _L3_ffn_setup():
        import jax, jax.numpy as jnp
        import numpy as np
        B, M, D = (4, 256, 128)
        N, P = (64, 32)
        key = jax.random.key(seed)
        k1, k2, k3, k4 = jax.random.split(key, 4)
        x = jax.random.normal(k1, (B, M, D), dtype=jnp.float32)
        phi = jax.random.normal(k2, (D, N, P), dtype=jnp.float32) * (1.0 / np.sqrt(D))
        W = jax.random.normal(k3, (N, D, D), dtype=jnp.float32) * (1.0 / np.sqrt(D))
        b = jax.random.normal(k4, (N, D), dtype=jnp.float32) * 0.01
        return {'x': x, 'phi': phi, 'W': W, 'b': b}
    _L3_ffn_all = _L3_ffn_setup()
    _L3_ffn_in = {k: v for k, v in _L3_ffn_all.items() if k in ('phi', 'W', 'b')}
    del _L3_ffn_all
    return {'x': x, 'ctx_2048': ctx_2048, 'mask_BxS2_if0': mask_BxS2_if0, 'mask_BxS2_ik0': mask_BxS2_ik0, 'L0_attn_wq': _L0_attn_in['wq'], 'L0_attn_wk': _L0_attn_in['wk'], 'L0_attn_wv': _L0_attn_in['wv'], 'L0_attn_wo': _L0_attn_in['wo'], 'L0_attn_bo': _L0_attn_in['bo'], 'L0_attn_cw1': _L0_attn_in['cw1'], 'L0_attn_cb1': _L0_attn_in['cb1'], 'L0_attn_cw2': _L0_attn_in['cw2'], 'L0_attn_cb2': _L0_attn_in['cb2'], 'L0_attn_cw3': _L0_attn_in['cw3'], 'L0_attn_cb3': _L0_attn_in['cb3'], 'L0_xattn_W_in': _L0_xattn_in['W_in'], 'L0_xattn_b_in': _L0_xattn_in['b_in'], 'L0_xattn_g_res': _L0_xattn_in['g_res'], 'L0_xattn_g_init': _L0_xattn_in['g_init'], 'L0_ffn_gate_w': _L0_ffn_in['gate_w'], 'L0_ffn_Wg': _L0_ffn_in['Wg'], 'L0_ffn_Wu': _L0_ffn_in['Wu'], 'L0_ffn_Wd': _L0_ffn_in['Wd'], 'L0_ffn_Ws_g': _L0_ffn_in['Ws_g'], 'L0_ffn_Ws_u': _L0_ffn_in['Ws_u'], 'L0_ffn_Ws_d': _L0_ffn_in['Ws_d'], 'L1_attn_Wq': _L1_attn_in['Wq'], 'L1_attn_Wk': _L1_attn_in['Wk'], 'L1_attn_Wv': _L1_attn_in['Wv'], 'L1_attn_Wg': _L1_attn_in['Wg'], 'L1_attn_Wo': _L1_attn_in['Wo'], 'L1_attn_conv_q': _L1_attn_in['conv_q'], 'L1_attn_conv_k': _L1_attn_in['conv_k'], 'L1_attn_conv_v': _L1_attn_in['conv_v'], 'L1_attn_Wgk': _L1_attn_in['Wgk'], 'L1_attn_Wb': _L1_attn_in['Wb'], 'L1_attn_b_b': _L1_attn_in['b_b'], 'L1_attn_A_log': _L1_attn_in['A_log'], 'L1_attn_dt_bias': _L1_attn_in['dt_bias'], 'L1_attn_g_norm_weight': _L1_attn_in['g_norm_weight'], 'L1_xattn_w_qkv': _L1_xattn_in['w_qkv'], 'L1_xattn_w_proj': _L1_xattn_in['w_proj'], 'L1_xattn_b_proj': _L1_xattn_in['b_proj'], 'L1_ffn_Wg': _L1_ffn_in['Wg'], 'L1_ffn_Wu': _L1_ffn_in['Wu'], 'L1_ffn_Wd': _L1_ffn_in['Wd'], 'L2_attn_t': _L2_attn_in['t'], 'L2_xattn_w_qkv': _L2_xattn_in['w_qkv'], 'L2_xattn_w_proj': _L2_xattn_in['w_proj'], 'L2_xattn_b_proj': _L2_xattn_in['b_proj'], 'L2_ffn_w1': _L2_ffn_in['w1'], 'L2_ffn_b1': _L2_ffn_in['b1'], 'L2_ffn_w2': _L2_ffn_in['w2'], 'L2_ffn_b2': _L2_ffn_in['b2'], 'L3_attn_A_log': _L3_attn_in['A_log'], 'L3_attn_g1': _L3_attn_in['g1'], 'L3_attn_g2': _L3_attn_in['g2'], 'L3_attn_W_in': _L3_attn_in['W_in'], 'L3_attn_W_param': _L3_attn_in['W_param'], 'L3_attn_W_out': _L3_attn_in['W_out'], 'L3_attn_W_ffn1': _L3_attn_in['W_ffn1'], 'L3_attn_b_ffn1': _L3_attn_in['b_ffn1'], 'L3_attn_W_ffn2': _L3_attn_in['W_ffn2'], 'L3_attn_b_ffn2': _L3_attn_in['b_ffn2'], 'L3_xattn_b': _L3_xattn_in['b'], 'L3_ffn_phi': _L3_ffn_in['phi'], 'L3_ffn_W': _L3_ffn_in['W'], 'L3_ffn_b': _L3_ffn_in['b']}

def reference(x, ctx_2048, mask_BxS2_if0, mask_BxS2_ik0, L0_attn_wq, L0_attn_wk, L0_attn_wv, L0_attn_wo, L0_attn_bo, L0_attn_cw1, L0_attn_cb1, L0_attn_cw2, L0_attn_cb2, L0_attn_cw3, L0_attn_cb3, L0_xattn_W_in, L0_xattn_b_in, L0_xattn_g_res, L0_xattn_g_init, L0_ffn_gate_w, L0_ffn_Wg, L0_ffn_Wu, L0_ffn_Wd, L0_ffn_Ws_g, L0_ffn_Ws_u, L0_ffn_Ws_d, L1_attn_Wq, L1_attn_Wk, L1_attn_Wv, L1_attn_Wg, L1_attn_Wo, L1_attn_conv_q, L1_attn_conv_k, L1_attn_conv_v, L1_attn_Wgk, L1_attn_Wb, L1_attn_b_b, L1_attn_A_log, L1_attn_dt_bias, L1_attn_g_norm_weight, L1_xattn_w_qkv, L1_xattn_w_proj, L1_xattn_b_proj, L1_ffn_Wg, L1_ffn_Wu, L1_ffn_Wd, L2_attn_t, L2_xattn_w_qkv, L2_xattn_w_proj, L2_xattn_b_proj, L2_ffn_w1, L2_ffn_b1, L2_ffn_w2, L2_ffn_b2, L3_attn_A_log, L3_attn_g1, L3_attn_g2, L3_attn_W_in, L3_attn_W_param, L3_attn_W_out, L3_attn_W_ffn1, L3_attn_b_ffn1, L3_attn_W_ffn2, L3_attn_b_ffn2, L3_xattn_b, L3_ffn_phi, L3_ffn_W, L3_ffn_b):
    import jax
    import jax.numpy as jnp

    def _L0_attn_ref(x, wq, wk, wv, wo, bo, cw1, cb1, cw2, cb2, cw3, cb3):
        import jax, jax.numpy as jnp
        import numpy as np
        D_MODEL = 128
        H = 16
        DH = D_MODEL // H
        WIN = 7
        PAD = WIN // 2
        B, L = (2, 512)
        b, l, d = x.shape

        def heads(w):
            return (x @ w.T).reshape(b, l, H, DH).transpose(0, 2, 1, 3)
        Q, K, V = (heads(wq), heads(wk), heads(wv))
        Kp = jnp.pad(K, ((0, 0), (0, 0), (PAD, PAD), (0, 0)))
        Vp = jnp.pad(V, ((0, 0), (0, 0), (PAD, PAD), (0, 0)))
        idx = jnp.arange(l)[:, None] + jnp.arange(WIN)[None, :]
        Kw = Kp[:, :, idx]
        Vw = Vp[:, :, idx]
        scores = jnp.einsum('bhld,bhlwd->bhlw', Q, Kw) / np.float32(np.sqrt(DH))
        attn = jax.nn.softmax(scores, axis=-1)
        pos = jnp.linspace(0.0, 1.0, WIN, dtype=jnp.float32)[:, None]
        gelu = lambda z: jax.nn.gelu(z, approximate=False)
        h = gelu(jnp.einsum('wi,hji->hwj', pos, cw1) + cb1[:, None, :])
        h = gelu(jnp.einsum('hwi,hji->hwj', h, cw2) + cb2[:, None, :])
        cwt = (jnp.einsum('hwi,hji->hwj', h, cw3) + cb3[:, None, :])[..., 0]
        conn = jax.nn.softmax(cwt, axis=-1)[None, :, None, :]
        fw = attn * conn
        fw = fw / (fw.sum(axis=-1, keepdims=True) + 1e-09)
        out = jnp.einsum('bhlw,bhlwd->bhld', fw, Vw)
        out = out.transpose(0, 2, 1, 3).reshape(b, l, d)
        return out @ wo.T + bo

    def _L0_xattn_ref(embeds, patch_embeds, patch_lens, W_in, b_in, g_res, g_init):
        import jax, jax.numpy as jnp
        import numpy as np
        B, L, P = (4, 512, 128)
        D_MODEL = 128
        D_GLOBAL = 256
        HEADDIM = 32
        EPSILON = 0.001
        RMS_EPS = 1e-05

        def rmsnorm(x, g, eps=RMS_EPS):
            var = jnp.mean(jnp.square(x), axis=-1, keepdims=True)
            return x * jax.lax.rsqrt(var + eps) * g

        def _hnet_depool(h, h_patch_full, patch_lens):
            h_patch = h_patch_full[..., :D_MODEL]
            bsz, plen = (h_patch.shape[0], h_patch.shape[1])
            seqlen = h.shape[1]
            logp = jnp.full((bsz, plen), -EPSILON, dtype=jnp.float32)
            bidx = jnp.cumsum(patch_lens, axis=1) - 1
            boundary_mask = jnp.zeros((bsz, seqlen), dtype=jnp.int32)
            boundary_mask = boundary_mask.at[jnp.arange(bsz)[:, None], bidx].set(1)
            dt = (-jnp.log(-jnp.expm1(logp))).astype(h_patch.dtype)
            x = h_patch / dt[..., None]
            n_heads = D_MODEL // HEADDIM
            A = -jnp.ones((n_heads,), dtype=jnp.float32)
            bcoef = jnp.exp(logp).astype(h_patch.dtype)
            x4 = x.reshape(bsz, plen, n_heads, HEADDIM)
            a = jnp.exp(dt[:, :, None] * A[None, None, :])
            u = (dt * bcoef)[:, :, None, None] * x4
            a_b = jnp.broadcast_to(a[..., None], u.shape)

            def comb(lft, rgt):
                aL, uL = lft
                aR, uR = rgt
                return (aL * aR, uL * aR + uR)
            _, s = jax.lax.associative_scan(comb, (a_b, u), axis=1)
            depool = s.reshape(bsz, plen, D_MODEL)
            plug = jnp.clip(jnp.cumsum(boundary_mask, axis=1) - 1, 0, plen - 1)
            depool_out = depool[jnp.arange(bsz)[:, None], plug]
            return depool_out + h
        h = rmsnorm(embeds, g_res)
        h = jnp.einsum('bld,ed->ble', h, W_in) + b_in
        h_patch = rmsnorm(patch_embeds, g_init)
        return _hnet_depool(h, h_patch, patch_lens)

    def _L0_ffn_ref(hidden_states, gate_w, Wg, Wu, Wd, Ws_g, Ws_u, Ws_d):
        import jax, jax.numpy as jnp
        import numpy as np
        B, S, D = (4, 512, 128)
        E, F_EXP = (16, 256)
        F_C = 2.0
        F_SH = 256
        b, s, d = hidden_states.shape
        e = gate_w.shape[0]
        cap = int(s * F_C / e)
        logits = jnp.einsum('bsd,ed->bse', hidden_states, gate_w)
        scores = jax.nn.softmax(logits, axis=-1).transpose(0, 2, 1)
        topk_w, topk_idx = jax.lax.top_k(scores, cap)
        x_tok = jnp.take_along_axis(hidden_states[:, None, :, :], topk_idx[..., None], axis=2)
        g = jnp.einsum('becd,efd->becf', x_tok, Wg)
        u = jnp.einsum('becd,efd->becf', x_tok, Wu)
        h = jax.nn.gelu(g, approximate=False) * u
        eo = jnp.einsum('becf,edf->becd', h, Wd) * topk_w[..., None]
        offs = (jnp.arange(b) * s)[:, None, None]
        flat_idx = (topk_idx + offs).reshape(-1)
        flat = jnp.zeros((b * s, d), hidden_states.dtype)
        flat = flat.at[flat_idx].add(eo.reshape(-1, d))
        out = flat.reshape(b, s, d)
        gs = jnp.einsum('bsd,fd->bsf', hidden_states, Ws_g)
        us = jnp.einsum('bsd,fd->bsf', hidden_states, Ws_u)
        shared = jnp.einsum('bsf,df->bsd', jax.nn.gelu(gs, approximate=False) * us, Ws_d)
        return out + shared

    def _L1_attn_ref(hidden_states, Wq, Wk, Wv, Wg, Wo, conv_q, conv_k, conv_v, Wgk, Wb, b_b, A_log, dt_bias, g_norm_weight):
        import jax, jax.numpy as jnp
        import numpy as np
        import math
        B, L, HID = (2, 512, 128)
        NH, DK, DV = (12, 64, 128)
        KD, VD, CS = (NH * DK, NH * DV, 4)
        SCALE = DK ** (-0.5)

        def _causal_depthwise_conv(x, w):
            c, k = w.shape
            xt = jnp.transpose(x, (0, 2, 1))
            out = jax.lax.conv_general_dilated(xt, w[:, None, :], window_strides=(1,), padding=[(k - 1, 0)], feature_group_count=c, dimension_numbers=('NCH', 'OIH', 'NCH'))
            return jnp.transpose(out, (0, 2, 1))

        def _l2norm(x, eps=1e-06):
            return x * jax.lax.rsqrt(jnp.sum(x * x, axis=-1, keepdims=True) + eps)

        def _gated_delta_net(hidden_states, Wq, Wk, Wv, Wg, Wo, conv_q, conv_k, conv_v, Wgk, Wb, b_b, A_log, dt_bias, g_norm_weight):
            b, l, _ = hidden_states.shape
            q = jax.nn.silu(_causal_depthwise_conv(hidden_states @ Wq, conv_q))
            k = jax.nn.silu(_causal_depthwise_conv(hidden_states @ Wk, conv_k))
            v = jax.nn.silu(_causal_depthwise_conv(hidden_states @ Wv, conv_v))
            gk = -jnp.exp(A_log) * jax.nn.softplus(hidden_states @ Wgk + dt_bias)
            beta = jax.nn.sigmoid(hidden_states @ Wb + b_b)
            q = jnp.transpose(q.reshape(b, l, NH, DK), (0, 2, 1, 3))
            k = jnp.transpose(k.reshape(b, l, NH, DK), (0, 2, 1, 3))
            v = jnp.transpose(v.reshape(b, l, NH, DV), (0, 2, 1, 3))
            q = _l2norm(q) * SCALE
            k = _l2norm(k)
            qs = jnp.moveaxis(q, 2, 0)
            ks_ = jnp.moveaxis(k, 2, 0)
            vs = jnp.moveaxis(v, 2, 0)
            bs = jnp.moveaxis(beta, 1, 0)
            gs = jnp.moveaxis(gk, 1, 0)

            def step(S, inp):
                qt, kt, vt, bt, gt = inp
                S = S * jnp.exp(gt)[..., None, None]
                kv = jnp.einsum('bhk,bhkv->bhv', kt, S)
                delta = (vt - kv) * bt[..., None]
                S = S + jnp.einsum('bhk,bhv->bhkv', kt, delta)
                ot = jnp.einsum('bhk,bhkv->bhv', qt, S)
                return (S, ot)
            S0 = jnp.zeros((b, NH, DK, DV), hidden_states.dtype)
            _, os_ = jax.lax.scan(step, S0, (qs, ks_, vs, bs, gs))
            o = jnp.moveaxis(os_, 0, 1)
            g = (hidden_states @ Wg).reshape(b, l, NH, DV)
            var = jnp.mean(o * o, axis=-1, keepdims=True)
            o = o * jax.lax.rsqrt(var + 1e-05) * g_norm_weight
            o = o * g * jax.nn.sigmoid(g)
            return o.reshape(b, l, VD) @ Wo
        return _gated_delta_net(hidden_states, Wq, Wk, Wv, Wg, Wo, conv_q, conv_k, conv_v, Wgk, Wb, b_b, A_log, dt_bias, g_norm_weight)

    def _L1_xattn_ref(x, context, w_qkv, w_proj, b_proj):
        import jax, jax.numpy as jnp
        import numpy as np
        NUM_HEADS = 16
        B, N, C = x.shape
        H = NUM_HEADS
        D = C // H
        scale = D ** (-0.5)
        qkv = (x @ w_qkv.T).reshape(B, N, 3, H, D).transpose(2, 0, 3, 1, 4)
        q, k, v = (qkv[0], qkv[1], qkv[2])
        N_c = context.shape[1]
        kv = context.reshape(B, N_c, 2, H, D).transpose(2, 0, 3, 1, 4)
        extra_k, extra_v = (kv[0], kv[1])
        k = jnp.concatenate([extra_k, k], axis=2)
        v = jnp.concatenate([extra_v, v], axis=2)
        dtype = q.dtype
        attn = jnp.einsum('bhnd,bhmd->bhnm', q * scale, k).astype(jnp.float32)
        attn = jax.nn.softmax(attn, axis=-1).astype(dtype)
        out = jnp.einsum('bhnm,bhmd->bhnd', attn, v)
        out = out.transpose(0, 2, 1, 3).reshape(B, N, C)
        return out @ w_proj.T + b_proj

    def _L1_ffn_ref(hidden_states, Wg, Wu, Wd):
        import jax, jax.numpy as jnp
        import numpy as np
        NUM_EXPERTS = 8
        HIDDEN = 128
        FFN = 512
        BATCH = 2
        SEQ = 256
        B, S, H = hidden_states.shape
        x = hidden_states.reshape(-1, H)

        def expert_step(acc, w):
            wg, wu, wd = w
            h = jax.nn.silu(x @ wg) * (x @ wu)
            return (acc + h @ wd, None)
        acc, _ = jax.lax.scan(expert_step, jnp.zeros_like(x), (Wg, Wu, Wd))
        return acc.reshape(B, S, H)

    def _L2_attn_ref(x, t):
        import jax, jax.numpy as jnp
        import numpy as np
        B, N, D = (8, 512, 128)
        'Causal per-channel Toeplitz mix: y[b,i,d] = sum_{j<=i} t[i-j,d] * x[b,j,d].\n\n            Computed via zero-padded FFT convolution (O(n log n) per channel) instead of\n            the O(n^2) dense triangular matmul; the causal truncation [:n] keeps only the\n            lower-triangular (relative-position j<=i) contributions, matching the CUDA kernel.\n            '
        b, n, d = x.shape
        L = 2 * n
        Xf = jnp.fft.rfft(x, n=L, axis=1)
        Tf = jnp.fft.rfft(t, n=L, axis=0)
        y = jnp.fft.irfft(Xf * Tf[None], n=L, axis=1)[:, :n, :]
        return y.astype(x.dtype)

    def _L2_xattn_ref(x, context, w_qkv, w_proj, b_proj):
        import jax, jax.numpy as jnp
        import numpy as np
        NUM_HEADS = 16
        B, N, C = x.shape
        H = NUM_HEADS
        D = C // H
        scale = D ** (-0.5)
        qkv = (x @ w_qkv.T).reshape(B, N, 3, H, D).transpose(2, 0, 3, 1, 4)
        q, k, v = (qkv[0], qkv[1], qkv[2])
        N_c = context.shape[1]
        kv = context.reshape(B, N_c, 2, H, D).transpose(2, 0, 3, 1, 4)
        extra_k, extra_v = (kv[0], kv[1])
        k = jnp.concatenate([extra_k, k], axis=2)
        v = jnp.concatenate([extra_v, v], axis=2)
        dtype = q.dtype
        attn = jnp.einsum('bhnd,bhmd->bhnm', q * scale, k).astype(jnp.float32)
        attn = jax.nn.softmax(attn, axis=-1).astype(dtype)
        out = jnp.einsum('bhnm,bhmd->bhnd', attn, v)
        out = out.transpose(0, 2, 1, 3).reshape(B, N, C)
        return out @ w_proj.T + b_proj

    def _L2_ffn_ref(x, w1, b1, w2, b2):
        import jax, jax.numpy as jnp
        import numpy as np
        EPS = 1e-08

        def _ste(x, q):
            return x + jax.lax.stop_gradient(q - x)

        def quant_act_uint8(x):
            s = jax.lax.stop_gradient(jnp.maximum(jnp.max(x), EPS)) / 255.0
            q = jnp.clip(jnp.round(x / s), 0.0, 255.0) * s
            return (_ste(x, q), s)

        def quant_weight_int8_perchannel(w):
            s = jax.lax.stop_gradient(jnp.maximum(jnp.max(jnp.abs(w), axis=1, keepdims=True), EPS)) / 127.0
            q = jnp.clip(jnp.round(w / s), -128.0, 127.0) * s
            return (_ste(w, q), s[:, 0])

        def quant_bias_int32(b, s_in, s_w):
            s = jax.lax.stop_gradient(s_in * s_w)
            q = jnp.round(b / s) * s
            return _ste(b, q)

        def quant_linear(x, w, b):
            xq, s_in = quant_act_uint8(x)
            wq, s_w = quant_weight_int8_perchannel(w)
            bq = quant_bias_int32(b, s_in, s_w)
            return jnp.einsum('btd,fd->btf', xq, wq) + bq
        h = jax.nn.relu(quant_linear(x, w1, b1))
        return quant_linear(h, w2, b2)

    def _L3_attn_ref(x, A_log, g1, g2, W_in, W_param, W_out, W_ffn1, b_ffn1, W_ffn2, b_ffn2):
        import jax, jax.numpy as jnp
        import numpy as np
        D_MODEL = 128
        D_STATE = 16
        EXPANSION = 2
        GROUPS = 16
        D_INNER = EXPANSION * D_MODEL
        GROUP_SIZE = D_INNER // GROUPS
        B, T = (2, 128)

        def _rmsnorm(x, g, eps=1e-06):
            return x * jax.lax.rsqrt(jnp.mean(x * x, axis=-1, keepdims=True) + eps) * g

        def _ssm(u, delta, b, c, A_log):
            A = -jnp.exp(A_log)
            deltaA = jnp.clip(delta[..., None] * A, -10.0, 10.0)
            expA = jnp.exp(deltaA)
            frac_exact = (expA - 1.0) / (A + 1e-12)
            frac = jnp.where(jnp.abs(deltaA) < 0.0001, delta[..., None], frac_exact)
            Bu = frac * (b * u[..., None])

            def step(h, inp):
                Ah_t, Bu_t, c_t = inp
                h = Ah_t * h + Bu_t
                return (h, jnp.sum(h * c_t, axis=-1))
            tm = lambda a: jnp.moveaxis(a, 1, 0)
            h0 = jnp.zeros(u.shape[:1] + u.shape[2:] + (A.shape[0],), u.dtype)
            _, ys = jax.lax.scan(step, h0, (tm(expA), tm(Bu), tm(c)))
            return jnp.moveaxis(ys, 0, 1)
        Bsz, Tlen, _ = x.shape
        z = _rmsnorm(x, g1)
        xz_gate = jnp.einsum('btd,ed->bte', z, W_in)
        xz, gate = jnp.split(xz_gate, 2, axis=-1)
        xz = jax.nn.silu(xz)
        params = jnp.einsum('btd,pd->btp', xz, W_param)
        params = params.reshape(Bsz, Tlen, GROUPS, 1 + 2 * D_STATE)
        delta_g = params[..., :1]
        b_g = params[..., 1:1 + D_STATE]
        c_g = params[..., 1 + D_STATE:]
        delta = jax.nn.softplus(jnp.repeat(delta_g[..., 0], GROUP_SIZE, axis=2))
        b = jnp.repeat(b_g, GROUP_SIZE, axis=2)
        c = jnp.repeat(c_g, GROUP_SIZE, axis=2)
        y_ssm = _ssm(xz, delta, b, c, A_log)
        y = y_ssm * jax.nn.silu(gate)
        y = jnp.einsum('bte,de->btd', y, W_out)
        x = x + y
        h2 = _rmsnorm(x, g2)
        ffn = jnp.einsum('btf,df->btd', jax.nn.silu(jnp.einsum('btd,fd->btf', h2, W_ffn1) + b_ffn1), W_ffn2) + b_ffn2
        return x + ffn

    def _L3_xattn_ref(memory, query, seq_mask, b):
        import jax, jax.numpy as jnp
        import numpy as np
        UNITS = 128
        NUM_HEADS = 8

        def _split_heads(x, n):
            B, S, D = x.shape
            return x.reshape(B, S, n, D // n).transpose(0, 2, 1, 3)
        H = NUM_HEADS
        depth = UNITS // H
        Q = _split_heads(query, H) * depth ** (-0.5)
        k_mem, v_mem = jnp.split(memory, 2, axis=2)
        K = _split_heads(k_mem, H)
        V = _split_heads(v_mem, H)
        logits = jnp.einsum('bhqd,bhkd->bhqk', Q, K) + b[0]
        mask = seq_mask.astype(jnp.float32)[:, None, None, :]
        logits = logits + -1e+30 * (1.0 - mask)
        weights = jax.nn.softmax(logits, axis=-1)
        out = jnp.einsum('bhqk,bhkd->bhqd', weights, V)
        B, _, S, _ = out.shape
        return out.transpose(0, 2, 1, 3).reshape(B, S, UNITS)

    def _L3_ffn_ref(x, phi, W, b):
        import jax, jax.numpy as jnp
        import numpy as np
        B, M, D = (4, 256, 128)
        N, P = (64, 32)
        logits = jnp.einsum('bmd,dnp->bmnp', x, phi)
        dispatch = jax.nn.softmax(logits, axis=0)
        bsz, m, n, p = logits.shape
        combine = jax.nn.softmax(logits.reshape(bsz, m, n * p), axis=-1).reshape(bsz, m, n, p)
        slots = jnp.einsum('bmd,bmnp->bnpd', x, dispatch)
        y = jnp.einsum('bnpd,nde->bnpe', slots, W) + b[None, :, None, :]
        out = jnp.einsum('bnpd,bmnp->bmd', y, combine)
        return out
    x = _layernorm(x + _L0_attn_ref(x, L0_attn_wq, L0_attn_wk, L0_attn_wv, L0_attn_wo, L0_attn_bo, L0_attn_cw1, L0_attn_cb1, L0_attn_cw2, L0_attn_cb2, L0_attn_cw3, L0_attn_cb3), axis=-1)
    x = _layernorm(x + _L0_xattn_ref(x, ctx_2048, mask_BxS2_if0, L0_xattn_W_in, L0_xattn_b_in, L0_xattn_g_res, L0_xattn_g_init), axis=-1)
    x = _layernorm(x + _L0_ffn_ref(x, L0_ffn_gate_w, L0_ffn_Wg, L0_ffn_Wu, L0_ffn_Wd, L0_ffn_Ws_g, L0_ffn_Ws_u, L0_ffn_Ws_d), axis=-1)
    x = _layernorm(x + _L1_attn_ref(x, L1_attn_Wq, L1_attn_Wk, L1_attn_Wv, L1_attn_Wg, L1_attn_Wo, L1_attn_conv_q, L1_attn_conv_k, L1_attn_conv_v, L1_attn_Wgk, L1_attn_Wb, L1_attn_b_b, L1_attn_A_log, L1_attn_dt_bias, L1_attn_g_norm_weight), axis=-1)
    x = _layernorm(x + _L1_xattn_ref(x, ctx_2048, L1_xattn_w_qkv, L1_xattn_w_proj, L1_xattn_b_proj), axis=-1)
    x = _layernorm(x + _L1_ffn_ref(x, L1_ffn_Wg, L1_ffn_Wu, L1_ffn_Wd), axis=-1)
    x = _layernorm(x + _L2_attn_ref(x, L2_attn_t), axis=-1)
    x = _layernorm(x + _L2_xattn_ref(x, ctx_2048, L2_xattn_w_qkv, L2_xattn_w_proj, L2_xattn_b_proj), axis=-1)
    x = _layernorm(x + _L2_ffn_ref(x, L2_ffn_w1, L2_ffn_b1, L2_ffn_w2, L2_ffn_b2), axis=-1)
    x = _layernorm(x + _L3_attn_ref(x, L3_attn_A_log, L3_attn_g1, L3_attn_g2, L3_attn_W_in, L3_attn_W_param, L3_attn_W_out, L3_attn_W_ffn1, L3_attn_b_ffn1, L3_attn_W_ffn2, L3_attn_b_ffn2), axis=-1)
    x = _layernorm(x + _L3_xattn_ref(ctx_2048, x, mask_BxS2_ik0, L3_xattn_b), axis=-1)
    x = _layernorm(x + _L3_ffn_ref(x, L3_ffn_phi, L3_ffn_W, L3_ffn_b), axis=-1)
    return x

_drawn_inputs = setup_inputs


def setup_inputs(seed=0):
    import zlib

    import numpy as np

    out = dict(_drawn_inputs(seed))
    spreads = {'L0_xattn_b_in': (0.0, 0.1),
     'L0_xattn_g_res': (1.0, 0.2),
     'L0_xattn_g_init': (1.0, 0.2),
     'L1_attn_g_norm_weight': (1.0, 0.2),
     'L3_attn_g1': (1.0, 0.6),
     'L3_attn_g2': (1.0, 0.2),
     'L3_attn_b_ffn1': (0.0, 0.277),
     'L3_attn_b_ffn2': (0.0, 0.1)}
    factors = {'L0_attn_wq': 8.0,
     'L0_attn_wk': 8.0,
     'L0_attn_cw1': 28.573,
     'L0_attn_cb1': 28.665,
     'L0_attn_cw2': 28.524,
     'L0_attn_cb2': 31.53,
     'L0_attn_cw3': 28.549,
     'L0_ffn_gate_w': 8.0,
     'L0_ffn_Wg': 8.0,
     'L0_ffn_Wu': 8.0,
     'L0_ffn_Wd': 8.0,
     'L0_ffn_Ws_g': 4.331,
     'L0_ffn_Ws_u': 4.289,
     'L0_ffn_Ws_d': 4.265,
     'L1_attn_b_b': 7.341,
     'L1_xattn_w_qkv': 5.395,
     'L2_xattn_w_qkv': 7.002,
     'L2_xattn_b_proj': 2.827,
     'L2_ffn_b1': 8.0,
     'L2_ffn_b2': 6.205,
     'L3_ffn_b': 44.126,
     'L0_attn_cb3': 8.0}
    for name, (base, spread) in spreads.items():
        noise = np.random.default_rng([zlib.crc32(name.encode()), seed]).standard_normal(out[name].shape)
        drawn = base * np.exp(spread * noise) if base else spread * noise
        out[name] = jnp.asarray(drawn.astype(out[name].dtype))
    for name, factor in factors.items():
        out[name] = (out[name] * factor).astype(out[name].dtype)
    return out
```

```python
from contextlib import ExitStack

import numpy as np
import concourse.bass as bass
from concourse import mybir

ALU = mybir.AluOpType
ACT = mybir.ActivationFunctionType
AX = mybir.AxisListType.X
F32 = mybir.dt.float32
BF16 = mybir.dt.bfloat16
I32 = mybir.dt.int32

B, L, D = 32, 100, 128
N = B * L
GB = 4
GT = GB * L
NG = B // GB


def setup(nc, ctx):
    k = {}
    def sb(name, shape, dt=F32):
        k[name] = ctx.enter_context(nc.sbuf_tensor(name, shape, dt))
        return k[name]
    sb("xT", [D, N])
    sb("ident", [128, 128])
    sb("center", [128, 128])
    sb("mean", [128, 128])
    sb("eps", [128, 1])
    made = ctx.enter_context(nc.semaphore("consts_made"))
    with nc.Block() as block:
        @block.gpsimd
        def _(pool):
            nc.gpsimd.memset(k["mean"][:], 1.0 / D)
            nc.gpsimd.memset(k["eps"][:], 1e-5)
            nc.gpsimd.memset(k["ident"][:], 0.0).then_inc(made, 1)
            pool.wait_ge(made, 1)
            nc.gpsimd.affine_select(out=k["ident"][:], in_=k["ident"][:], compare_op=ALU.not_equal, fill=1.0,
                                    base=0, pattern=[[-1, 128]], channel_multiplier=1).then_inc(made, 1)
            pool.wait_ge(made, 2)
            nc.gpsimd.tensor_tensor(k["center"][:], k["ident"][:], k["mean"][:], ALU.subtract).then_inc(made, 1)
    return k


def norm_pass(nc, k, tag):
    xT = k["xT"]
    with ExitStack() as ctx:
        sem = Stage(nc, ctx, tag).sem
        ps_c = [ctx.enter_context(nc.psum_tensor(f"{tag}_c{p}", [128, 512], F32)) for p in range(2)]
        ps_v = [ctx.enter_context(nc.psum_tensor(f"{tag}_v{p}", [128, 512], F32)) for p in range(2)]
        sq = [ctx.enter_context(nc.sbuf_tensor(f"{tag}_sq{p}", [128, GT], F32)) for p in range(2)]
        rs = [ctx.enter_context(nc.sbuf_tensor(f"{tag}_rs{p}", [128, GT], F32)) for p in range(2)]
        centered, squared, summed, logged, rooted, scaled = [[sem(f"{n}{p}") for p in range(2)] for n in
            ("centered", "squared", "summed", "logged", "rooted", "scaled")]
        block = ctx.enter_context(nc.Block())

        @block.tensor
        def _(pe):
            with pe.Fori(0, NG // 2) as i:
                for p in range(2):
                    pe.wait_ge(scaled[p], i + 1)
                    nc.tensor.matmul(ps_c[p][:, 0:GT], k["center"][:], xT[:, bass.ds((2 * i + p) * GT, GT)],
                                     start=True, stop=True).then_inc(centered[p], 1)
                for p in range(2):
                    pe.wait_ge(squared[p], i + 1)
                    nc.tensor.matmul(ps_v[p][:, 0:GT], k["mean"][:], sq[p][:], start=True, stop=True).then_inc(summed[p], 1)

        @block.scalar
        def _(act):
            nc.scalar.preload_act_table_set("natural_log_exp_and_others")
            with act.Fori(0, NG // 2) as i:
                for p in range(2):
                    act.wait_ge(centered[p], i + 1)
                    nc.scalar.activation(sq[p][:], ps_c[p][:, 0:GT], ACT.Square).then_inc(squared[p], 1)
                for p in range(2):
                    act.wait_ge(summed[p], i + 1)
                    act.wait_ge(scaled[p], i + 1)
                    nc.scalar.activation(rs[p][:], ps_v[p][:, 0:GT], ACT.Ln, bias=k["eps"][:]).then_inc(logged[p], 1)
                    act.wait_ge(logged[p], i + 1)
                    nc.scalar.activation(rs[p][:], rs[p][:], ACT.Exp, scale=-0.5).then_inc(rooted[p], 1)

        @block.vector
        def _(dve):
            for p in range(2):
                dve.sem_inc(scaled[p], 1)
            with dve.Fori(0, NG // 2) as i:
                for p in range(2):
                    dve.wait_ge(rooted[p], i + 1)
                    nc.vector.tensor_tensor(xT[:, bass.ds((2 * i + p) * GT, GT)], ps_c[p][:, 0:GT], rs[p][:],
                                            ALU.mult).then_inc(scaled[p], 1)


class Stage:

    def __init__(self, nc, ctx, tag):
        self.nc, self.ctx, self.tag, self.sems = nc, ctx, tag, []
        ctx.callback(self.clear)

    def clear(self):
        self.nc.clear_and_free_semaphores(self.sems)
        self.nc.all_engine_barrier()

    def sb(self, name, shape, dt=F32):
        return self.ctx.enter_context(self.nc.sbuf_tensor(f"{self.tag}_{name}", shape, dt))

    def ps(self, name, shape=(128, 512), dt=F32):
        return self.ctx.enter_context(self.nc.psum_tensor(f"{self.tag}_{name}", list(shape), dt))

    def sem(self, name):
        self.sems.append(self.nc.alloc_semaphore(f"{self.tag}_{name}"))
        return self.sems[-1]


def load(nc, tag, pairs):
    with ExitStack() as ctx:
        loaded = Stage(nc, ctx, tag).sem("loaded")
        with nc.Block() as block:
            @block.sync
            def _(sp):
                for dst, src in pairs[0::2]:
                    sp.dma_start(dst, src, allow_slow_non_contiguous=True).then_inc(loaded, 16)
                sp.wait_ge(loaded, 16 * len(pairs))

            @block.scalar
            def _(act):
                for dst, src in pairs[1::2]:
                    act.dma_start(dst, src, allow_slow_non_contiguous=True).then_inc(loaded, 16)


def load_transposed(nc, k, tag, items, by=None):
    W = 4
    with ExitStack() as ctx:
        s = Stage(nc, ctx, tag)
        nat = s.sb("nat", [128, len(items), 128])
        turned = [s.ps(f"turned{p}") for p in range(2)]
        loaded, transposed, copied = s.sem("loaded"), s.sem("transposed"), s.sem("copied")
        block = ctx.enter_context(nc.Block())

        @block.sync
        def _(sp):
            for n, (dst, src) in enumerate(items):
                sp.dma_start(nat[0:src.shape[0], n, 0:src.shape[1]], src).then_inc(loaded, 16)

        @block.tensor
        def _(pe):
            pe.wait_ge(loaded, 16 * len(items))
            for n, (dst, src) in enumerate(items):
                o, i = src.shape
                if n >= 2 * W and n % W == 0:
                    pe.wait_ge(copied, n - W)
                bank = turned[n // W % 2][0:i, n % W * 128:n % W * 128 + o]
                if by is None:
                    nc.tensor.transpose(bank, nat[0:o, n, 0:i], k["ident"][0:o, 0:o]).then_inc(transposed, 1)
                else:
                    nc.tensor.matmul(bank, nat[0:o, n, 0:i], by[0:o, 0:o], start=True, stop=True).then_inc(transposed, 1)

        @block.vector
        def _(dve):
            for n, (dst, src) in enumerate(items):
                o, i = src.shape
                dve.wait_ge(transposed, min((n // W + 1) * W, len(items)))
                nc.vector.tensor_copy(dst, turned[n // W % 2][0:i, n % W * 128:n % W * 128 + o]).then_inc(copied, 1)


def col(ap):
    return ap.rearrange("(n o) -> n o", o=1)


def l1_ffn(nc, k, a):
    E, F = a["L1_ffn_Wg"].shape[0], a["L1_ffn_Wg"].shape[2]
    C = F // 128
    S = E * C
    xT = k["xT"]
    with ExitStack() as ctx:
        s = Stage(nc, ctx, "l1f")
        wg, wu, wd = s.sb("wg", [D, E, F]), s.sb("wu", [D, E, F]), s.sb("wd", [128, E, C, D])
        load(nc, "l1fw", [(wg[:], a["L1_ffn_Wg"].rearrange("e d f -> d e f")),
                          (wu[:], a["L1_ffn_Wu"].rearrange("e d f -> d e f")),
                          (wd[:], a["L1_ffn_Wd"].rearrange("e (c f) d -> f e c d", f=128))])
        g, u, acc = [s.ps(f"g{p}") for p in range(2)], [s.ps(f"u{p}") for p in range(2)], s.ps("acc")
        sg, h = [s.sb(f"sg{p}", [128, GT]) for p in range(2)], [s.sb(f"h{p}", [128, GT]) for p in range(2)]
        gated, upped, activated, multiplied, downed, added = [s.sem(n) for n in
            ("gated", "upped", "activated", "multiplied", "downed", "added")]
        block = ctx.enter_context(nc.Block())

        @block.tensor
        def _(pe):
            def down(i, n):
                pe.wait_ge(multiplied, i * S + n + 1)
                if n == 0:
                    pe.wait_ge(added, i + 1)
                nc.tensor.matmul(acc[:, 0:GT], wd[:, n // C, n % C, :], h[n % 2][:], start=(n == 0),
                                 stop=(n == S - 1)).then_inc(downed, 1)
            with pe.Fori(0, NG) as i:
                x = xT[:, bass.ds(i * GT, GT)]
                for n in range(S):
                    e, f = n // C, slice(n % C * 128, n % C * 128 + 128)
                    if n >= 2:
                        pe.wait_ge(multiplied, i * S + n - 1)
                    nc.tensor.matmul(g[n % 2][:, 0:GT], wg[:, e, f], x, start=True, stop=True).then_inc(gated, 1)
                    nc.tensor.matmul(u[n % 2][:, 0:GT], wu[:, e, f], x, start=True, stop=True).then_inc(upped, 1)
                    if n >= 1:
                        down(i, n - 1)
                down(i, S - 1)

        @block.scalar
        def _(act):
            with act.Fori(0, NG) as i:
                for n in range(S):
                    act.wait_ge(gated, i * S + n + 1)
                    if n >= 2:
                        act.wait_ge(multiplied, i * S + n - 1)
                    else:
                        act.wait_ge(added, i + 1)
                    nc.scalar.activation(sg[n % 2][:], g[n % 2][:, 0:GT], ACT.Silu).then_inc(activated, 1)

        @block.vector
        def _(dve):
            dve.sem_inc(added, 1)
            with dve.Fori(0, NG) as i:
                for n in range(S):
                    dve.wait_ge(activated, i * S + n + 1)
                    dve.wait_ge(upped, i * S + n + 1)
                    if n >= 2:
                        dve.wait_ge(downed, i * S + n - 1)
                    nc.vector.tensor_tensor(h[n % 2][:], sg[n % 2][:], u[n % 2][:, 0:GT], ALU.mult).then_inc(multiplied, 1)
                dve.wait_ge(downed, i * S + S)
                x = xT[:, bass.ds(i * GT, GT)]
                nc.vector.tensor_tensor(x, x, acc[:, 0:GT], ALU.add).then_inc(added, 1)


def l2_attn(nc, k, a):
    xT = k["xT"]
    DC = 32
    NC = D // DC
    with ExitStack() as ctx:
        s = Stage(nc, ctx, "l2a")
        u, flip = s.sb("u", [D, 2 * L]), s.sb("flip", [L, L])
        flipped = s.sem("flipped")
        with nc.Block() as block:
            @block.gpsimd
            def _(pool):
                nc.gpsimd.memset(flip[:], 0.0).then_inc(flipped, 1)
                pool.wait_ge(flipped, 1)
                nc.gpsimd.affine_select(out=flip[:], in_=flip[:], compare_op=ALU.not_equal, fill=1.0, base=1 - L,
                                        pattern=[[1, L]], channel_multiplier=1)
        t = a["L2_attn_t"]
        load_transposed(nc, k, "l2at", [(u[:, 0:L], t[0:L, :]), (u[:, L:2 * L], t[L:2 * L, :])], by=flip)
        ud = nc.dram_tensor("l2a_ud", [D, 2 * L], F32).ap()
        toe = [s.sb(f"toe{p}", [L, DC, L]) for p in range(2)]
        xs, xtm, ytm = [s.sb(f"xs{p}", [D, GT]) for p in range(2)], s.sb("xtm", [L, D, B]), s.sb("ytm", [L, B, D])
        pt, py = [s.ps(f"pt{p}") for p in range(2)], [s.ps(f"py{p}", (128, 1024)) for p in range(2)]
        wrote, staged, turned, kept = s.sem("wrote"), s.sem("staged"), s.sem("turned"), s.sem("kept")
        filled = [s.sem(f"filled{p}") for p in range(2)]
        convolved, out, back, added = s.sem("convolved"), s.sem("out"), s.sem("back"), s.sem("added")
        block = ctx.enter_context(nc.Block())
        hb = DC // 2

        @block.sync
        def _(sp):
            sp.dma_start(ud, u[:]).then_inc(wrote, 16)
            sp.wait_ge(wrote, 16)
            for c in range(NC):
                if c >= 2:
                    sp.wait_ge(convolved, c - 1)
                src = bass.AP(tensor=ud.tensor, offset=ud.offset + c * DC * 2 * L, ap=[[1, L], [2 * L, DC], [1, L]])
                sp.dma_start(toe[c % 2][:], src).then_inc(filled[c % 2], 16)

        @block.vector
        def _(dve):
            dve.sem_inc(turned, 2)
            with dve.Fori(0, NG // 2) as i:
                for p in range(2):
                    dve.wait_ge(turned, 2 * i + p + 1)
                    nc.vector.tensor_copy(xs[p][:], xT[:, bass.ds((2 * i + p) * GT, GT)]).then_inc(staged, 1)
            for c in range(NC):
                dve.wait_ge(convolved, c + 1)
                for n in range(2):
                    d0 = c * DC + n * hb
                    ins = nc.vector.tensor_copy(ytm[:, :, d0:d0 + hb].rearrange("i b d -> i d b"),
                                                py[c % 2][0:L, n * 512:n * 512 + 512].rearrange("i (d b) -> i d b", b=B))
                ins.then_inc(out, 1)
            for g in range(NG):
                dve.wait_ge(back, g + 1)
                x = xT[:, g * GT:(g + 1) * GT]
                nc.vector.tensor_tensor(x, x, pt[g % 2][:, 0:GT], ALU.add).then_inc(added, 1)

        @block.scalar
        def _(act):
            with act.Fori(0, NG // 2) as i:
                for p in range(2):
                    act.wait_ge(turned, 2 * i + p + 3)
                    nc.scalar.activation(xtm[:, :, bass.ds((2 * i + p) * GB, GB)].rearrange("t d b -> t b d"),
                                         pt[p][0:L, :].rearrange("t (b d) -> t b d", d=D), ACT.Copy).then_inc(kept, 1)

        @block.tensor
        def _(pe):
            pe.sem_inc(kept, 2)
            with pe.Fori(0, NG // 2) as i:
                for p in range(2):
                    pe.wait_ge(staged, 2 * i + p + 1)
                    pe.wait_ge(kept, 2 * i + p + 1)
                    for b in range(GB):
                        ins = nc.tensor.transpose(pt[p][0:L, b * D:(b + 1) * D], xs[p][:, b * L:(b + 1) * L], k["ident"][:])
                    ins.then_inc(turned, 1)
            pe.wait_ge(kept, NG + 2)
            for c in range(NC):
                pe.wait_ge(filled[c % 2], 16 * (c // 2 + 1))
                if c >= 2:
                    pe.wait_ge(out, c - 1)
                for d in range(DC):
                    ins = nc.tensor.matmul(py[c % 2][0:L, d * B:(d + 1) * B], toe[c % 2][:, d, :], xtm[:, c * DC + d, :],
                                           start=True, stop=True)
                ins.then_inc(convolved, 1)
            pe.wait_ge(out, NC)
            for g in range(NG):
                if g >= 2:
                    pe.wait_ge(added, g - 1)
                for b in range(GB):
                    ins = nc.tensor.matmul(pt[g % 2][:, b * L:(b + 1) * L], ytm[:, g * GB + b, :], flip[:], start=True, stop=True)
                ins.then_inc(back, 1)


def l0_attn(nc, k, a):
    xT = k["xT"]
    H, J, W = a["L0_attn_cw1"].shape[0], a["L0_attn_cw1"].shape[1], 7
    DH, PAD, HC = D // H, W // 2, 128 // J
    NC = H // HC
    LP = L + 2 * PAD
    with ExitStack() as ctx:
        s = Stage(nc, ctx, "l0a")
        w = s.sb("w", [D, 4, D])
        cw2T, cw3c, cb = s.sb("cw2T", [128, NC, 128]), s.sb("cw3c", [128, NC, 1]), s.sb("cb", [128, 2, NC])
        cw1c, pos, headof, bo, cb3 = s.sb("cw1c", [128, NC]), s.sb("pos", [128, W]), s.sb("headof", [128, 128]), s.sb("bo", [D, 1]), s.sb("cb3", [D, 1])
        cw2n = s.sb("cw2n", [128, NC, J])
        hid = [s.sb(f"hid{n}", [128, NC, W]) for n in range(3)]
        place, conn, stat = s.sb("place", [128, NC, D]), s.sb("conn", [D, W]), s.sb("stat", [D, 4])
        load_transposed(nc, k, "l0at", [(w[:, n, :], a[f"L0_attn_w{c}"]) for n, c in enumerate("qkvo")])
        flat = lambda name, n: a[name].rearrange("(c h) j -> (h j) c", c=n)
        load(nc, "l0al", [
            (cw1c[:], a["L0_attn_cw1"].rearrange("(c h) j o -> (h j) (c o)", c=NC)),
            (cb[:, 0, :], flat("L0_attn_cb1", NC)), (cb[:, 1, :], flat("L0_attn_cb2", NC)),
            (cw3c[:], a["L0_attn_cw3"].rearrange("(c h) o j -> (h j) c o", c=NC)),
            (bo[:], col(a["L0_attn_bo"])),
            (cw2n[:], a["L0_attn_cw2"].rearrange("(c h) j i -> (h j) c i", c=NC))]
            + [(cb3[h * DH:(h + 1) * DH, :], a["L0_attn_cb3"][h:h + 1, :].to_broadcast([DH, 1])) for h in range(H)])
        m = s.sem("m")
        pc = s.ps("pc")
        cw2d = s.sb("cw2d", [128, NC, 128])
        with nc.Block() as block:
            @block.gpsimd
            def _(pool):
                for j in range(W):
                    nc.gpsimd.memset(pos[:, j:j + 1], float(np.linspace(0.0, 1.0, W, dtype=np.float32)[j]))
                nc.gpsimd.memset(headof[:], 1.0)
                nc.gpsimd.memset(place[:], 1.0)
                nc.gpsimd.memset(cw2d[:], 0.0).then_inc(m, 1)
                pool.wait_ge(m, 1)
                hv = headof[:].rearrange("p (h d) -> p h d", d=DH)
                nc.gpsimd.affine_select(out=hv, in_=hv, compare_op=ALU.is_ge, fill=0.0, base=0,
                                        pattern=[[-DH, H], [0, DH]], channel_multiplier=1).then_inc(m, 1)
                pv = place[:].rearrange("p c (g d) -> p c g d", d=DH)
                for c in range(NC):
                    nc.gpsimd.affine_select(out=pv[:, c], in_=pv[:, c], compare_op=ALU.is_ge, fill=0.0, base=J * HC * c,
                                            pattern=[[-J, H], [0, DH]], channel_multiplier=1)
                pool.wait_ge(m, 2)
                nc.gpsimd.affine_select(out=hv, in_=hv, compare_op=ALU.is_ge, fill=0.0, base=DH - 1,
                                        pattern=[[DH, H], [0, DH]], channel_multiplier=-1).then_inc(m, 1)
                pool.wait_ge(m, 3)
                for c in range(NC):
                    last = nc.gpsimd.affine_select(out=pv[:, c], in_=pv[:, c], compare_op=ALU.is_ge, fill=0.0,
                                                   base=J - 1 - J * HC * c, pattern=[[J, H], [0, DH]], channel_multiplier=-1)
                last.then_inc(m, 1)

            @block.vector
            def _(dve):
                dve.wait_ge(m, 4)
                for c in range(NC):
                    for h in range(HC):
                        r = slice(h * J, h * J + J)
                        nc.vector.tensor_copy(cw2d[r, c, h * J:h * J + J], cw2n[r, c, :])
                    nc.vector.tensor_scalar(hid[0][:, c, :], pos[:], cw1c[:, c:c + 1], cb[:, 0, c:c + 1], ALU.mult, ALU.add)
                    last = nc.vector.tensor_scalar(place[:, c, :], place[:, c, :], cw3c[:, c, :], None, ALU.mult)
                last.then_inc(m, 1)
                dve.wait_ge(m, 6)
                nc.vector.tensor_copy(cw2T[:].rearrange("p c n -> p (c n)"), pc[:]).then_inc(m, 1)
                dve.wait_ge(m, 9)
                for c in range(NC):
                    last = nc.vector.tensor_scalar(hid[2][:, c, :], pc[:, c * W:c * W + W], cb[:, 1, c:c + 1], None, ALU.add)
                last.then_inc(m, 1)
                dve.wait_ge(m, 12)
                nc.vector.tensor_scalar(conn[:], pc[:, 64:64 + W], cb3[:], None, ALU.add).then_inc(m, 1)
                dve.wait_ge(m, 13)
                nc.vector.reduce_max(stat[:, 0:1], conn[:], AX).then_inc(m, 1)
                dve.wait_ge(m, 14)
                nc.vector.tensor_scalar(stat[:, 1:2], stat[:, 0:1], -1.0, None, ALU.mult).then_inc(m, 1)
                dve.wait_ge(m, 16)
                nc.vector.reduce_sum(stat[:, 2:3], conn[:], AX).then_inc(m, 1)
                dve.wait_ge(m, 17)
                nc.vector.reciprocal(stat[:, 3:4], stat[:, 2:3]).then_inc(m, 1)
                dve.wait_ge(m, 18)
                nc.vector.tensor_scalar(conn[:], conn[:], stat[:, 3:4], None, ALU.mult).then_inc(m, 1)

            @block.tensor
            def _(pe):
                pe.wait_ge(m, 5)
                for c in range(NC):
                    last = nc.tensor.transpose(pc[:, c * 128:c * 128 + 128], cw2d[:, c, :], k["ident"][:])
                last.then_inc(m, 1)
                pe.wait_ge(m, 8)
                for c in range(NC):
                    last = nc.tensor.matmul(pc[:, c * W:c * W + W], cw2T[:, c, :], hid[1][:, c, :], start=True, stop=True)
                last.then_inc(m, 1)
                pe.wait_ge(m, 11)
                for c in range(NC):
                    last = nc.tensor.matmul(pc[:, 64:64 + W], place[:, c, :], hid[1][:, c, :], start=(c == 0), stop=(c == NC - 1))
                last.then_inc(m, 1)

            @block.scalar
            def _(act):
                act.wait_ge(m, 7)
                nc.scalar.activation(hid[1][:], hid[0][:], ACT.Gelu).then_inc(m, 1)
                act.wait_ge(m, 10)
                nc.scalar.activation(hid[1][:], hid[2][:], ACT.Gelu).then_inc(m, 1)
                act.wait_ge(m, 15)
                nc.scalar.activation(conn[:], conn[:], ACT.Exp, bias=stat[:, 1:2]).then_inc(m, 1)

        ps = {n: s.ps(f"p{n}") for n in "qkvo"}
        psc = [s.ps(f"sc{p}") for p in range(2)]
        q = s.sb("q", [D, GT])
        kp, vp = s.sb("kp", [D, GB, LP]), s.sb("vp", [D, GB, LP])
        prod = [s.sb(f"prod{p}", [D, GT]) for p in range(2)]
        sc = s.sb("sc", [D, W, GT])
        top, zs, cs, o = s.sb("top", [D, GT]), s.sb("zs", [D, GT]), s.sb("cs", [D, GT]), s.sb("o", [D, GT])
        projected, moved, timesed, headed, scored, shifted, exped, outed, wod, addd = [s.sem(n) for n in
            ("projected", "moved", "timesed", "headed", "scored", "shifted", "exped", "outed", "wod", "addd")]
        chain = s.sem("chain")
        block = ctx.enter_context(nc.Block())
        shape = lambda ap: ap.rearrange("d (b t) -> d b t", t=L)

        @block.tensor
        def _(pe):
            with pe.Fori(0, NG) as i:
                pe.wait_ge(addd, i + 1)
                x = xT[:, bass.ds(i * GT, GT)]
                for n, c in enumerate("qkv"):
                    nc.tensor.matmul(ps[c][:, 0:GT], w[:, n, :], x, start=True, stop=True).then_inc(projected, 1)
                for j in range(W):
                    pe.wait_ge(timesed, i * W + j + 1)
                    if j >= 2:
                        pe.wait_ge(scored, i * W + j - 1)
                    nc.tensor.matmul(psc[j % 2][:, 0:GT], headof[:], prod[j % 2][:], start=True, stop=True).then_inc(headed, 1)
                pe.wait_ge(outed, i + 1)
                nc.tensor.matmul(ps["o"][:, 0:GT], w[:, 3, :], o[:], start=True, stop=True).then_inc(wod, 1)

        @block.scalar
        def _(act):
            nc.scalar.preload_act_table_set("natural_log_exp_and_others")
            with act.Fori(0, NG) as i:
                for n, (c, dst) in enumerate((("q", shape(q[:])), ("k", kp[:, :, PAD:PAD + L]), ("v", vp[:, :, PAD:PAD + L]))):
                    act.wait_ge(projected, 3 * i + n + 1)
                    if c == "q":
                        act.wait_ge(addd, i + 1)
                    nc.scalar.activation(dst, shape(ps[c][:, 0:GT]), ACT.Copy,
                                         scale=float(DH ** -0.5) if c == "q" else 1.0).then_inc(moved, 1)
                act.wait_ge(shifted, i + 1)
                nc.scalar.activation(sc[:], sc[:], ACT.Exp).then_inc(exped, 1)

        @block.vector
        def _(dve):
            nc.vector.memset(kp[:], 0.0).then_inc(chain, 1)
            nc.vector.memset(vp[:], 0.0).then_inc(chain, 1)
            dve.wait_ge(chain, 2)
            dve.sem_inc(addd, 1)
            CH = 2 * W + 6
            with dve.Fori(0, NG) as i:
                at = [0]

                def link(ins):
                    at[0] += 1
                    ins.then_inc(chain, 1)
                    dve.wait_ge(chain, i * CH + 2 + at[0])
                dve.wait_ge(moved, 3 * i + 3)
                for j in range(W + 1):
                    if j < W:
                        if j >= 2:
                            dve.wait_ge(headed, i * W + j - 1)
                        nc.vector.tensor_tensor(shape(prod[j % 2][:]), shape(q[:]), kp[:, :, j:j + L], ALU.mult).then_inc(timesed, 1)
                    if j >= 1:
                        dve.wait_ge(headed, i * W + j)
                        nc.vector.tensor_copy(sc[:, j - 1, :], psc[(j - 1) % 2][:, 0:GT]).then_inc(scored, 1)
                dve.wait_ge(scored, i * W + W)
                link(nc.vector.tensor_reduce(top[:], sc[:].rearrange("d w t -> d t w"), AX, ALU.max))
                nc.vector.tensor_tensor(sc[:], sc[:], top[:].unsqueeze(1).to_broadcast([D, W, GT]), ALU.subtract).then_inc(shifted, 1)
                dve.wait_ge(exped, i + 1)
                link(nc.vector.tensor_reduce(zs[:], sc[:].rearrange("d w t -> d t w"), AX, ALU.add))
                for j in range(W):
                    link(nc.vector.tensor_scalar(sc[:, j, :], sc[:, j, :], conn[:, j:j + 1], None, ALU.mult))
                link(nc.vector.tensor_reduce(cs[:], sc[:].rearrange("d w t -> d t w"), AX, ALU.add))
                link(nc.vector.scalar_tensor_tensor(out=cs[:], in0=zs[:], scalar=1e-9, in1=cs[:], op0=ALU.mult, op1=ALU.add))
                link(nc.vector.reciprocal(cs[:], cs[:]))
                for j in range(W):
                    link(nc.vector.tensor_tensor(shape(sc[:, j, :]), shape(sc[:, j, :]), vp[:, :, j:j + L], ALU.mult))
                link(nc.vector.tensor_reduce(o[:], sc[:].rearrange("d w t -> d t w"), AX, ALU.add))
                nc.vector.tensor_tensor(o[:], o[:], cs[:], ALU.mult).then_inc(outed, 1)
                dve.wait_ge(wod, i + 1)
                x = xT[:, bass.ds(i * GT, GT)]
                nc.vector.scalar_tensor_tensor(out=x, in0=ps["o"][:, 0:GT], scalar=bo[:], in1=x, op0=ALU.add,
                                               op1=ALU.add).then_inc(addd, 1)
                assert at[0] == CH


def l0_xattn(nc, k, a):
    xT, ctxd, lens = k["xT"], a["ctx_2048"], a["mask_BxS2_if0"]
    P = lens.shape[1]
    Q = 4
    PQ = P // Q
    C = ctxd.shape[2]
    DT = float(-np.log(-np.expm1(np.float32(-0.001))))
    BC = float(np.exp(np.float32(-0.001)))
    with ExitStack() as ctx:
        s = Stage(nc, ctx, "l0x")
        winT, cols, decay = s.sb("winT", [D, D]), s.sb("cols", [D, 3]), s.sb("decay", [L, L])
        plug = s.sb("plug", [L, N])
        rowid, ln_bc = s.sb("rowid", [L, 1]), s.sb("ln_bc", [L, 1])
        plug_d = nc.dram_tensor("l0x_plug_d", [B, L], F32).ap()
        m = s.sem("m")
        load_transposed(nc, k, "l0xt", [(winT[:], a["L0_xattn_W_in"])])
        with ExitStack() as own:
            t = Stage(nc, own, "l0xp")
            li, lf, one, cs = t.sb("li", [B * Q, PQ], I32), t.sb("lf", [B * Q, PQ]), t.sb("one", [B * Q, PQ]), t.sb("cs", [B * Q, PQ])
            neg, hit, dump = t.sb("neg", [B * Q, PQ]), t.sb("hit", [B * Q, L]), t.sb("dump", [B * Q, PQ])
            before, same = t.sb("before", [128, 128]), t.sb("same", [128, B])
            carry, bm, cnt = t.sb("carry", [128, 1]), t.sb("bm", [B, L]), t.sb("cnt", [B, L])
            pp = t.ps("pp")
            load(nc, "l0xl", [(li[:], lens.rearrange("b (q s) -> (b q) s", q=Q)), (cols[:, 0:1], col(a["L0_xattn_g_res"])),
                              (cols[:, 1:2], col(a["L0_xattn_b_in"])), (cols[:, 2:3], col(a["L0_xattn_g_init"][0:D]))])
            with nc.Block() as block:
                @block.gpsimd
                def _(pool):
                    nc.gpsimd.memset(before[:], 1.0)
                    nc.gpsimd.memset(same[:], 1.0)
                    nc.gpsimd.memset(one[:], 1.0)
                    nc.gpsimd.memset(ln_bc[:], float(np.log(BC)))
                    nc.gpsimd.iota(rowid[:], pattern=[[0, 1]], base=0, channel_multiplier=1,
                                   allow_small_or_imprecise_dtypes=True)
                    nc.gpsimd.iota(decay[:], pattern=[[-1, L]], base=0, channel_multiplier=1,
                                   allow_small_or_imprecise_dtypes=True).then_inc(m, 1)
                    pool.wait_ge(m, 1)
                    nc.gpsimd.affine_select(out=decay[:], in_=decay[:], compare_op=ALU.is_ge, fill=1e4, base=0,
                                            pattern=[[-1, L]], channel_multiplier=1)
                    bv = before[:].rearrange("p (b q) -> p b q", q=Q)
                    nc.gpsimd.affine_select(out=bv, in_=bv, compare_op=ALU.is_ge, fill=0.0, base=0,
                                            pattern=[[-Q, B], [0, Q]], channel_multiplier=1)
                    nc.gpsimd.affine_select(out=same[:], in_=same[:], compare_op=ALU.is_ge, fill=0.0, base=0,
                                            pattern=[[-Q, B]], channel_multiplier=1).then_inc(m, 1)
                    pool.wait_ge(m, 2)
                    nc.gpsimd.affine_select(out=before[:], in_=before[:], compare_op=ALU.is_gt, fill=0.0, base=0,
                                            pattern=[[1, 128]], channel_multiplier=-1)
                    nc.gpsimd.affine_select(out=same[:], in_=same[:], compare_op=ALU.is_ge, fill=0.0, base=Q - 1,
                                            pattern=[[Q, B]], channel_multiplier=-1).then_inc(m, 1)

                @block.scalar
                def _(act):
                    nc.scalar.preload_act_table_set("natural_log_exp_and_others")
                    act.wait_ge(m, 3)
                    nc.scalar.activation(decay[:], decay[:], ACT.Exp, bias=ln_bc[:], scale=-DT)

                chain = t.sem("chain")

                @block.vector
                def _(dve):
                    at = [0]

                    def link(ins):
                        at[0] += 1
                        ins.then_inc(chain, 1)
                        dve.wait_ge(chain, at[0])
                    dve.wait_ge(m, 3)
                    nc.vector.tensor_scalar(winT[:], winT[:], cols[:, 0:1], None, ALU.mult)
                    link(nc.vector.tensor_copy(lf[:], li[:]))
                    nc.vector.tensor_tensor_scan(cs[:], one[:], lf[:], 0.0, ALU.mult, ALU.add).then_inc(m, 1)
                    dve.wait_ge(m, 5)
                    link(nc.vector.tensor_copy(carry[:], pp[:, 0:1]))
                    link(nc.vector.tensor_scalar(cs[:], cs[:], carry[:], -1.0, ALU.add, ALU.add))
                    link(nc.vector.tensor_scalar(neg[:], cs[:], 0.0, float(L), ALU.is_lt, ALU.mult))
                    link(nc.vector.tensor_tensor(cs[:], cs[:], neg[:], ALU.add))
                    for j in range(L):
                        ins = nc.vector.tensor_scalar(dump[:], cs[:], float(j), 0.0, ALU.is_equal, ALU.max,
                                                      accum_out=hit[:, j:j + 1])
                        link(ins)
                    dve.sem_inc(m, 1)
                    dve.wait_ge(m, 7)
                    link(nc.vector.tensor_scalar(bm[:], pp[0:B, 64:64 + L], 1.0, None, ALU.min))
                    link(nc.vector.tensor_tensor_scan(cnt[:], one[0:B, 0:L], bm[:], 0.0, ALU.mult, ALU.add))
                    nc.vector.tensor_scalar(cnt[:], cnt[:], -1.0, 0.0, ALU.add, ALU.max).then_inc(m, 1)

                @block.tensor
                def _(pe):
                    pe.wait_ge(m, 4)
                    nc.tensor.matmul(pp[:, 0:1], before[:], cs[:, PQ - 1:PQ], start=True, stop=True).then_inc(m, 1)
                    pe.wait_ge(m, 6)
                    nc.tensor.matmul(pp[0:B, 64:64 + L], same[:], hit[:], start=True, stop=True).then_inc(m, 1)

                @block.sync
                def _(sp):
                    sp.wait_ge(m, 8)
                    sp.dma_start(plug_d, cnt[:]).then_inc(m, 16)
                    sp.wait_ge(m, 24)
                    sp.dma_start(plug[:], plug_d.rearrange("b t -> (b t)").unsqueeze(0).to_broadcast([L, N])).then_inc(m, 16)
                    sp.wait_ge(m, 40)

        cx = [s.sb(f"cx{p}", [L, GB, C]) for p in range(2)]
        scr, ss, sel, wt = s.sb("scr", [L, C]), s.sb("ss", [L, GB]), s.sb("sel", [L, GT]), s.sb("wt", [L, GT])
        sq, rs, h = s.sb("sq", [D, GT]), s.sb("rs", [D, GT]), s.sb("h", [D, GT])
        pw, pd, pv, ph = [[s.ps(f"{n}{p}") for p in range(2)] for n in ("pw", "pd", "pv", "ph")]
        loaded = [s.sem(f"loaded{p}") for p in range(2)]
        squared, rooted, selected, spread, weighed, pooled, hsquared, hsummed, hrooted, hscaled, projected, added, chain = [
            s.sem(n) for n in ("squared", "rooted", "selected", "spread", "weighed", "pooled", "hsquared", "hsummed",
                               "hrooted", "hscaled", "projected", "added", "chain")]
        block = ctx.enter_context(nc.Block())
        H = NG // 2

        @block.sync
        def _(sp):
            with sp.Fori(0, H) as i:
                for p in range(2):
                    sp.wait_ge(added, 2 * i + p + 1)
                    sp.dma_start(cx[p][:], ctxd[bass.ds((2 * i + p) * GB, GB), 0:L, :].rearrange("b t c -> t b c")).then_inc(loaded[p], 16)

        @block.scalar
        def _(act):
            nc.scalar.preload_act_table_set("natural_log_exp_and_others")
            with act.Fori(0, H) as i:
                for p in range(2):
                    g = 2 * i + p
                    act.wait_ge(loaded[p], 16 * i + 16)
                    act.wait_ge(added, g + 2)
                    for b in range(GB):
                        nc.scalar.activation(scr[:], cx[p][:, b, :], ACT.Square, accum_out=ss[:, b:b + 1]).then_inc(squared, 1)
                        act.wait_ge(squared, g * GB + b + 1)
                    nc.scalar.activation(ss[:], ss[:], ACT.Ln, bias=k["eps"][0:L], scale=1.0 / C).then_inc(chain, 1)
                    act.wait_ge(chain, g * 2 + 1)
                    nc.scalar.activation(ss[:], ss[:], ACT.Exp, scale=-0.5).then_inc(rooted, 1)
                    nc.scalar.activation(sq[:], xT[:, bass.ds(g * GT, GT)], ACT.Square).then_inc(hsquared, 1)
                    act.wait_ge(hsummed, g + 1)
                    nc.scalar.activation(rs[:], pv[p][:, 0:GT], ACT.Ln, bias=k["eps"][:]).then_inc(chain, 1)
                    act.wait_ge(chain, g * 2 + 2)
                    nc.scalar.activation(rs[:], rs[:], ACT.Exp, scale=-0.5).then_inc(hrooted, 1)

        @block.vector
        def _(dve):
            dve.sem_inc(added, 2)
            with dve.Fori(0, H) as i:
                for p in range(2):
                    g = 2 * i + p
                    nc.vector.tensor_scalar(sel[:], plug[:, bass.ds(g * GT, GT)], rowid[:], None, ALU.is_equal).then_inc(selected, 1)
                    dve.wait_ge(spread, g + 1)
                    dve.wait_ge(rooted, g + 1)
                    v = lambda x: x.rearrange("t (b u) -> t b u", u=L)
                    nc.vector.tensor_tensor(v(wt[:]), v(pw[p][0:L, 0:GT]), ss[:].unsqueeze(2).to_broadcast([L, GB, L]),
                                            ALU.mult).then_inc(weighed, 1)
                    dve.wait_ge(hrooted, g + 1)
                    x = xT[:, bass.ds(g * GT, GT)]
                    nc.vector.tensor_tensor(h[:], x, rs[:], ALU.mult).then_inc(hscaled, 1)
                    dve.wait_ge(projected, g + 1)
                    nc.vector.scalar_tensor_tensor(out=h[:], in0=ph[p][:, 0:GT], scalar=cols[:, 1:2], in1=x, op0=ALU.add,
                                                   op1=ALU.add).then_inc(pooled, 1)
                    dve.wait_ge(pooled, 2 * g + 2)
                    nc.vector.scalar_tensor_tensor(out=x, in0=pd[p][:, 0:GT], scalar=cols[:, 2:3], in1=h[:], op0=ALU.mult,
                                                   op1=ALU.add).then_inc(added, 1)
                    dve.wait_ge(added, g + 3)

        @block.tensor
        def _(pe):
            with pe.Fori(0, H) as i:
                for p in range(2):
                    g = 2 * i + p
                    pe.wait_ge(added, g + 1)
                    pe.wait_ge(selected, g + 1)
                    nc.tensor.matmul(pw[p][0:L, 0:GT], decay[:], sel[:], start=True, stop=True).then_inc(spread, 1)
                    pe.wait_ge(hsquared, g + 1)
                    nc.tensor.matmul(pv[p][:, 0:GT], k["mean"][:], sq[:], start=True, stop=True).then_inc(hsummed, 1)
                    pe.wait_ge(loaded[p], 16 * i + 16)
                    pe.wait_ge(weighed, g + 1)
                    for b in range(GB):
                        ins = nc.tensor.matmul(pd[p][:, b * L:(b + 1) * L], cx[p][:, b, 0:D], wt[:, b * L:(b + 1) * L],
                                               start=True, stop=True)
                    ins.then_inc(pooled, 1)
                    pe.wait_ge(hscaled, g + 1)
                    nc.tensor.matmul(ph[p][:, 0:GT], winT[:], h[:], start=True, stop=True).then_inc(projected, 1)


def l0_ffn(nc, k, a):
    xT, gw = k["xT"], a["L0_ffn_gate_w"]
    E, F = a["L0_ffn_Wg"].shape[0], a["L0_ffn_Wg"].shape[1]
    FC = F // 128
    CAP = int(L * 2.0 / E)
    BT = 128 // E
    TT = BT * L
    SL = BT * CAP
    EH = E // 2
    HS = EH * CAP
    NT = B // BT
    W8 = L + 4
    assert 8 < CAP <= 12
    with ExitStack() as ctx:
        s = Stage(nc, ctx, "l0f")
        gT = s.sb("gT", [D, E])
        wgT, wuT, wdT = s.sb("wgT", [D, E + 1, F]), s.sb("wuT", [D, E + 1, F]), s.sb("wdT", [128, E + 1, FC, D])
        items = [(gT[:], gw)]
        for e in range(E + 1):
            g_, u_, d_ = (a["L0_ffn_Wg"][e], a["L0_ffn_Wu"][e], a["L0_ffn_Wd"][e]) if e < E else (
                a["L0_ffn_Ws_g"], a["L0_ffn_Ws_u"], a["L0_ffn_Ws_d"])
            for c in range(FC):
                f = slice(c * 128, c * 128 + 128)
                items += [(wgT[:, e, f], g_[f, :]), (wuT[:, e, f], u_[f, :]), (wdT[:, e, c, :], d_[:, f])]
        load_transposed(nc, k, "l0ft", items)
        xs, xtm = s.sb("xs", [D, TT]), s.sb("xtm", [L, BT, D])
        sco, st = s.sb("sco", [L, BT, E]), s.sb("st", [L, 4, BT])
        row, rep, rep2, m8, m8b = s.sb("row", [128, W8]), s.sb("rep", [128, W8]), s.sb("rep2", [128, W8]), s.sb("m8", [128, 8]), s.sb("m8b", [128, 8])
        one, pos = s.sb("one", [128, L]), s.sb("pos", [128, L])
        slot = s.sb("slot", [L, E, CAP])
        oh, ohw = s.sb("oh", [L, BT, E, CAP]), s.sb("ohw", [L, BT, E, CAP])
        posT = s.sb("posT", [L, BT, E])
        xg, eog = s.sb("xg", [D, E, BT, CAP]), s.sb("eog", [D, BT, E * CAP])
        act_g, hh = [s.sb(f"ag{p}", [128, FC, TT // 2]) for p in range(2)], [s.sb(f"hh{p}", [128, FC, TT // 2]) for p in range(2)]
        eoS, owS = [s.sb(f"eoS{p}", [HS, 2, D]) for p in range(2)], [s.sb(f"owS{p}", [HS, 2, L]) for p in range(2)]
        pt = [s.ps(f"pt{p}") for p in range(2)]
        pg, pu, pa = [s.ps(f"pg{p}") for p in range(2)], [s.ps(f"pu{p}") for p in range(2)], [s.ps(f"pa{p}") for p in range(2)]
        names = ("staged", "turned", "tcopied", "scored", "smaxed", "exped", "weighted", "rowed", "rowcopied", "posed",
                 "posturned", "hot", "gathered", "gcopied", "gated", "upped", "geluted", "multiplied", "downed", "ecopied",
                 "slotted", "scopied", "scattered", "added")
        q = {n: s.sem(n) for n in names}
        vch, m = s.sem("vch"), s.sem("m")
        steps = [(e, SL) for e in range(E)] + [(E, TT // 2), (E, TT // 2)]
        NS = len(steps)
        block = ctx.enter_context(nc.Block())

        def moving(n):
            return xg[:, n].rearrange("d b c -> d (b c)") if n < E else xs[:, (n - E) * (TT // 2):(n - E + 1) * (TT // 2)]

        @block.gpsimd
        def _(pool):
            nc.gpsimd.memset(one[:], 1.0)
            for j in range(4):
                nc.gpsimd.memset(row[:, L + j:L + j + 1], -2.0 - j)
                nc.gpsimd.memset(m8b[:, 4 + j:5 + j], -2.0 - j)
            nc.gpsimd.iota(slot[:], pattern=[[0, E], [1, CAP]], base=1, channel_multiplier=0,
                           allow_small_or_imprecise_dtypes=True).then_inc(m, 1)

        @block.tensor
        def _(pe):
            with pe.Fori(0, NT) as i:
                pe.wait_ge(q["staged"], i + 1)
                for b in range(BT):
                    n = i * BT + b
                    if b >= 2:
                        pe.wait_ge(q["tcopied"], n - 1)
                    nc.tensor.transpose(pt[b % 2][0:L, 0:D], xs[:, b * L:(b + 1) * L], k["ident"][:]).then_inc(q["turned"], 1)
                pe.wait_ge(q["tcopied"], i * BT + BT)
                for b in range(BT):
                    ins = nc.tensor.matmul(pt[0][0:L, b * E:(b + 1) * E], xs[:, b * L:(b + 1) * L], gT[:], start=True, stop=True)
                ins.then_inc(q["scored"], 1)
                pe.wait_ge(q["weighted"], i + 1)
                nc.tensor.transpose(pt[1][:, 0:L], sco[:].rearrange("t b e -> t (b e)"), k["ident"][0:L, 0:L]).then_inc(q["rowed"], 1)
                pe.wait_ge(q["posed"], i + 1)
                nc.tensor.transpose(pt[0][0:L, 0:128], pos[:], k["ident"][:]).then_inc(q["posturned"], 1)
                pe.wait_ge(q["hot"], i + 1)
                for b in range(BT):
                    n = i * BT + b
                    if b >= 2:
                        pe.wait_ge(q["gcopied"], n - 1)
                    nc.tensor.matmul(pt[b % 2][:, 0:E * CAP], xtm[:, b, :], oh[:, b].rearrange("t e c -> t (e c)"),
                                     start=True, stop=True).then_inc(q["gathered"], 1)
                pe.wait_ge(q["gcopied"], i * BT + BT)

                def down(n):
                    e, w = steps[n]
                    pe.wait_ge(q["multiplied"], i * NS + n + 1)
                    if n >= 2:
                        pe.wait_ge(q["ecopied"], i * E + min(n - 1, E))
                    for c in range(FC):
                        ins = nc.tensor.matmul(pa[n % 2][:, 0:w], wdT[:, e, c, :], hh[n % 2][:, c, 0:w],
                                               start=(c == 0), stop=(c == FC - 1 and n < E), skip_group_check=True)
                    ins.then_inc(q["downed"], 1)
                for n, (e, w) in enumerate(steps):
                    for c in range(FC):
                        o, f = c * (512 // FC), slice(c * 128, c * 128 + 128)
                        if w > 512 // FC:
                            if n > E or c == 0:
                                pe.wait_ge(q["multiplied"], i * NS + n)
                            nc.tensor.matmul(pg[c][:, 0:w], wgT[:, e, f], moving(n), start=True, stop=True).then_inc(q["gated"], 1)
                            nc.tensor.matmul(pu[c][:, 0:w], wuT[:, e, f], moving(n), start=True, stop=True).then_inc(q["upped"], 1)
                        else:
                            if n >= 2 and c == 0:
                                pe.wait_ge(q["multiplied"], i * NS + n - 1)
                            nc.tensor.matmul(pg[n % 2][:, o:o + w], wgT[:, e, f], moving(n), start=True, stop=True).then_inc(q["gated"], 1)
                            nc.tensor.matmul(pu[n % 2][:, o:o + w], wuT[:, e, f], moving(n), start=True, stop=True).then_inc(q["upped"], 1)
                    if n >= 1 and n < E + 1:
                        down(n - 1)
                down(E)
                down(E + 1)
                for b in range(BT):
                    n = i * BT + b
                    if b >= 2:
                        pe.wait_ge(q["scopied"], n - 1)
                    for h in range(2):
                        nc.tensor.transpose(pt[b % 2][0:HS, h * D:(h + 1) * D],
                                            eog[:, b, h * HS:(h + 1) * HS],
                                            k["ident"][:])
                    for h in range(2):
                        ins = nc.tensor.transpose(pt[b % 2][0:HS, 2 * D + h * L:2 * D + (h + 1) * L],
                                                  ohw[:, b, h * EH:(h + 1) * EH].rearrange("t e c -> t (e c)"), k["ident"][0:L, 0:L])
                    ins.then_inc(q["slotted"], 1)
                    pe.wait_ge(q["scopied"], n + 1)
                    dst = pa[b // (BT // 2)][:, b % (BT // 2) * L:(b % (BT // 2) + 1) * L]
                    for h in range(2):
                        ins = nc.tensor.matmul(dst, eoS[b % 2][:, h, :], owS[b % 2][:, h, :], start=False, stop=(h == 1),
                                               skip_group_check=True)
                    ins.then_inc(q["scattered"], 1)

        @block.scalar
        def _(act):
            with act.Fori(0, NT) as i:
                for b in range(BT):
                    n = i * BT + b
                    act.wait_ge(q["turned"], n + 1)
                    nc.scalar.activation(xtm[:, b, :], pt[b % 2][0:L, 0:D], ACT.Copy).then_inc(q["tcopied"], 1)
                act.wait_ge(q["smaxed"], i + 1)
                nc.scalar.activation(sco[:], sco[:], ACT.Exp).then_inc(q["exped"], 1)
                for b in range(BT):
                    n = i * BT + b
                    act.wait_ge(q["gathered"], n + 1)
                    nc.scalar.activation(xg[:, :, b, :], pt[b % 2][:, 0:E * CAP].rearrange("d (e c) -> d e c", c=CAP),
                                         ACT.Copy).then_inc(q["gcopied"], 1)
                for n, (e, w) in enumerate(steps):
                    act.wait_ge(q["gated"], (i * NS + n + 1) * FC)
                    if n >= 2:
                        act.wait_ge(q["multiplied"], i * NS + n - 1)
                    if w > 512 // FC:
                        for c in range(FC):
                            ins = nc.scalar.activation(act_g[n % 2][:, c, 0:w], pg[c][:, 0:w], ACT.Gelu)
                    else:
                        ins = nc.scalar.activation(act_g[n % 2][:, :, 0:w],
                                                   pg[n % 2][:].rearrange("f (c s) -> f c s", c=FC)[:, :, 0:w], ACT.Gelu)
                    ins.then_inc(q["geluted"], 1)
                for b in range(BT):
                    n = i * BT + b
                    act.wait_ge(q["slotted"], n + 1)
                    if b >= 2:
                        act.wait_ge(q["scattered"], n - 1)
                    nc.scalar.activation(eoS[b % 2][:].rearrange("s h d -> s (h d)"), pt[b % 2][0:HS, 0:2 * D], ACT.Copy)
                    nc.scalar.activation(owS[b % 2][:].rearrange("s h t -> s (h t)"), pt[b % 2][0:HS, 2 * D:2 * D + 2 * L],
                                         ACT.Copy).then_inc(q["scopied"], 1)

        held = s.sem("held")

        @block.vector
        def _(dve):
            dve.wait_ge(m, 1)
            CH = 11
            with dve.Fori(0, NT) as i:
                at = [0]

                def link(ins):
                    at[0] += 1
                    ins.then_inc(vch, 1)
                    dve.wait_ge(vch, i * CH + at[0])
                bc = lambda n: st[:, n, :].unsqueeze(2).to_broadcast([L, BT, E])
                logit = pt[0][0:L, 0:128].rearrange("t (b e) -> t b e", e=E)
                nc.vector.tensor_copy(xs[:], xT[:, bass.ds(i * TT, TT)]).then_inc(q["staged"], 1)
                dve.wait_ge(q["scored"], i + 1)
                link(nc.vector.tensor_reduce(st[:, 0, :], logit, AX, ALU.max))
                nc.vector.tensor_tensor(sco[:], logit, bc(0), ALU.subtract).then_inc(q["smaxed"], 1)
                dve.wait_ge(q["exped"], i + 1)
                link(nc.vector.tensor_reduce(st[:, 1, :], sco[:], AX, ALU.add))
                link(nc.vector.reciprocal(st[:, 2, :], st[:, 1, :]))
                nc.vector.tensor_tensor(sco[:], sco[:], bc(2), ALU.mult).then_inc(q["weighted"], 1)
                dve.wait_ge(q["rowed"], i + 1)
                link(nc.vector.tensor_copy(row[:, 0:L], pt[1][:, 0:L]))
                dve.sem_inc(held, 1)
                link(nc.vector.max(m8[:], row[:]))
                dve.sem_inc(held, 1)
                link(nc.vector.match_replace(rep[:], m8[:], row[:], -1.0))
                dve.sem_inc(held, 1)
                link(nc.vector.max(m8[:], rep[:]))
                link(nc.vector.tensor_copy(m8b[:, 0:CAP - 8], m8[:, 0:CAP - 8]))
                dve.sem_inc(held, 1)
                link(nc.vector.match_replace(rep2[:], m8b[:], rep[:], -1.0))
                link(nc.vector.tensor_scalar(rep2[:, 0:L], rep2[:, 0:L], -1.0, None, ALU.is_equal))
                link(nc.vector.tensor_tensor_scan(pos[:], one[:], rep2[:, 0:L], 0.0, ALU.mult, ALU.add))
                nc.vector.tensor_tensor(pos[:], pos[:], rep2[:, 0:L], ALU.mult).then_inc(q["posed"], 1)
                dve.wait_ge(q["posturned"], i + 1)
                nc.vector.tensor_copy(posT[:].rearrange("t b e -> t (b e)"), pt[0][0:L, 0:128]).then_inc(q["rowcopied"], 1)
                dve.wait_ge(q["rowcopied"], i + 1)
                for b in range(BT):
                    ins = nc.vector.tensor_tensor(oh[:, b], posT[:, b, :].unsqueeze(2).to_broadcast([L, E, CAP]), slot[:], ALU.is_equal)
                ins.then_inc(q["hot"], 1)
                dve.wait_ge(q["hot"], i + 1)
                for b in range(BT):
                    nc.vector.tensor_tensor(ohw[:, b], oh[:, b], sco[:, b, :].unsqueeze(2).to_broadcast([L, E, CAP]), ALU.mult)

                def take(n):
                    dve.wait_ge(q["downed"], i * NS + n + 1)
                    dst = eog[:].rearrange("d b (e c) -> d e b c", c=CAP)[:, n]
                    nc.vector.tensor_copy(dst, pa[n % 2][:, 0:SL].rearrange("d (b c) -> d b c", c=CAP)).then_inc(q["ecopied"], 1)
                for n, (e, w) in enumerate(steps):
                    dve.wait_ge(q["geluted"], i * NS + n + 1)
                    dve.wait_ge(q["upped"], (i * NS + n + 1) * FC)
                    if n >= 2:
                        dve.wait_ge(q["downed"], i * NS + n - 1)
                    if w > 512 // FC:
                        for c in range(FC):
                            ins = nc.vector.tensor_tensor(hh[n % 2][:, c, 0:w], act_g[n % 2][:, c, 0:w], pu[c][:, 0:w], ALU.mult)
                    else:
                        ins = nc.vector.tensor_tensor(hh[n % 2][:, :, 0:w], act_g[n % 2][:, :, 0:w],
                                                      pu[n % 2][:].rearrange("f (c s) -> f c s", c=FC)[:, :, 0:w], ALU.mult)
                    ins.then_inc(q["multiplied"], 1)
                    if 1 <= n <= E:
                        take(n - 1)
                dve.wait_ge(q["scattered"], i * BT + BT)
                x = xT[:, bass.ds(i * TT, TT)].rearrange("d (h t) -> d h t", h=2)
                xh = xs[:].rearrange("d (h t) -> d h t", h=2)
                for h in range(2):
                    ins = nc.vector.tensor_tensor(x[:, h], xh[:, h], pa[h][:, 0:TT // 2], ALU.add)
                ins.then_inc(q["added"], 1)
                dve.wait_ge(q["added"], i + 1)
                assert at[0] == CH, at[0]


MAGIC = 1.5 * 2.0 ** 23


def l2_ffn(nc, k, a):
    xT = k["xT"]
    F = a["L2_ffn_w1"].shape[0]
    C = F // 128
    with ExitStack() as ctx:
        s = Stage(nc, ctx, "l2f")
        w1, w2, b1, b2 = s.sb("w1", [128, C, D]), s.sb("w2", [128, C, 128]), s.sb("b1", [128, C]), s.sb("b2", [D, 1])
        load(nc, "l2fl", [(w1[:], a["L2_ffn_w1"].rearrange("(c f) d -> f c d", f=128)),
                          (w2[:], a["L2_ffn_w2"].rearrange("d (c f) -> d c f", f=128)),
                          (b1[:], a["L2_ffn_b1"].rearrange("(c f) -> f c", f=128)), (b2[:], col(a["L2_ffn_b2"]))])
        w1q, w2q = s.sb("w1q", [128, C, D], BF16), s.sb("w2q", [128, C, 128], BF16)
        w1t, w2t = s.sb("w1t", [D, C, 128], BF16), s.sb("w2t", [128, C, D], BF16)
        identb, absw = s.sb("identb", [128, 128], BF16), s.sb("absw", [128, C, 128])
        sw, rsw = s.sb("sw", [128, C + 1]), s.sb("rsw", [128, C + 1])
        top, tall, sx, rsx = s.sb("top", [128, NG + 1]), s.sb("tall", [128, 2]), s.sb("sx", [128, 2]), s.sb("rsx", [128, 2])
        sb1, rb1, bq1 = s.sb("sb1", [128, C]), s.sb("rb1", [128, C]), s.sb("bq1", [128, C])
        sb2, rb2, bq2 = s.sb("sb2", [128, 1]), s.sb("rb2", [128, 1]), s.sb("bq2", [128, 1])
        h = s.sb("h", [128, C, N])
        xr, xq, magic = s.sb("xr", [D, GT]), s.sb("xq", [D, GT], BF16), s.sb("magic", [128, 1])
        hr, hq = [s.sb(f"hr{p}", [128, C, GT]) for p in range(2)], [s.sb(f"hq{p}", [128, C, GT], BF16) for p in range(2)]
        pq = s.ps("pq", (128, 1024), BF16)
        ph = s.ps("ph", (128, 2048))
        po = [s.ps(f"po{p}") for p in range(2)]
        v, weighed, turned, topped, maxed = [s.sem(x) for x in ("v", "weighed", "turned", "topped", "maxed")]
        with nc.Block() as block:
            @block.vector
            def _(dve):
                at = [0]

                def link(ins):
                    at[0] += 1
                    ins.then_inc(v, 1)
                    dve.wait_ge(v, at[0])
                def integers(dst, src, tmp):
                    link(nc.vector.tensor_scalar(tmp, src, MAGIC, MAGIC - 128, ALU.add, ALU.max))
                    link(nc.vector.tensor_scalar(dst, tmp, MAGIC + 127, MAGIC, ALU.min, ALU.subtract))
                nc.vector.memset(magic[:], MAGIC)
                nc.vector.tensor_copy(identb[:], k["ident"][:])
                nc.vector.reduce_max(top[:, 0:1], xT[:], AX).then_inc(topped, 1)
                link(nc.vector.scalar_tensor_tensor(out=absw[:], in0=w1[:], scalar=-1.0, in1=w1[:], op0=ALU.mult, op1=ALU.max))
                link(nc.vector.tensor_reduce(sw[:, 0:C], absw[:], AX, ALU.max))
                link(nc.vector.scalar_tensor_tensor(out=absw[:], in0=w2[:], scalar=-1.0, in1=w2[:], op0=ALU.mult, op1=ALU.max))
                link(nc.vector.reduce_max(sw[:, C:C + 1], absw[:].rearrange("d c f -> d (c f)"), AX))
                link(nc.vector.tensor_scalar(sw[:], sw[:], 1e-8, 1.0 / 127.0, ALU.max, ALU.mult))
                link(nc.vector.reciprocal(rsw[:], sw[:]))
                link(nc.vector.tensor_tensor(absw[:], w1[:], rsw[:, 0:C].unsqueeze(2).to_broadcast([128, C, D]), ALU.mult))
                integers(w1q[:], absw[:], absw[:])
                link(nc.vector.tensor_scalar(absw[:], w2[:], rsw[:, C:C + 1], None, ALU.mult))
                integers(w2q[:], absw[:], absw[:])
                dve.sem_inc(weighed, 1)
                dve.wait_ge(turned, 1)
                dve.wait_ge(maxed, 1)
                pv = pq[:].rearrange("p (n d) -> p n d", d=128)
                nc.vector.tensor_copy(w1t[:], pv[:, 0:C])
                nc.vector.tensor_copy(w2t[:], pv[:, C:2 * C])
                link(nc.vector.tensor_scalar(sx[:, 0:1], tall[:, 0:1], 1e-8, 1.0 / 255.0, ALU.max, ALU.mult))
                link(nc.vector.reciprocal(rsx[:, 0:1], sx[:, 0:1]))
                link(nc.vector.tensor_scalar(sb1[:], sw[:, 0:C], sx[:, 0:1], None, ALU.mult))
                link(nc.vector.reciprocal(rb1[:], sb1[:]))
                link(nc.vector.tensor_tensor(bq1[:], b1[:], rb1[:], ALU.mult))
                link(nc.vector.tensor_scalar(bq1[:], bq1[:], MAGIC, MAGIC, ALU.add, ALU.subtract))
                link(nc.vector.tensor_tensor(bq1[:], bq1[:], sb1[:], ALU.mult))

            @block.tensor
            def _(pe):
                pe.wait_ge(weighed, 1)
                for c in range(C):
                    nc.tensor.transpose(pq[:, c * 128:c * 128 + 128], w1q[:, c, :], identb[:])
                for c in range(C):
                    ins = nc.tensor.transpose(pq[:, (C + c) * 128:(C + c + 1) * 128], w2q[:, c, :], identb[:])
                ins.then_inc(turned, 1)

            @block.gpsimd
            def _(pool):
                pool.wait_ge(topped, 1)
                nc.gpsimd.partition_all_reduce(tall[:, 0:1], top[:, 0:1], 128, bass.bass_isa.ReduceOp.max).then_inc(maxed, 1)

        rounded, clamped, ready, producted, relued = [s.sem(n) for n in ("rounded", "clamped", "ready", "producted", "relued")]
        with nc.Block() as block:
            @block.scalar
            def _(act):
                with act.Fori(0, NG) as i:
                    act.wait_ge(ready, i + 1)
                    nc.scalar.activation(xr[:], xT[:, bass.ds(i * GT, GT)], ACT.Identity, bias=magic[:],
                                         scale=rsx[:, 0:1]).then_inc(rounded, 1)
                    for c in range(C):
                        act.wait_ge(producted, i * C + c + 1)
                        nc.scalar.activation(h[:, c, bass.ds(i * GT, GT)], ph[:, c * 512:c * 512 + GT], ACT.Relu,
                                             bias=bq1[:, c:c + 1], scale=sb1[:, c:c + 1]).then_inc(relued, 1)

            @block.vector
            def _(dve):
                dve.sem_inc(ready, 1)
                with dve.Fori(0, NG) as i:
                    dve.wait_ge(rounded, i + 1)
                    nc.vector.tensor_scalar(xr[:], xr[:], MAGIC, MAGIC + 255, ALU.max, ALU.min).then_inc(clamped, 1)
                    dve.wait_ge(clamped, i + 1)
                    nc.vector.tensor_scalar(xq[:], xr[:], MAGIC, None, ALU.subtract).then_inc(ready, 1)
                    dve.wait_ge(relued, (i + 1) * C)
                    nc.vector.tensor_reduce(top[:, bass.ds(i + 1, 1)], h[:, :, bass.ds(i * GT, GT)], mybir.AxisListType.XY, ALU.max)

            @block.tensor
            def _(pe):
                with pe.Fori(0, NG) as i:
                    pe.wait_ge(ready, i + 2)
                    for c in range(C):
                        nc.tensor.matmul(ph[:, c * 512:c * 512 + GT], w1t[:, c, :], xq[:], start=True,
                                         stop=True).then_inc(producted, 1)

        n = s.sem("n")
        with nc.Block() as block:
            @block.vector
            def _(dve):
                at = [0]

                def link(ins):
                    at[0] += 1
                    ins.then_inc(n, 1)
                    dve.wait_ge(n, at[0])
                link(nc.vector.reduce_max(top[:, 0:1], top[:, 1:NG + 1], AX))
                dve.wait_ge(n, 2)
                at[0] += 1
                link(nc.vector.tensor_scalar(sx[:, 1:2], tall[:, 1:2], 1e-8, 1.0 / 255.0, ALU.max, ALU.mult))
                link(nc.vector.reciprocal(rsx[:, 1:2], sx[:, 1:2]))
                link(nc.vector.tensor_tensor(sb2[:], sw[:, C:C + 1], sx[:, 1:2], ALU.mult))
                link(nc.vector.reciprocal(rb2[:], sb2[:]))
                link(nc.vector.tensor_tensor(bq2[:], b2[:], rb2[:], ALU.mult))
                link(nc.vector.tensor_scalar(bq2[:], bq2[:], MAGIC, MAGIC, ALU.add, ALU.subtract))
                link(nc.vector.tensor_tensor(bq2[:], bq2[:], sb2[:], ALU.mult))

            @block.gpsimd
            def _(pool):
                pool.wait_ge(n, 1)
                nc.gpsimd.partition_all_reduce(tall[:, 1:2], top[:, 0:1], 128, bass.bass_isa.ReduceOp.max).then_inc(n, 1)

        hrounded, hclamped, hready, hproducted, scaled, added = [s.sem(x) for x in
            ("hrounded", "hclamped", "hready", "hproducted", "scaled", "added")]
        block = ctx.enter_context(nc.Block())

        @block.scalar
        def _(act):
            with act.Fori(0, NG // 2) as i:
                for p in range(2):
                    g = 2 * i + p
                    act.wait_ge(hready, g + 1)
                    nc.scalar.activation(hr[p][:], h[:, :, bass.ds(g * GT, GT)], ACT.Identity, bias=magic[:],
                                         scale=rsx[:, 1:2]).then_inc(hrounded, 1)

        @block.vector
        def _(dve):
            dve.sem_inc(hready, 2)
            dve.sem_inc(added, 2)
            with dve.Fori(0, NG // 2) as i:
                for p in range(2):
                    g = 2 * i + p
                    dve.wait_ge(hrounded, g + 1)
                    nc.vector.tensor_scalar(hr[p][:], hr[p][:], MAGIC, MAGIC + 255, ALU.max, ALU.min).then_inc(hclamped, 1)
                    dve.wait_ge(hclamped, g + 1)
                    nc.vector.tensor_scalar(hq[p][:], hr[p][:], MAGIC, None, ALU.subtract).then_inc(hready, 1)
                for p in range(2):
                    g = 2 * i + p
                    dve.wait_ge(hproducted, g + 1)
                    x = xT[:, bass.ds(g * GT, GT)]
                    nc.vector.tensor_scalar(xr[:], po[p][:, 0:GT], sb2[:], bq2[:], ALU.mult, ALU.add).then_inc(scaled, 1)
                    dve.wait_ge(scaled, g + 1)
                    nc.vector.tensor_tensor(x, x, xr[:], ALU.add).then_inc(added, 1)
                    dve.wait_ge(added, g + 3)

        @block.tensor
        def _(pe):
            with pe.Fori(0, NG // 2) as i:
                for p in range(2):
                    g = 2 * i + p
                    pe.wait_ge(hready, g + 3)
                    for c in range(C):
                        ins = nc.tensor.matmul(po[p][:, 0:GT], w2t[:, c, :], hq[p][:, c, :], start=(c == 0), stop=(c == C - 1))
                    ins.then_inc(hproducted, 1)


def l3_attn(nc, k, a):
    xT = k["xT"]
    DI, DS, G = 2 * D, a["L3_attn_A_log"].shape[0], 16
    GS = DI // G
    HG = 128 // DS
    F = a["L3_attn_W_ffn1"].shape[0]
    FC = F // 128
    R = 1 + 2 * DS
    with ExitStack() as ctx:
        s = Stage(nc, ctx, "l3a")
        winT, wparT = s.sb("winT", [D, 2 * DI]), s.sb("wparT", [128, 2, 2, 3, 128])
        woutT, wf1T, wf2T = s.sb("woutT", [128, 2, D]), s.sb("wf1T", [D, F]), s.sb("wf2T", [128, FC, D])
        cols, alog, bf1 = s.sb("cols", [D, 4]), s.sb("alog", [128, 4]), s.sb("bf1", [128, FC])
        wp = a["L3_attn_W_param"]
        par = s.sb("par", [128, 2, 3, DI])
        wpg = wp.rearrange("(g r) i -> g r i", r=R)
        pairs = [(par[:, h, 1 + kind, :], wpg[h * HG:(h + 1) * HG, 1 + kind * DS:1 + (kind + 1) * DS, :])
                 for h in range(2) for kind in range(2)]
        pairs += [(par[:, h, 0, :], wpg[h * HG:(h + 1) * HG, 0:1, :].to_broadcast([HG, DS, DI])) for h in range(2)]
        pairs += [(cols[:, 0:1], col(a["L3_attn_g1"])), (cols[:, 1:2], col(a["L3_attn_g2"])), (cols[:, 2:3], col(a["L3_attn_b_ffn2"])),
                  (bf1[:], a["L3_attn_b_ffn1"].rearrange("(c f) -> f c", f=128)),
                  (alog[:, 0:1], a["L3_attn_A_log"].rearrange("(o n x) -> o n x", o=1, x=1).to_broadcast([HG, DS, 1]))]
        load(nc, "l3al", pairs)
        blk = lambda name, o, i: a[name][o * 128:(o + 1) * 128, i * 128:(i + 1) * 128]
        load_transposed(nc, k, "l3at", [(winT[:, c * 128:(c + 1) * 128], blk("L3_attn_W_in", c, 0)) for c in range(4)]
                        + [(woutT[:, c, :], blk("L3_attn_W_out", 0, c)) for c in range(2)]
                        + [(wf1T[:, c * 128:(c + 1) * 128], blk("L3_attn_W_ffn1", c, 0)) for c in range(FC)]
                        + [(wf2T[:, c, :], blk("L3_attn_W_ffn2", 0, c)) for c in range(FC)])
        pick, drop = s.sb("pick", [128, GS, 128]), s.sb("drop", [128, GS, 128])
        eps6 = s.sb("eps6", [128, 1])
        m, mv = s.sem("m"), s.sem("mv")
        pt = s.ps("pt", (128, 1536))
        with nc.Block() as block:
            @block.gpsimd
            def _(pool):
                nc.gpsimd.memset(eps6[:], 1e-6)
                nc.gpsimd.memset(pick[:], 1.0)
                nc.gpsimd.memset(drop[:], 1.0).then_inc(m, 1)
                pool.wait_ge(m, 1)
                dv = drop[:].rearrange("p c (g e) -> p c g e", e=GS)
                for c in range(GS):
                    pv = pick[:, c].rearrange("p (g n) -> p g n", n=DS)
                    nc.gpsimd.affine_select(out=pv, in_=pv, compare_op=ALU.is_equal, fill=0.0, base=-c,
                                            pattern=[[-GS, HG], [0, DS]], channel_multiplier=1)
                    ins = nc.gpsimd.affine_select(out=dv[:, c], in_=dv[:, c], compare_op=ALU.is_ge, fill=0.0, base=0,
                                                  pattern=[[-DS, HG], [0, GS]], channel_multiplier=1)
                ins.then_inc(m, 1)
                pool.wait_ge(m, 2)
                for c in range(GS):
                    ins = nc.gpsimd.affine_select(out=dv[:, c], in_=dv[:, c], compare_op=ALU.is_ge, fill=0.0, base=DS - 1,
                                                  pattern=[[DS, HG], [0, GS]], channel_multiplier=-1)
                ins.then_inc(m, 1)
                pool.wait_ge(m, 3)
                for c in range(GS):
                    ins = nc.gpsimd.affine_select(out=dv[:, c], in_=dv[:, c], compare_op=ALU.is_equal, fill=0.0, base=-c,
                                                  pattern=[[0, HG], [1, GS]], channel_multiplier=0)

            @block.tensor
            def _(pe):
                for n in range(12):
                    j, h, kind = n // 6, n // 3 % 2, n % 3
                    ins = nc.tensor.transpose(pt[:, n * 128:(n + 1) * 128], par[:, h, kind, j * 128:(j + 1) * 128], k["ident"][:])
                ins.then_inc(mv, 1)

            @block.scalar
            def _(act):
                nc.scalar.activation(alog[:, 1:2], alog[:, 0:1], ACT.Exp).then_inc(mv, 1)

            @block.vector
            def _(dve):
                nc.vector.tensor_scalar(winT[:], winT[:], cols[:, 0:1], None, ALU.mult)
                nc.vector.tensor_scalar(wf1T[:], wf1T[:], cols[:, 1:2], None, ALU.mult)
                dve.wait_ge(mv, 2)
                nc.vector.tensor_copy(wparT[:].rearrange("i j h z n -> i (j h z n)"), pt[:])
                nc.vector.tensor_scalar(alog[:, 2:3], alog[:, 1:2], -1.0, None, ALU.mult).then_inc(mv, 1)
                dve.wait_ge(mv, 3)
                nc.vector.tensor_scalar(alog[:, 1:2], alog[:, 2:3], 1e-12, None, ALU.add).then_inc(mv, 1)
                dve.wait_ge(mv, 4)
                nc.vector.reciprocal(alog[:, 3:4], alog[:, 1:2])

        pg, pu, py = [[pt[:, 512 * p:512 * p + GT] for p in range(2)], [s.ps(f"pu{p}") for p in range(2)], [s.ps(f"py{p}") for p in range(2)]]
        pn = pt[:, 1024:1024 + GT]
        pw = s.ps("pw")
        sq, r, z, x1 = [s.sb(n, [D, GT]) for n in ("sq", "r", "z", "x1")]
        xz, prm = s.sb("xz", [128, 4, GT]), s.sb("prm", [128, 3, 2, GT])
        sp_, ea, fr, dl = [s.sb(n, [128, 2, GT]) for n in ("sp", "ea", "fr", "dl")]
        bu, hs, hc = [[s.sb(f"{n}{p}", [128, GT]) for p in range(2)] for n in ("bu", "hs", "hc")]
        ym, hf = s.sb("ym", [128, 2, GT]), s.sb("hf", [128, FC, GT])
        q = {n: s.sem(n) for n in ("squared", "summed", "logged", "rooted", "normed", "inned", "silued", "parmed", "pcopied",
                                   "absed", "soft1", "soft2", "delta", "clipped", "exped", "ready", "picked", "bued",
                                   "scanned", "used", "dropped", "gated", "outed", "x1ed", "ffed", "ffsilued", "ffouted", "added")}
        ch = s.sem("ch")
        NS = 2 * GS
        block = ctx.enter_context(nc.Block())

        @block.tensor
        def _(pe):
            with pe.Fori(0, NG) as i:
                pe.wait_ge(q["squared"], 2 * i + 1)
                nc.tensor.matmul(pn, k["mean"][:], sq[:], start=True, stop=True).then_inc(q["summed"], 1)
                pe.wait_ge(q["normed"], 2 * i + 1)
                for n in range(4):
                    if n >= 2:
                        pe.wait_ge(q["silued"], 4 * i + n - 1)
                    nc.tensor.matmul(pg[n % 2], winT[:, n * 128:(n + 1) * 128], z[:], start=True, stop=True).then_inc(q["inned"], 1)
                pe.wait_ge(q["silued"], 4 * i + 4)
                for n in range(6):
                    kind, h = n // 2, n % 2
                    if n >= 2:
                        pe.wait_ge(q["pcopied"], 6 * i + n - 1)
                    for j in range(2):
                        ins = nc.tensor.matmul(pg[n % 2], wparT[:, j, h, kind, :], xz[:, j, :], start=(j == 0), stop=(j == 1))
                    ins.then_inc(q["parmed"], 1)

                def drop_(n):
                    pe.wait_ge(q["used"], i * NS + n + 1)
                    nc.tensor.matmul(py[n % 2][:, 0:GT], drop[:, n // 2, :], hc[n % 2][:], start=(n < 2),
                                     stop=(n >= NS - 2)).then_inc(q["dropped"], 1)
                for n in range(NS):
                    if n >= 2:
                        pe.wait_ge(q["bued"], i * NS + n - 1)
                    nc.tensor.matmul(pu[n % 2][:, 0:GT], pick[:, n // 2, :], xz[:, n % 2, :], start=True, stop=True).then_inc(q["picked"], 1)
                    if n >= 2:
                        drop_(n - 2)
                drop_(NS - 2)
                drop_(NS - 1)
                pe.wait_ge(q["gated"], i + 1)
                for h in range(2):
                    ins = nc.tensor.matmul(pw[:, 0:GT], woutT[:, h, :], ym[:, h, :], start=(h == 0), stop=(h == 1))
                ins.then_inc(q["outed"], 1)
                pe.wait_ge(q["squared"], 2 * i + 2)
                nc.tensor.matmul(pn, k["mean"][:], sq[:], start=True, stop=True).then_inc(q["summed"], 1)
                pe.wait_ge(q["normed"], 2 * i + 2)
                for c in range(FC):
                    if c >= 2:
                        pe.wait_ge(q["ffsilued"], FC * i + c - 1)
                    nc.tensor.matmul(pg[c % 2], wf1T[:, c * 128:(c + 1) * 128], z[:], start=True, stop=True).then_inc(q["ffed"], 1)
                for c in range(FC):
                    pe.wait_ge(q["ffsilued"], FC * i + c + 1)
                    ins = nc.tensor.matmul(pw[:, 0:GT], wf2T[:, c, :], hf[:, c, :], start=(c == 0), stop=(c == FC - 1))
                ins.then_inc(q["ffouted"], 1)

        @block.scalar
        def _(act):
            def root(i, src, n):
                nc.scalar.activation(sq[:], src, ACT.Square).then_inc(q["squared"], 1)
                act.wait_ge(q["summed"], 2 * i + n)
                nc.scalar.activation(r[:], pn, ACT.Ln, bias=eps6[:]).then_inc(q["logged"], 1)
                act.wait_ge(q["logged"], 2 * i + n)
                nc.scalar.activation(r[:], r[:], ACT.Exp, scale=-0.5).then_inc(q["rooted"], 1)
            with act.Fori(0, NG) as i:
                nc.scalar.preload_act_table_set("natural_log_exp_and_others")
                act.wait_ge(q["added"], i + 1)
                root(i, xT[:, bass.ds(i * GT, GT)], 1)
                for n in range(4):
                    act.wait_ge(q["inned"], 4 * i + n + 1)
                    nc.scalar.activation(xz[:, n, :], pg[n % 2], ACT.Silu).then_inc(q["silued"], 1)
                nc.scalar.preload_act_table_set("natural_log_exp_and_others")
                for n in range(6):
                    act.wait_ge(q["parmed"], 6 * i + n + 1)
                    nc.scalar.activation(prm[:, n // 2, n % 2, :], pg[n % 2], ACT.Copy).then_inc(q["pcopied"], 1)
                act.wait_ge(q["pcopied"], 6 * i + 2)
                nc.scalar.activation(sp_[:], prm[:, 0], ACT.Abs).then_inc(q["absed"], 1)
                act.wait_ge(q["absed"], i + 1)
                nc.scalar.activation(sp_[:], sp_[:], ACT.Exp, scale=-1.0).then_inc(q["soft1"], 1)
                act.wait_ge(q["soft1"], i + 1)
                nc.scalar.activation(sp_[:], sp_[:], ACT.Ln, bias=1.0).then_inc(q["soft2"], 1)
                act.wait_ge(q["clipped"], i + 1)
                nc.scalar.activation(ea[:], ea[:], ACT.Exp).then_inc(q["exped"], 1)
                act.wait_ge(q["x1ed"], i + 1)
                root(i, x1[:], 2)
                for c in range(FC):
                    act.wait_ge(q["ffed"], FC * i + c + 1)
                    nc.scalar.activation(hf[:, c, :], pg[c % 2], ACT.Silu, bias=bf1[:, c:c + 1]).then_inc(q["ffsilued"], 1)

        @block.gpsimd
        def _(pool):
            with pool.Fori(0, NG) as i:
                for n in range(NS):
                    pool.wait_ge(q["scanned"], i * NS + n + 1)
                    if n >= 2:
                        pool.wait_ge(q["dropped"], i * NS + n - 1)
                    nc.gpsimd.tensor_tensor(hc[n % 2][:], hs[n % 2][:], prm[:, 2, n % 2, :], ALU.mult).then_inc(q["used"], 1)

        @block.vector
        def _(dve):
            dve.sem_inc(q["added"], 1)
            CH = 9
            with dve.Fori(0, NG) as i:
                at = [0]

                def link(ins):
                    at[0] += 1
                    ins.then_inc(ch, 1)
                    dve.wait_ge(ch, i * CH + at[0])
                x = xT[:, bass.ds(i * GT, GT)]
                dve.wait_ge(q["rooted"], 2 * i + 1)
                nc.vector.tensor_tensor(z[:], x, r[:], ALU.mult).then_inc(q["normed"], 1)
                dve.wait_ge(q["soft2"], i + 1)
                dve.wait_ge(q["pcopied"], 6 * i + 6)
                link(nc.vector.scalar_tensor_tensor(out=dl[:], in0=prm[:, 0], scalar=0.0, in1=sp_[:], op0=ALU.max, op1=ALU.add))
                link(nc.vector.tensor_scalar(ea[:], dl[:], alog[:, 2:3], -10.0, ALU.mult, ALU.max))
                nc.vector.tensor_scalar(sp_[:], ea[:], -1e-4, None, ALU.is_gt).then_inc(q["clipped"], 1)
                dve.wait_ge(q["exped"], i + 1)
                link(nc.vector.tensor_scalar(fr[:], ea[:], -1.0, alog[:, 3:4], ALU.add, ALU.mult))
                link(nc.vector.tensor_tensor(dl[:], dl[:], fr[:], ALU.subtract))
                link(nc.vector.tensor_tensor(dl[:], dl[:], sp_[:], ALU.mult))
                link(nc.vector.tensor_tensor(fr[:], fr[:], dl[:], ALU.add))
                link(nc.vector.memset(ea[:].rearrange("p h (b t) -> p h b t", t=L)[:, :, :, 0], 0.0))
                link(nc.vector.tensor_tensor(fr[:], fr[:], prm[:, 1], ALU.mult))

                def bu_(n):
                    dve.wait_ge(q["picked"], i * NS + n + 1)
                    if n >= 2:
                        dve.wait_ge(q["scanned"], i * NS + n - 1)
                    nc.vector.tensor_tensor(bu[n % 2][:], fr[:, n % 2, :], pu[n % 2][:, 0:GT], ALU.mult).then_inc(q["bued"], 1)
                bu_(0)
                for n in range(NS):
                    if n + 1 < NS:
                        bu_(n + 1)
                    dve.wait_ge(q["bued"], i * NS + n + 1)
                    if n >= 2:
                        dve.wait_ge(q["used"], i * NS + n - 1)
                    nc.vector.tensor_tensor_scan(hs[n % 2][:], ea[:, n % 2, :], bu[n % 2][:], 0.0, ALU.mult, ALU.add).then_inc(q["scanned"], 1)
                dve.wait_ge(q["dropped"], (i + 1) * NS)
                for h in range(2):
                    ins = nc.vector.tensor_tensor(ym[:, h, :], py[h][:, 0:GT], xz[:, 2 + h, :], ALU.mult)
                ins.then_inc(q["gated"], 1)
                dve.wait_ge(q["outed"], i + 1)
                nc.vector.tensor_tensor(x1[:], pw[:, 0:GT], x, ALU.add).then_inc(q["x1ed"], 1)
                dve.wait_ge(q["rooted"], 2 * i + 2)
                nc.vector.tensor_tensor(z[:], x1[:], r[:], ALU.mult).then_inc(q["normed"], 1)
                dve.wait_ge(q["x1ed"], i + 1)
                link(nc.vector.tensor_tensor(x1[:], x1[:], x, ALU.add))
                dve.wait_ge(q["ffouted"], i + 1)
                nc.vector.scalar_tensor_tensor(out=x, in0=pw[:, 0:GT], scalar=cols[:, 2:3], in1=x1[:], op0=ALU.add,
                                               op1=ALU.add).then_inc(q["added"], 1)
                dve.wait_ge(q["added"], i + 2)
                assert at[0] == CH, at[0]


def l1_attn(nc, k, a):
    xT = k["xT"]
    NH = a["L1_attn_Wb"].shape[1]
    DK, DV = a["L1_attn_Wq"].shape[1] // NH, a["L1_attn_Wv"].shape[1] // NH
    assert DV == 128 and DK == 64
    C = 16
    KC = NH * DK // 128
    U = 4
    NU = NH // U
    UT, UV = U * L, U * DV
    R2 = 32
    with ExitStack() as ctx:
        s = Stage(nc, ctx, "l1a")
        wqk, wv, wg, wo = s.sb("wqk", [D, 2, NH * DK]), s.sb("wv", [D, NH, DV]), s.sb("wg", [D, NH, DV]), s.sb("wo", [DV, NH, D])
        taps = s.sb("taps", [128, 2 * KC + NH, 4])
        wgb, hb, gnw = s.sb("wgb", [D, 2, NH]), s.sb("hb", [NH, 4]), s.sb("gnw", [DV, 1])
        load(nc, "l1al", [(wqk[:, 0, :], a["L1_attn_Wq"]), (wqk[:, 1, :], a["L1_attn_Wk"]),
                          (wv[:].rearrange("d h v -> d (h v)"), a["L1_attn_Wv"]), (wg[:].rearrange("d h v -> d (h v)"), a["L1_attn_Wg"]),
                          (wo[:], a["L1_attn_Wo"].rearrange("(h v) d -> v h d", v=DV)),
                          (taps[:, 0:KC, :], a["L1_attn_conv_q"].rearrange("(c p) j -> p c j", p=128)),
                          (taps[:, KC:2 * KC, :], a["L1_attn_conv_k"].rearrange("(c p) j -> p c j", p=128)),
                          (taps[:, 2 * KC:, :], a["L1_attn_conv_v"].rearrange("(c p) j -> p c j", p=128)),
                          (wgb[:, 0, :], a["L1_attn_Wgk"]), (wgb[:, 1, :], a["L1_attn_Wb"]),
                          (hb[:, 0:1], col(a["L1_attn_dt_bias"])), (hb[:, 1:2], col(a["L1_attn_b_b"])),
                          (hb[:, 2:3], col(a["L1_attn_A_log"])), (gnw[:], col(a["L1_attn_g_norm_weight"]))])
        upto, within, below = s.sb("upto", [L, U, L]), s.sb("within", [L, U, L]), s.sb("below", [L, U, L])
        inblk, outblk, eyes = s.sb("inblk", [L, U, L]), s.sb("outblk", [L, U, L]), s.sb("eyes", [L, U, L])
        pair, keep, eps6, lnsc = s.sb("pair", [128, 128]), s.sb("keep", [NH, GB, L]), s.sb("eps6", [128, 1]), s.sb("lnsc", [128, 1])
        ind = s.sb("ind", [NH, NH, L])
        lhsA, lhsL = s.sb("lhsA", [R2 + NH, GT]), s.sb("lhsL", [R2 + NH, GT])
        rhsA, rhsT, rhsL = [s.sb(n, [R2 + NH, NH, L]) for n in ("rhsA", "rhsT", "rhsL")]
        m = s.sem("m")
        FAR = -1e30
        with nc.Block() as block:
            @block.gpsimd
            def _(pool):
                aff = nc.gpsimd.affine_select
                steps = [0]

                def link(ins):
                    steps[0] += 1
                    ins.then_inc(m, 1)
                    pool.wait_ge(m, steps[0])
                for t in (upto, within, below):
                    nc.gpsimd.memset(t[:], 0.0)
                for t in (inblk, pair, keep, ind, lhsA, lhsL, rhsA, rhsT, rhsL):
                    nc.gpsimd.memset(t[:], 1.0)
                nc.gpsimd.memset(eps6[:], 1e-6)
                nc.gpsimd.memset(lnsc[:, :], float(np.log(DK ** -0.5)))
                link(nc.gpsimd.memset(eyes[:], 0.0))
                link(aff(out=upto[:], in_=upto[:], compare_op=ALU.is_ge, fill=FAR, base=0, pattern=[[0, U], [1, L]], channel_multiplier=-1))
                link(aff(out=within[:], in_=within[:], compare_op=ALU.is_gt, fill=FAR, base=0, pattern=[[0, U], [1, L]], channel_multiplier=-1))
                link(aff(out=below[:], in_=below[:], compare_op=ALU.is_gt, fill=FAR, base=0, pattern=[[0, U], [-1, L]], channel_multiplier=1))
                link(aff(out=eyes[:], in_=eyes[:], compare_op=ALU.not_equal, fill=1.0, base=0, pattern=[[0, U], [-1, L]], channel_multiplier=1))
                for c0 in range(0, L, C):
                    w = min(C, L - c0)
                    for t, fill in ((within, FAR), (inblk, 0.0)):
                        v = t[:, :, c0:c0 + w]
                        link(aff(out=v, in_=v, compare_op=ALU.is_ge, fill=fill, base=-c0, pattern=[[0, U], [0, w]], channel_multiplier=1))
                        link(aff(out=v, in_=v, compare_op=ALU.is_ge, fill=fill, base=c0 + w - 1, pattern=[[0, U], [0, w]], channel_multiplier=-1))
                link(nc.gpsimd.tensor_scalar(outblk[:], inblk[:], -1.0, 1.0, ALU.mult, ALU.add))
                pv = pair[:].rearrange("p (g e) -> p g e", e=DK)
                link(aff(out=pv, in_=pv, compare_op=ALU.is_ge, fill=0.0, base=0, pattern=[[-DK, 2], [0, DK]], channel_multiplier=1))
                link(aff(out=pv, in_=pv, compare_op=ALU.is_ge, fill=0.0, base=DK - 1, pattern=[[DK, 2], [0, DK]], channel_multiplier=-1))
                link(nc.gpsimd.memset(keep[:, :, 0:1], 0.0))
                link(aff(out=ind[:], in_=ind[:], compare_op=ALU.is_equal, fill=0.0, base=0, pattern=[[-1, NH], [0, L]], channel_multiplier=1))
                for t in (lhsA, lhsL):
                    link(aff(out=t[0:R2], in_=t[0:R2], compare_op=ALU.is_ge, fill=0.0, base=NH - 1, pattern=[[0, GT]], channel_multiplier=-1))
                for t in (rhsA, rhsT, rhsL):
                    link(aff(out=t[0:R2], in_=t[0:R2], compare_op=ALU.is_equal, fill=0.0, base=0, pattern=[[-1, NH], [0, L]], channel_multiplier=1))

            sc = s.sem("sc")

            @block.scalar
            def _(act):
                nc.scalar.preload_act_table_set("natural_log_exp_and_others")
                nc.scalar.activation(hb[:, 3:4], hb[:, 2:3], ACT.Exp).then_inc(sc, 1)

            @block.vector
            def _(dve):
                dve.wait_ge(sc, 1)
                nc.vector.tensor_scalar(hb[:, 3:4], hb[:, 3:4], -1.0, None, ALU.mult)

        banks = [s.ps(f"bank{n}") for n in range(8)]
        NB = len(banks)
        qk, v = s.sb("qk", [128, 2 * KC, GT]), s.sb("v", [128, NH, GT])
        half = s.sb("half", [128, 2, KC, 2, GT])
        sg = qk
        sq, rt = [s.sb(f"sq{p}", [128, GT]) for p in range(2)], [s.sb(f"rt{p}", [128, GT]) for p in range(2)]
        raw, spl, spt = s.sb("raw", [NH, 2, GT]), s.sb("spl", [NH, 2, GT]), s.sb("spt", [NH, 2, GT])
        G, Gb, beta, betaT = s.sb("G", [NH, GT]), s.sb("Gb", [NH, GT]), s.sb("beta", [NH, GT]), s.sb("betaT", [L, GB, NH])
        buf = [{n: s.sb(f"{n}{u}", [L, UT]) for n in ("AT", "b1", "b2", "b3", "b4", "b5", "R")} for u in range(NU)]
        Z = [s.sb(f"Z{u}", [L, UV]) for u in range(NU)]
        NQ = 2 * KC + NH
        front = {n: s.sem(n) for n in ("projected", "tapped", "convolved", "silued", "squared", "summed", "logged", "rooted",
                                       "normed", "halved", "smalls", "biased", "absed", "soft1", "soft2", "soft", "gked", "summedG",
                                       "betaed", "turned", "ready", "rows", "argued", "gated",
                                       "osquared", "osummed", "ologged", "orooted", "oscaled", "ogated", "projO", "added")}
        PE_ = ["argA", "argT", "argL", "kk", "qk", "vT", "M2T", "M2", "R2", "M4T", "M4", "R3", "M8", "R4", "N", "NT", "Z", "Z1",
               "N2T", "N2", "Z2", "N4T", "Z3", "O"]
        DVE_ = ["minA", "minT", "minL", "MT", "M", "AT", "X", "R1", "R2", "R3", "R4", "Z1", "Z2", "Z3"]
        ACT_ = ["expA", "expT", "expL", "M2T", "M2", "M4T", "M4", "M8", "N", "NT", "Z", "N2T", "N2", "N4T", "O"]
        POOL_ = ["Md", "Mo"]
        reader = {"argA": "minA", "argT": "minT", "argL": "minL", "kk": "M", "qk": "AT", "vT": "X", "R2": "R2", "R3": "R3",
                  "R4": "R4", "Z1": "Z1", "Z2": "Z2", "Z3": "Z3"}
        pe_done, dve_done, act_done, pool_done = [[s.sem(f"{n}{u}") for u in range(NU)] for n in ("pe_done", "dve_done", "act_done", "pool_done")]
        held = s.sem("held")
        block = ctx.enter_context(nc.Block())

        def at(i, b, order, step):
            return (i * GB + b) * len(order) + order.index(step) + 1

        def shape(ap):
            return ap.rearrange("p (b t) -> p b t", t=L)

        @block.tensor
        def _(pe):
            with pe.Fori(0, NG) as i:
                x = xT[:, bass.ds(i * GT, GT)]
                pe.wait_ge(front["added"], i + 1)
                for n in range(NQ):
                    if n >= NB:
                        pe.wait_ge(front["convolved"], i * NQ + n - NB + 1)
                    w = wqk[:, n // KC, n % KC * 128:(n % KC + 1) * 128] if n < 2 * KC else wv[:, n - 2 * KC, :]
                    nc.tensor.matmul(banks[n % NB][:, 0:GT], w, x, start=True, stop=True).then_inc(front["projected"], 1)
                for n in range(2):
                    pe.wait_ge(front["convolved"], i * NQ + NQ - NB + n + 1)
                    pe.sem_inc(held, 1)
                    nc.tensor.matmul(banks[(NQ + n) % NB][0:NH, 0:GT], wgb[:, n, :], x, start=True, stop=True).then_inc(front["smalls"], 1)
                pe.wait_ge(front["convolved"], i * NQ + NQ)
                for n in range(2 * KC):
                    bk = (NQ + 2 + n) % NB
                    pe.wait_ge(front["squared"], i * 2 * KC + n + 1)
                    if n >= NB - 2:
                        pe.wait_ge(front["biased"], i + 1)
                    if n >= NB:
                        pe.wait_ge(front["logged"], i * 2 * KC + n - NB + 1)
                    nc.tensor.matmul(banks[bk][:, 0:GT], pair[:], sq[n % 2][:], start=True, stop=True).then_inc(front["summed"], 1)
                pe.wait_ge(front["betaed"], i + 1)
                pe.wait_ge(front["normed"], (i + 1) * 2 * KC)
                pe.sem_inc(held, 1)
                for b in range(GB):
                    ins = nc.tensor.transpose(banks[0][0:L, b * NH:(b + 1) * NH], beta[:, b * L:(b + 1) * L], k["ident"][0:NH, 0:NH])
                ins.then_inc(front["turned"], 1)
                pe.wait_ge(front["ready"], i + 1)
                pe.wait_ge(front["halved"], (i + 1) * 2 * KC + 1)
                for b in range(GB):
                    pe.wait_ge(front["rows"], i * GB + b + 1)
                    for j, step in enumerate(PE_):
                        for u in range(NU):
                            seq = (b * len(PE_) + j) * NU + u
                            bk = banks[seq % NB]
                            if seq >= NB:
                                b0, j0, u0 = (seq - NB) // NU // len(PE_), (seq - NB) // NU % len(PE_), (seq - NB) % NU
                                last = PE_[j0]
                                if last in reader:
                                    pe.wait_ge(dve_done[u0], at(i, b0, DVE_, reader[last]))
                                else:
                                    pe.wait_ge(act_done[u0], at(i, b0, ACT_, last))
                            B = buf[u]
                            dve = lambda what: pe.wait_ge(dve_done[u], at(i, b, DVE_, what))
                            act = lambda what: pe.wait_ge(act_done[u], at(i, b, ACT_, what))
                            pool = lambda what: pe.wait_ge(pool_done[u], at(i, b, POOL_, what))
                            tb = slice(b * L, (b + 1) * L)

                            def heads(lhs, rhs, w=L, width=L, rows=L):
                                for h in range(U):
                                    ins = nc.tensor.matmul(bk[0:rows, h * width:h * width + w], lhs(h), rhs(h), start=True, stop=True)
                                return ins
                            sl = lambda t: (lambda h: t[:, h * L:(h + 1) * L])
                            sv = lambda t: (lambda h: t[:, h * DV:(h + 1) * DV])
                            if step in ("argA", "argT", "argL"):
                                lhs, rhs = {"argA": (lhsA, rhsA), "argT": (lhsA, rhsT), "argL": (lhsL, rhsL)}[step]
                                ins = nc.tensor.matmul(bk[0:L, 0:UT], lhs[:, tb], rhs[:, u * U:(u + 1) * U, :].rearrange("r h t -> r (h t)"),
                                                       start=True, stop=True)
                            elif step in ("kk", "qk"):
                                ins = heads(lambda h: qk[:, KC + (u * U + h) // 2, tb],
                                            lambda h: half[:, int(step == "kk"), (u * U + h) // 2, (u * U + h) % 2, tb])
                            elif step == "vT":
                                for h in range(U):
                                    ins = nc.tensor.transpose(bk[0:L, h * DV:(h + 1) * DV], v[:, u * U + h, tb], k["ident"][:])
                            elif step == "M2T":
                                dve("MT"), pool("Md")
                                ins = heads(sl(B["b3"]), sl(B["b1"]))
                            elif step == "M2":
                                ins = heads(sl(B["b1"]), sl(B["b3"]))
                            elif step == "R2":
                                dve("R1"), act("M2")
                                ins = heads(sl(B["b5"]), sl(B["R"]))
                            elif step == "M4T":
                                act("M2T")
                                ins = heads(sl(B["b5"]), sl(B["b4"]))
                            elif step == "M4":
                                ins = heads(sl(B["b4"]), sl(B["b5"]))
                            elif step == "R3":
                                dve("R2"), act("M4")
                                ins = heads(sl(B["b3"]), sl(B["R"]))
                            elif step == "M8":
                                act("M4T")
                                ins = heads(sl(B["b1"]), sl(B["b3"]))
                            elif step == "R4":
                                dve("R3"), act("M8")
                                ins = heads(sl(B["b4"]), sl(B["R"]))
                            elif step == "N":
                                dve("R4"), pool("Mo")
                                ins = heads(sl(B["R"]), sl(B["b2"]))
                            elif step == "NT":
                                ins = heads(sl(B["b2"]), sl(B["R"]))
                            elif step == "Z":
                                dve("X")
                                ins = heads(sl(B["R"]), sv(Z[u]), DV, DV)
                            elif step == "Z1":
                                act("Z")
                                ins = heads(sl(B["b1"]), sv(Z[u]), DV, DV)
                            elif step == "N2T":
                                act("N")
                                ins = heads(sl(B["b5"]), sl(B["b1"]))
                            elif step == "N2":
                                ins = heads(sl(B["b1"]), sl(B["b5"]))
                            elif step == "Z2":
                                dve("Z1"), act("N2T")
                                ins = heads(sl(B["b3"]), sv(Z[u]), DV, DV)
                            elif step == "N4T":
                                act("N2")
                                ins = heads(sl(B["b4"]), sl(B["b3"]))
                            elif step == "Z3":
                                dve("Z2"), act("N4T")
                                ins = heads(sl(B["b2"]), sv(Z[u]), DV, DV)
                            elif step == "O":
                                dve("Z3")
                                ins = heads(sv(Z[u]), sl(B["AT"]), rows=DV)
                            ins.then_inc(pe_done[u], 1)
                for u in range(NU):
                    pe.wait_ge(act_done[u], at(i, GB - 1, ACT_, "O"))
                for h in range(NH):
                    if h >= 4:
                        pe.wait_ge(front["gated"], i * NH + h - 3)
                    nc.tensor.matmul(banks[2 + h % 4][:, 0:GT], wg[:, h, :], x, start=True, stop=True).then_inc(front["projected"], 1)
                for h in range(NH + 1):
                    if h < NH:
                        pe.wait_ge(front["osquared"], i * NH + h + 1)
                        nc.tensor.matmul(banks[h % 2][:, 0:GT], k["mean"][:], sq[h % 2][:], start=True, stop=True).then_inc(front["osummed"], 1)
                    if h >= 1:
                        pe.wait_ge(front["ogated"], i * NH + h)
                        nc.tensor.matmul(banks[7][:, 0:GT], wo[:, h - 1, :], sg[:, h - 1, :], start=(h == 1), stop=(h == NH)).then_inc(front["projO"], 1)

        def root(act, i, n):
            act.wait_ge(front["summed"], i * 2 * KC + n + 1)
            if n >= 2:
                act.wait_ge(front["normed"], i * 2 * KC + n - 1)
            r = rt[n % 2]
            nc.scalar.activation(r[:], banks[(NQ + 2 + n) % NB][:, 0:GT], ACT.Ln, bias=eps6[:]).then_inc(front["logged"], 1)
            act.wait_ge(front["logged"], i * 2 * KC + n + 1)
            nc.scalar.activation(r[:], r[:], ACT.Exp, scale=-0.5, bias=lnsc[:] if n < KC else 0.0).then_inc(front["rooted"], 1)

        @block.scalar
        def _(act):
            with act.Fori(0, NG) as i:
                for n in range(NQ + 2):
                    if n < NQ:
                        act.wait_ge(front["projected"], i * (NQ + NH) + n + 1)
                        src = banks[n % NB][:, 0:GT]
                    if n < NQ:
                        dst = qk[:, n, :] if n < 2 * KC else v[:, n - 2 * KC, :]
                        nc.scalar.activation(dst, src, ACT.Copy, scale=taps[:, n, 3:4]).then_inc(front["tapped"], 1)
                    if n >= 2:
                        c = n - 2
                        act.wait_ge(front["convolved"], i * NQ + c + 1)
                        dst = qk[:, c, :] if c < 2 * KC else v[:, c - 2 * KC, :]
                        nc.scalar.activation(dst, dst, ACT.Silu).then_inc(front["silued"], 1)
                nc.scalar.preload_act_table_set("natural_log_exp_and_others")
                for n in range(2 * KC):
                    if n == 0:
                        act.wait_ge(front["silued"], i * NQ + NQ)
                    if n >= 2:
                        act.wait_ge(front["summed"], i * 2 * KC + n - 1)
                    nc.scalar.activation(sq[n % 2][:], qk[:, n, :], ACT.Square).then_inc(front["squared"], 1)
                    if n >= 1:
                        root(act, i, n - 1)
                root(act, i, 2 * KC - 1)
                act.wait_ge(front["biased"], i + 1)
                nc.scalar.activation(spt[:], raw[:], ACT.Abs).then_inc(front["absed"], 1)
                act.wait_ge(front["absed"], i + 1)
                nc.scalar.activation(spt[:], spt[:], ACT.Exp, scale=-1.0).then_inc(front["soft1"], 1)
                act.wait_ge(front["soft1"], i + 1)
                nc.scalar.activation(spt[:], spt[:], ACT.Ln, bias=1.0).then_inc(front["soft2"], 1)
                act.wait_ge(front["soft"], i + 1)
                nc.scalar.activation(beta[:], spl[:, 1, :], ACT.Exp, scale=-1.0).then_inc(front["betaed"], 1)
                for b in range(GB):
                    for j, step in enumerate(ACT_):
                        for u in range(NU):
                            B = buf[u]
                            if step in ("expA", "expT", "expL"):
                                act.wait_ge(dve_done[u], at(i, b, DVE_, "min" + step[3]))
                                t = B[{"A": "AT", "T": "b1", "L": "b2"}[step[3]]]
                                nc.scalar.activation(t[:], t[:], ACT.Exp).then_inc(act_done[u], 1)
                                continue
                            act.wait_ge(pe_done[u], at(i, b, PE_, step))
                            seq = (b * len(PE_) + PE_.index(step)) * NU + u
                            bk = banks[seq % NB]
                            if step == "Z":
                                nc.scalar.activation(Z[u][:], bk[0:L, :], ACT.Copy).then_inc(act_done[u], 1)
                            elif step == "O":
                                nc.scalar.activation(v[:, u * U:(u + 1) * U, b * L:(b + 1) * L],
                                                     bk[:, 0:UT].rearrange("v (h t) -> v h t", t=L), ACT.Copy).then_inc(act_done[u], 1)
                            else:
                                t = B[{"M2T": "b4", "M2": "b5", "M4T": "b1", "M4": "b3", "M8": "b4", "N": "b5", "NT": "b1",
                                       "N2T": "b3", "N2": "b4", "N4T": "b2"}[step]]
                                nc.scalar.activation(t[:], bk[0:L, 0:UT], ACT.Copy).then_inc(act_done[u], 1)
                for u in range(NU):
                    act.wait_ge(act_done[u], at(i, GB - 1, ACT_, "O"))
                for h in range(NH):
                    act.wait_ge(front["projected"], i * (NQ + NH) + NQ + h + 1)
                    nc.scalar.activation(sg[:, h, :], banks[2 + h % 4][:, 0:GT], ACT.Silu).then_inc(front["gated"], 1)
                nc.scalar.preload_act_table_set("natural_log_exp_and_others")
                for h in range(NH + 1):
                    if h < NH:
                        if h >= 2:
                            act.wait_ge(front["osummed"], i * NH + h - 1)
                        nc.scalar.activation(sq[h % 2][:], v[:, h, :], ACT.Square).then_inc(front["osquared"], 1)
                    if h >= 1:
                        act.wait_ge(front["osummed"], i * NH + h)
                        if h >= 3:
                            act.wait_ge(front["oscaled"], i * NH + h - 2)
                        r = rt[(h - 1) % 2]
                        nc.scalar.activation(r[:], banks[(h - 1) % 2][:, 0:GT], ACT.Ln, bias=k["eps"][:]).then_inc(front["ologged"], 1)
                        act.wait_ge(front["ologged"], i * NH + h)
                        nc.scalar.activation(r[:], r[:], ACT.Exp, scale=-0.5).then_inc(front["orooted"], 1)

        @block.gpsimd
        def _(pool):
            nc.gpsimd.memset(half[:], 0.0).then_inc(front["halved"], 1)
            pool.wait_ge(front["halved"], 1)
            with pool.Fori(0, NG) as i:
                for n in range(2 * KC):
                    pool.wait_ge(front["normed"], i * 2 * KC + n + 1)
                    pool.sem_inc(held, 1)
                    for e in range(2):
                        r = slice(e * DK, (e + 1) * DK)
                        ins = nc.gpsimd.tensor_copy(half[r, n // KC, n % KC, e, :], qk[r, n, :])
                    ins.then_inc(front["halved"], 1)
                pool.wait_ge(front["halved"], (i + 1) * 2 * KC + 1)
                pool.wait_ge(front["ready"], i + 1)
                for b in range(GB):
                    tb = slice(b * L, (b + 1) * L)
                    if b:
                        for u in range(NU):
                            pool.wait_ge(pe_done[u], at(i, b - 1, PE_, "argL"))
                    bc = lambda t: t[:, tb].unsqueeze(1).to_broadcast([NH, NH, L])
                    nc.gpsimd.tensor_tensor(rhsA[R2:R2 + NH], ind[:], bc(G), ALU.mult)
                    nc.gpsimd.tensor_tensor(rhsT[R2:R2 + NH], ind[:], bc(Gb), ALU.mult)
                    nc.gpsimd.tensor_tensor(rhsL[R2:R2 + NH], ind[:], bc(lhsA[0:NH]), ALU.mult).then_inc(front["rows"], 1)
                    pool.wait_ge(front["rows"], i * GB + b + 1)
                    for u in range(NU):
                        B = buf[u]
                        pool.wait_ge(dve_done[u], at(i, b, DVE_, "M"))
                        nc.gpsimd.tensor_tensor(B["b3"][:], B["b2"][:], inblk[:].rearrange("p h t -> p (h t)"), ALU.mult).then_inc(pool_done[u], 1)
                        pool.wait_ge(pool_done[u], at(i, b, POOL_, "Md"))
                        nc.gpsimd.tensor_tensor(B["b2"][:], B["b2"][:], outblk[:].rearrange("p h t -> p (h t)"), ALU.mult).then_inc(pool_done[u], 1)
                    pool.wait_ge(pool_done[NU - 1], at(i, b, POOL_, "Mo"))

        @block.vector
        def _(dve):
            dve.sem_inc(front["added"], 1)
            ch = s.sem("ch")
            NC_ = NQ * 2
            with dve.Fori(0, NG) as i:
                for n in range(NQ):
                    dve.wait_ge(front["tapped"], i * NQ + n + 1)
                    dst = shape(qk[:, n, :] if n < 2 * KC else v[:, n - 2 * KC, :])
                    src = shape(banks[n % NB][:, 0:GT])
                    for j in range(1, 4):
                        ins = nc.vector.scalar_tensor_tensor(out=dst[:, :, j:L], in0=src[:, :, 0:L - j], scalar=taps[:, n, 3 - j:4 - j],
                                                             in1=dst[:, :, j:L], op0=ALU.mult, op1=ALU.add)
                        if j < 3:
                            ins.then_inc(ch, 1)
                            dve.wait_ge(ch, i * NC_ + n * 2 + j)
                    ins.then_inc(front["convolved"], 1)
                dve.wait_ge(front["smalls"], 2 * i + 2)
                nc.vector.tensor_scalar(raw[:, 0, :], banks[NQ % NB][0:NH, 0:GT], hb[:, 0:1], None, ALU.add)
                nc.vector.tensor_scalar(raw[:, 1, :], banks[(NQ + 1) % NB][0:NH, 0:GT], hb[:, 1:2], -1.0, ALU.add, ALU.mult).then_inc(front["biased"], 1)
                for n in range(2 * KC):
                    dve.wait_ge(front["rooted"], i * 2 * KC + n + 1)
                    nc.vector.tensor_tensor(qk[:, n, :], qk[:, n, :], rt[n % 2][:], ALU.mult).then_inc(front["normed"], 1)
                dve.wait_ge(front["soft2"], i + 1)
                nc.vector.scalar_tensor_tensor(out=spl[:], in0=raw[:], scalar=0.0, in1=spt[:], op0=ALU.max, op1=ALU.add).then_inc(front["soft"], 1)
                dve.wait_ge(front["soft"], i + 1)
                nc.vector.tensor_scalar(spl[:, 0, :], spl[:, 0, :], hb[:, 3:4], None, ALU.mult).then_inc(front["gked"], 1)
                dve.wait_ge(front["gked"], i + 1)
                nc.vector.tensor_tensor_scan(G[:], keep[:].rearrange("h b t -> h (b t)"), spl[:, 0, :], 0.0, ALU.mult, ALU.add).then_inc(front["summedG"], 1)
                dve.wait_ge(front["summedG"], i + 1)
                nc.vector.tensor_tensor(Gb[:], G[:], spl[:, 1, :], ALU.subtract)
                nc.vector.tensor_tensor(lhsL[0:NH, :], G[:], spl[:, 1, :], ALU.subtract)
                nc.vector.tensor_scalar(lhsA[0:NH, :], G[:], -1.0, None, ALU.mult)
                dve.wait_ge(front["turned"], i + 1)
                nc.vector.tensor_copy(betaT[:], banks[0][0:L, 0:GB * NH].rearrange("t (b h) -> t b h", h=NH)).then_inc(front["ready"], 1)
                dve.wait_ge(front["ready"], i + 1)
                for b in range(GB):
                    for j, step in enumerate(DVE_):
                        for u in range(NU):
                            B = buf[u]
                            src = {"minA": "argA", "minT": "argT", "minL": "argL", "MT": "kk", "M": "kk", "AT": "qk", "X": "vT"}.get(step, step)
                            if step != "R1":
                                dve.wait_ge(pe_done[u], at(i, b, PE_, src))
                                seq = (b * len(PE_) + PE_.index(src)) * NU + u
                                bk = banks[seq % NB]
                            wide, nar = (bk[0:L, 0:UT], bk[0:L, :])
                            if step.startswith("min"):
                                mask = {"A": upto, "T": within, "L": below}[step[3]]
                                t = B[{"A": "AT", "T": "b1", "L": "b2"}[step[3]]]
                                ins = nc.vector.tensor_tensor(t[:], wide, mask[:].rearrange("p h t -> p (h t)"), ALU.min)
                            elif step in ("MT", "M", "AT"):
                                dve.wait_ge(act_done[u], at(i, b, ACT_, {"MT": "expT", "M": "expL", "AT": "expA"}[step]))
                                t = B[{"MT": "b1", "M": "b2", "AT": "AT"}[step]]
                                ins = nc.vector.tensor_tensor(t[:], wide, t[:], ALU.mult)
                            elif step == "X":
                                bt = betaT[:, b, u * U:(u + 1) * U].unsqueeze(2).to_broadcast([L, U, DV])
                                ins = nc.vector.tensor_tensor(Z[u][:].rearrange("t (h v) -> t h v", v=DV),
                                                              nar.rearrange("t (h v) -> t h v", v=DV), bt, ALU.mult)
                            elif step == "R1":
                                dve.wait_ge(dve_done[u], at(i, b, DVE_, "MT"))
                                ins = nc.vector.tensor_tensor(B["R"][:], eyes[:].rearrange("p h t -> p (h t)"), B["b1"][:], ALU.subtract)
                            elif step[0] == "R":
                                ins = nc.vector.tensor_tensor(B["R"][:], B["R"][:], wide, ALU.add)
                            elif step == "Z1":
                                ins = nc.vector.tensor_tensor(Z[u][:], Z[u][:], nar, ALU.subtract)
                            else:
                                ins = nc.vector.tensor_tensor(Z[u][:], Z[u][:], nar, ALU.add)
                            ins.then_inc(dve_done[u], 1)
                for h in range(NH):
                    dve.wait_ge(front["orooted"], i * NH + h + 1)
                    nc.vector.tensor_tensor(v[:, h, :], v[:, h, :], rt[h % 2][:], ALU.mult).then_inc(front["oscaled"], 1)
                    dve.wait_ge(front["oscaled"], i * NH + h + 1)
                    nc.vector.scalar_tensor_tensor(out=sg[:, h, :], in0=v[:, h, :], scalar=gnw[:], in1=sg[:, h, :], op0=ALU.mult,
                                                   op1=ALU.mult).then_inc(front["ogated"], 1)
                dve.wait_ge(front["projO"], (i + 1) * NH)
                x = xT[:, bass.ds(i * GT, GT)]
                nc.vector.tensor_tensor(x, x, banks[7][:, 0:GT], ALU.add).then_inc(front["added"], 1)


def cross(nc, k, a, tag, H, own):
    xT, ctxd = k["xT"], a["ctx_2048"]
    S, DH = ctxd.shape[1], D // H
    FT, TAIL = S // 128, S % 128
    tiles = [128] * FT + [TAIL] + ([L] if own else [])
    first = [sum(tiles[:n]) for n in range(len(tiles))]
    NT, KEYS = len(tiles), sum(tiles)
    CK = 4
    KW = KEYS // CK
    assert KW * CK == KEYS and KW <= 512
    HQ = H * L
    NW = -(-HQ // 128)
    HW = GT
    half = 2 * HW
    steps = [(j, c) for j in range(NT) for c in range(HQ // half)]
    V1 = DH + 1
    scale = float(DH ** -0.5)
    with ExitStack() as ctx:
        s = Stage(nc, ctx, tag)
        headof, one16 = s.sb("headof", [128, H]), s.sb("one16", [1, 128], BF16)
        made = s.sem("made")
        with nc.Block() as block:
            @block.gpsimd
            def _(pool):
                nc.gpsimd.memset(one16[:], 1.0)
                nc.gpsimd.memset(headof[:], scale).then_inc(made, 1)
                pool.wait_ge(made, 1)
                nc.gpsimd.affine_select(out=headof[:], in_=headof[:], compare_op=ALU.is_ge, fill=0.0, base=0,
                                        pattern=[[-DH, H]], channel_multiplier=1).then_inc(made, 1)
                pool.wait_ge(made, 2)
                nc.gpsimd.affine_select(out=headof[:], in_=headof[:], compare_op=ALU.is_ge, fill=0.0, base=DH - 1,
                                        pattern=[[DH, H]], channel_multiplier=-1).then_inc(made, 1)
        if own:
            wT, bp = s.sb("wT", [D, 4, D]), s.sb("bp", [D, 1])
            qT, kS, vS, oT = s.sb("qT", [D, N]), s.sb("kS", [D, N]), s.sb("vS", [L, B, D]), s.sb("oT", [D, N])
            pre = a[f"{tag}_w_qkv"]
            load(nc, tag + "l", [(bp[:], col(a[f"{tag}_b_proj"]))])
            load_transposed(nc, k, tag + "t", [(wT[:, n, :], pre[n * D:(n + 1) * D, :]) for n in range(3)]
                            + [(wT[:, 3, :], a[f"{tag}_w_proj"])])
            with ExitStack() as mine:
                t = Stage(nc, mine, tag + "p")
                xs = [t.sb(f"xs{p}", [D, GT]) for p in range(2)]
                pp = [[t.ps(f"pp{n}{p}") for n in range(3)] for p in range(2)]
                held = t.sem("held")
                staged, projected, kept, keptv = t.sem("staged"), t.sem("projected"), t.sem("kept"), t.sem("keptv")
                with nc.Block() as block:
                    @block.gpsimd
                    def _(pool):
                        with pool.Fori(0, NG // 2) as i:
                            for p in range(2):
                                g = 2 * i + p
                                pool.wait_ge(kept, g + 1)
                                pool.wait_ge(keptv, g + 1)
                                pool.sem_inc(held, 1)
                                nc.gpsimd.tensor_copy(xs[p][:], xT[:, bass.ds(g * GT, GT)]).then_inc(staged, 1)

                    @block.tensor
                    def _(pe):
                        with pe.Fori(0, NG // 2) as i:
                            for p in range(2):
                                g = 2 * i + p
                                pe.wait_ge(staged, g + 1)
                                for n in range(2):
                                    nc.tensor.matmul(pp[p][n][:, 0:GT], wT[:, n, :], xs[p][:], start=True, stop=True)
                                for b in range(GB):
                                    ins = nc.tensor.matmul(pp[p][2][0:L, b * D:(b + 1) * D], xs[p][:, b * L:(b + 1) * L], wT[:, 2, :],
                                                           start=True, stop=True)
                                ins.then_inc(projected, 1)

                    @block.scalar
                    def _(act):
                        act.sem_inc(kept, 2)
                        with act.Fori(0, NG // 2) as i:
                            for p in range(2):
                                g = 2 * i + p
                                act.wait_ge(projected, g + 1)
                                nc.scalar.activation(qT[:, bass.ds(g * GT, GT)], pp[p][0][:, 0:GT], ACT.Copy)
                                nc.scalar.activation(kS[:, bass.ds(g * GT, GT)], pp[p][1][:, 0:GT], ACT.Copy).then_inc(kept, 1)

                    @block.vector
                    def _(dve):
                        dve.sem_inc(keptv, 2)
                        with dve.Fori(0, NG // 2) as i:
                            for p in range(2):
                                g = 2 * i + p
                                dve.wait_ge(projected, g + 1)
                                nc.vector.tensor_copy(vS[:, bass.ds(g * GB, GB), :].rearrange("t b d -> t (b d)"),
                                                      pp[p][2][0:L, :]).then_inc(keptv, 1)
            q = qT
        else:
            q = xT
            mk, mf, live, bb = s.sb("mk", [B, S], I32), s.sb("mf", [B, S]), s.sb("live", [B, 1]), s.sb("bb", [128, 1])
            m16, liveall = s.sb("m16", [B, S], BF16), s.sb("liveall", [128, B])
            bias_d, bias16_d = nc.dram_tensor(tag + "_bias_d", [B, S], F32).ap(), nc.dram_tensor(tag + "_bias16_d", [B, S], BF16).ap()
            live_d = nc.dram_tensor(tag + "_live_d", [B, 1], F32).ap()
            load(nc, tag + "l", [(mk[:], a["mask_BxS2_ik0"]), (bb[:], a["L3_xattn_b"].unsqueeze(0).to_broadcast([128, 1]))])
            c, w = s.sem("c"), s.sem("w")
            with nc.Block() as block:
                @block.vector
                def _(dve):
                    nc.vector.tensor_copy(mf[:], mk[:]).then_inc(c, 1)
                    dve.wait_ge(c, 1)
                    nc.vector.reduce_max(live[:], mf[:], AX).then_inc(c, 1)
                    nc.vector.tensor_scalar(mf[:], mf[:], -1.0, 1e30, ALU.add, ALU.mult).then_inc(c, 1)
                    dve.wait_ge(c, 3)
                    nc.vector.tensor_scalar(mf[:], mf[:], live[:], bb[0:B], ALU.mult, ALU.add).then_inc(c, 1)
                    dve.wait_ge(c, 4)
                    nc.vector.tensor_copy(m16[:], mf[:]).then_inc(c, 1)

                @block.sync
                def _(sp):
                    sp.wait_ge(c, 5)
                    sp.dma_start(bias_d, mf[:]).then_inc(w, 16)
                    sp.dma_start(bias16_d, m16[:]).then_inc(w, 16)
                    sp.dma_start(live_d, live[:]).then_inc(w, 16)
                    sp.wait_ge(w, 48)
                    sp.dma_start(liveall[:], live_d.rearrange("b o -> o b").to_broadcast([128, B])).then_inc(w, 16)
                    sp.wait_ge(w, 64)

        kv = [s.sb(f"kv{p}", [128, FT + 1, 2 * D]) for p in range(2)]
        kT, kT16 = [s.sb(f"kT{p}", [D, KEYS]) for p in range(2)], [s.sb(f"kT16{p}", [D, KEYS], BF16) for p in range(2)]
        v1 = [s.sb(f"v1{p}", [128, NT, H, V1]) for p in range(2)]
        qb, qb16 = [s.sb(f"qb{p}", [D, H, L]) for p in range(2)], [s.sb(f"qb16{p}", [D, H, L], BF16) for p in range(2)]
        mx, top, top16 = s.sb("mx", [128, NW, CK]), s.sb("top", [128, NW]), s.sb("top16", [NW, 128], BF16)
        row = [s.sb(f"row{p}", [1, NW * 128], BF16) for p in range(2)]
        E = [s.sb(f"E{p}", [128, half]) for p in range(2)]
        rec, on = s.sb("rec", [L, H]), s.sb("on", [L, H, DH])
        bk, br = [s.sb(f"bk{p}", [128, FT + 1]) for p in range(2)], [s.sb(f"br{p}", [1, KEYS], BF16) for p in range(2)]
        sc, pm = [s.ps(f"sc{p}", (128, 1024)) for p in range(2)], [s.ps(f"pm{p}") for p in range(2)]
        po, px = s.ps("po"), s.ps("px")
        loaded, biased = [s.sem(f"loaded{p}") for p in range(2)], [s.sem(f"biased{p}") for p in range(2)]
        z = {n: s.sem(n) for n in ("turned", "keyed", "keyed16", "queried", "queried16", "valued", "scored", "maxed", "topped",
                                   "toprow", "toprow16", "ready", "exped", "pved", "recd", "normed", "oturned", "done", "held")}
        rowed = [s.sem(f"rowed{p}") for p in range(2)]
        NS, NM = len(steps), NW * CK
        TG = [range(t, min(t + 4, FT + 1)) for t in range(0, FT + 1, 4)]
        NK = len(TG) + int(own)
        flat = lambda t: t.rearrange("p h t -> p (h t)")
        number = lambda bt: 2 * bt[0] + bt[1]
        after = lambda bt: (bt[0], 1) if bt[1] == 0 else (bt[0] + 1, 0)
        block_stack = ExitStack()
        block = block_stack.enter_context(nc.Block())

        def batches(eng, prepare, attend):
            prepare((0, 0))
            with eng.Fori(0, B // 2 - 1) as i:
                for p in range(2):
                    attend((i, p), True)
            attend((B // 2 - 1, 0), True)
            attend((B // 2 - 1, 1), False)

        @block.sync
        def _(sp):
            def fetch(bt):
                b, p = number(bt), bt[1]
                sp.dma_start(kv[p][:, 0:FT, :], ctxd[bass.ds(b, 1), 0:FT * 128, :].rearrange("o (j p) c -> p (o j) c", p=128)).then_inc(loaded[p], 16)
                sp.dma_start(kv[p][0:TAIL, FT, :], ctxd[bass.ds(b, 1), FT * 128:S, :].rearrange("o s c -> (o s) c")).then_inc(loaded[p], 16)

            def fetch_bias(bt):
                b, p = number(bt), bt[1]
                sp.dma_start(bk[p][:, 0:FT], bias_d[bass.ds(b, 1), 0:FT * 128].rearrange("o (j p) -> p (o j)", p=128),
                             allow_slow_non_contiguous=True).then_inc(biased[p], 16)
                sp.dma_start(bk[p][0:TAIL, FT:FT + 1], bias_d[bass.ds(b, 1), FT * 128:S].rearrange("o s -> s o"),
                             allow_slow_non_contiguous=True).then_inc(biased[p], 16)
                sp.dma_start(br[p][:], bias16_d[bass.ds(b, 1), :]).then_inc(biased[p], 16)

            def prepared(bt, more):
                b = number(bt)
                sp.wait_ge(z["toprow16"], b + 1)
                sp.sem_inc(z["held"], 1)
                sp.dma_start(row[bt[1]][:], top16[:]).then_inc(rowed[bt[1]], 16)
                if more:
                    sp.wait_ge(z["turned"], (b + 1) * len(TG))
                    sp.sem_inc(z["held"], 1)
                    sp.wait_ge(z["valued"], b + 1)
                    sp.sem_inc(z["held"], 1)
                    fetch((bt[0] + 1, bt[1]))

            def attended(bt):
                if not own:
                    b = number(bt)
                    sp.wait_ge(z["exped"], (b + 1) * NS)
                    sp.sem_inc(z["held"], 1)
                    fetch_bias((bt[0] + 1, bt[1]))
            for p in range(2):
                fetch((0, p))
                if not own:
                    fetch_bias((0, p))
            last = B // 2 - 1
            prepared((0, 0), True)
            with sp.Fori(0, last - 1) as i:
                prepared((i, 1), True)
                attended((i, 0))
                prepared((i + 1, 0), True)
                attended((i, 1))
            prepared((last - 1, 1), True)
            attended((last - 1, 0))
            prepared((last, 0), False)
            attended((last - 1, 1))
            prepared((last, 1), False)

        def landed(eng, bt):
            eng.wait_ge(loaded[bt[1]], 32 * bt[0] + 32)

        @block.gpsimd
        def _(pool):
            for p in range(2):
                nc.gpsimd.memset(v1[p][:], 1.0)
            nc.gpsimd.memset(top[:], 0.0).then_inc(made, 1)
            pool.wait_ge(made, 4)

            def prepare(bt):
                b, p = number(bt), bt[1]
                pool.wait_ge(z["done"], b + 1)
                nc.gpsimd.tensor_tensor(qb[p][:], q[:, bass.ds(b * L, L)].unsqueeze(1).to_broadcast([D, H, L]),
                                        headof[:].unsqueeze(2).to_broadcast([D, H, L]), ALU.mult).then_inc(z["queried"], 1)
                if not own:
                    pool.wait_ge(z["queried"], 2 * b + 1)
                    nc.gpsimd.tensor_tensor(qb[p][:], qb[p][:], liveall[:, bass.ds(b, 1)].unsqueeze(2).to_broadcast([D, H, L]),
                                            ALU.mult).then_inc(z["queried"], 1)
                pool.wait_ge(z["queried"], (b + 1) * (1 if own else 2))
                pool.sem_inc(z["held"], 1)
                nc.gpsimd.tensor_copy(qb16[p][:], qb[p][:]).then_inc(z["queried16"], 1)
                for n, ts in enumerate(TG):
                    piece = slice(first[ts[0]], first[ts[0]] + sum(tiles[j] for j in ts))
                    pool.wait_ge(z["keyed"], b * NK + n + 1)
                    pool.sem_inc(z["held"], 1)
                    nc.gpsimd.tensor_copy(kT16[p][:, piece], kT[p][:, piece]).then_inc(z["keyed16"], 1)
                if own:
                    nc.gpsimd.tensor_copy(kT16[p][:, S:KEYS], kS[:, bass.ds(b * L, L)]).then_inc(z["keyed16"], 1)
                landed(pool, bt)
                pool.sem_inc(z["held"], 1)
                nc.gpsimd.tensor_copy(v1[p][:, 0:FT, :, 0:DH], kv[p][:, 0:FT, D:2 * D].rearrange("s j (h d) -> s j h d", d=DH))
                ins = nc.gpsimd.tensor_copy(v1[p][0:TAIL, FT, :, 0:DH], kv[p][0:TAIL, FT, D:2 * D].rearrange("s (h d) -> s h d", d=DH))
                if own:
                    ins = nc.gpsimd.tensor_copy(v1[p][0:L, FT + 1, :, 0:DH],
                                                vS[:, bass.ds(b, 1), :].rearrange("t o (h d) -> t (o h) d", d=DH))
                ins.then_inc(z["valued"], 1)
            prepare((0, 0))
            prepare((0, 1))
            with pool.Fori(1, B // 2) as i:
                for p in range(2):
                    prepare((i, p))

        @block.tensor
        def _(pe):
            pe.wait_ge(made, 4)

            def preparation(bt):
                b, p = number(bt), bt[1]

                def turn(n):
                    if n == 0:
                        landed(pe, bt)
                        if not isinstance(b, int):
                            pe.wait_ge(z["maxed"], b * NM)
                    if n >= 2:
                        pe.wait_ge(z["keyed"], b * NK + n - 1)
                    for j in TG[n]:
                        r = tiles[j]
                        ins = nc.tensor.transpose(pm[n % 2][:, (j - TG[n][0]) * 128:(j - TG[n][0]) * 128 + r], kv[p][0:r, j, 0:D],
                                                  k["ident"][0:r, 0:r])
                    ins.then_inc(z["turned"], 1)

                def score(n):
                    w, c = n // CK, n % CK
                    if n == 0:
                        pe.wait_ge(z["keyed"], (b + 1) * NK)
                        pe.wait_ge(z["keyed16"], (b + 1) * NK)
                        pe.wait_ge(z["queried16"], b + 1)
                        if not own:
                            pe.wait_ge(biased[p], 48 * bt[0] + 48)
                    if n >= 2:
                        pe.wait_ge(z["maxed"], b * NM + n - 1)
                    r = min(128, HQ - w * 128)
                    dst, cols = pm[n % 2][0:r, 0:KW], slice(c * KW, (c + 1) * KW)
                    ins = nc.tensor.matmul(dst, flat(qb16[p][:])[:, w * 128:w * 128 + r], kT16[p][:, cols], start=True, stop=own)
                    if not own:
                        ins = nc.tensor.matmul(dst, one16[0:1, 0:r], br[p][:, cols], start=False, stop=True)
                    ins.then_inc(z["scored"], 1)

                def toprow():
                    pe.wait_ge(z["done"], b + 1)
                    pe.wait_ge(z["topped"], 2 * b + 2)
                    nc.tensor.transpose(px[0:NW, 0:128], top[:], k["ident"][:]).then_inc(z["toprow"], 1)
                return ([(turn, n) for n in range(len(TG))], [(score, n) for n in range(NM)], toprow)

            def prepare(bt):
                turns, scores, toprow = preparation(bt)
                for f, n in turns + scores:
                    f(n)
                toprow()

            def attend(bt, more):
                b, p = number(bt), bt[1]
                turns, scores, toprow = preparation(after(bt)) if more else ([], [], None)
                pe.wait_ge(rowed[p], 16 * bt[0] + 16)
                pe.wait_ge(z["valued"], b + 1)
                pe.wait_ge(z["normed"], b + 1)

                def weigh(n):
                    j, c = steps[n]
                    pe.wait_ge(z["exped"], b * NS + n + 1)
                    for h in range(half // L):
                        hd = c * (half // L) + h
                        ins = nc.tensor.matmul(po[0:L, hd * V1:(hd + 1) * V1], E[n % 2][0:tiles[j], h * L:(h + 1) * L],
                                               v1[p][0:tiles[j], j, hd, :], start=(n == 0 and h == 0), stop=(n == NS - 1),
                                               skip_group_check=True)
                    ins.then_inc(z["pved"], 1)
                def between(n):
                    if scores and n >= 5:
                        f, m = scores.pop(0)
                        f(m)
                for n, (j, c) in enumerate(steps):
                    if n >= 2:
                        pe.wait_ge(z["exped"], b * NS + n - 1)
                    r = tiles[j]
                    for e in range(2):
                        qc = slice((2 * c + e) * HW, (2 * c + e + 1) * HW)
                        dst = sc[n % 2][0:r, e * 512:e * 512 + HW]
                        nc.tensor.matmul(dst, kT[p][:, first[j]:first[j] + r], flat(qb[p][:])[:, qc], start=True, stop=False)
                        ins = nc.tensor.matmul(dst, one16[0:1, 0:r], row[p][:, qc], start=False, stop=True)
                        if e == 0:
                            between(n)
                    ins.then_inc(z["ready"], 1)
                    if turns and n >= 1:
                        f, m = turns.pop(0)
                        f(m)
                    else:
                        between(n)
                    if n >= 1:
                        weigh(n - 1)
                        between(n)
                    if more and n == NS - 3:
                        for f, m in scores:
                            f(m)
                        scores = []
                        toprow()
                weigh(NS - 1)
                pe.wait_ge(z["normed"], b + 2)
                if more:
                    pe.wait_ge(z["toprow16"], b + 2)
                nc.tensor.transpose(px[:, 0:L], on[:].rearrange("t h d -> t (h d)"), k["ident"][0:L, 0:L]).then_inc(z["oturned"], 1)
            batches(pe, prepare, attend)

        @block.scalar
        def _(act):
            nc.scalar.preload_act_table_set("natural_log_exp_and_others")
            if own:
                act.sem_inc(z["done"], 2)
            with act.Fori(0, B // 2) as i:
                for p in range(2):
                    b = 2 * i + p
                    if not own:
                        act.wait_ge(biased[p], 48 * i + 48)
                    for n, (j, c) in enumerate(steps):
                        act.wait_ge(z["ready"], b * NS + n + 1)
                        if n >= 2:
                            act.wait_ge(z["pved"], b * NS + n - 1)
                        r = tiles[j]
                        src = sc[n % 2][0:r, :].rearrange("s (e w) -> s e w", e=2)[:, :, 0:HW]
                        nc.scalar.activation(E[n % 2][0:r, :].rearrange("s (e w) -> s e w", e=2), src, ACT.Exp,
                                             bias=0.0 if own else bk[p][0:r, j:j + 1]).then_inc(z["exped"], 1)
                    if own:
                        act.wait_ge(z["oturned"], b + 1)
                        nc.scalar.activation(oT[:, bass.ds(b * L, L)], px[:, 0:L], ACT.Copy).then_inc(z["done"], 1)

        @block.vector
        def _(dve):
            if not own:
                dve.sem_inc(z["done"], 2)
            dve.sem_inc(z["normed"], 1)

            def prepare(bt):
                b, p = number(bt), bt[1]
                dve.wait_ge(z["done"], b + 1)
                for n, ts in enumerate(TG):
                    w = sum(tiles[j] for j in ts)
                    dve.wait_ge(z["turned"], b * len(TG) + n + 1)
                    nc.vector.tensor_copy(kT[p][:, first[ts[0]]:first[ts[0]] + w], pm[n % 2][:, 0:w]).then_inc(z["keyed"], 1)
                if own:
                    nc.vector.tensor_copy(kT[p][:, S:KEYS], kS[:, bass.ds(b * L, L)]).then_inc(z["keyed"], 1)
                for n in range(NM):
                    w, c = n // CK, n % CK
                    r = min(128, HQ - w * 128)
                    dve.wait_ge(z["scored"], b * NM + n + 1)
                    nc.vector.reduce_max(mx[0:r, w, c:c + 1], pm[n % 2][0:r, 0:KW], AX).then_inc(z["maxed"], 1)
                dve.wait_ge(z["maxed"], (b + 1) * NM)
                full = HQ // 128
                ins = nc.vector.tensor_reduce(top[:, 0:full], mx[:, 0:full, :], AX, ALU.max)
                if HQ % 128:
                    ins = nc.vector.tensor_reduce(top[0:HQ % 128, full:NW], mx[0:HQ % 128, full:NW, :], AX, ALU.max)
                ins.then_inc(z["topped"], 1)
                dve.wait_ge(z["topped"], 2 * b + 1)
                nc.vector.tensor_scalar(top[:], top[:], -1.0, None, ALU.mult).then_inc(z["topped"], 1)
                dve.wait_ge(z["toprow"], b + 1)
                nc.vector.tensor_copy(top16[:], px[0:NW, 0:128]).then_inc(z["toprow16"], 1)

            def attend(bt, more):
                b, p = number(bt), bt[1]
                if more:
                    prepare(after(bt))
                dve.wait_ge(z["pved"], (b + 1) * NS)
                o = po[0:L, 0:H * V1].rearrange("t (h v) -> t h v", v=V1)
                nc.vector.reciprocal(rec[:], o[:, :, DH]).then_inc(z["recd"], 1)
                dve.wait_ge(z["recd"], b + 1)
                nc.vector.tensor_tensor(on[:], o[:, :, 0:DH], rec[:].unsqueeze(2).to_broadcast([L, H, DH]), ALU.mult).then_inc(z["normed"], 1)
                if not own:
                    dve.wait_ge(z["oturned"], b + 1)
                    x = xT[:, bass.ds(b * L, L)]
                    nc.vector.tensor_tensor(x, x, px[:, 0:L], ALU.add).then_inc(z["done"], 1)
            batches(dve, prepare, attend)

        block_stack.close()
        if own:
            project(nc, tag + "o", xT, oT, wT[:, 3, :], bp, [sc[0], sc[1]])


def project(nc, tag, xT, src, wT, bias, banks):
    with ExitStack() as ctx:
        s = Stage(nc, ctx, tag)
        projected, added = s.sem("projected"), s.sem("added")
        with nc.Block() as block:
            @block.tensor
            def _(pe):
                with pe.Fori(0, NG // 2) as i:
                    for p in range(2):
                        g = 2 * i + p
                        pe.wait_ge(added, g + 1)
                        nc.tensor.matmul(banks[p][:, 0:GT], wT, src[:, bass.ds(g * GT, GT)], start=True, stop=True).then_inc(projected, 1)

            @block.vector
            def _(dve):
                dve.sem_inc(added, 2)
                with dve.Fori(0, NG // 2) as i:
                    for p in range(2):
                        g = 2 * i + p
                        dve.wait_ge(projected, g + 1)
                        x = xT[:, bass.ds(g * GT, GT)]
                        nc.vector.scalar_tensor_tensor(out=x, in0=banks[p][:, 0:GT], scalar=bias[:], in1=x, op0=ALU.add,
                                                       op1=ALU.add).then_inc(added, 1)


def l1_xattn(nc, k, a):
    cross(nc, k, a, "L1_xattn", 16, True)


def l2_xattn(nc, k, a):
    cross(nc, k, a, "L2_xattn", 16, True)


def l3_xattn(nc, k, a):
    cross(nc, k, a, "L3_xattn", 8, False)


def l3_ffn(nc, k, a, out):
    xT, phid, Wd = k["xT"], a["L3_ffn_phi"], a["L3_ffn_W"]
    NE, PS = phid.shape[1], phid.shape[2]
    SLOTS = NE * PS
    QS = 512
    NQ, SUB, EQ = SLOTS // QS, QS // 128, QS // PS
    EW = 128 // PS
    GB_ = 4
    D1 = D + 1
    pre = 2
    with ExitStack() as ctx:
        s = Stage(nc, ctx, "l3f")
        phi, phiS = s.sb("phi", [D, SLOTS]), s.sb("phiS", [D, QS])
        bias, one16, nrow = s.sb("bias", [128, NQ * SUB, D]), s.sb("one16", [1, 128], BF16), s.sb("nrow", [1, N], BF16)
        xtm = s.sb("xtm", [L, B, D])
        xs = [s.sb(f"xs{p}", [D, L]) for p in range(2)]
        bd = a["L3_ffn_b"].rearrange("(w e) d -> e w d", e=EW)
        load(nc, "l3fl", [(phi[:], phid.rearrange("d n p -> d (n p)"))]
             + [(bias[e * PS:(e + 1) * PS], bd[e:e + 1].to_broadcast([PS, NQ * SUB, D])) for e in range(EW)])

        with ExitStack() as first:
            t = Stage(nc, first, "l3m")
            phi16, xs16 = t.sb("phi16", [D, SLOTS], BF16), [t.sb(f"xs16{p}", [D, L], BF16) for p in range(2)]
            mx, neg, negr = t.sb("mx", [L, 2, B]), t.sb("neg", [L, B]), t.sb("negr", [B, L], BF16)
            pl, pt = [t.ps(f"pl{h}", (128, 1024)) for h in range(2)], [t.ps(f"pt{p}") for p in range(2)]
            phid16, staged, staged16, turned, kept, scored, maxed, c, rowed, held = [t.sem(n) for n in
                ("phied", "staged", "staged16", "turned", "kept", "scored", "maxed", "c", "rowed", "held")]
            with nc.Block() as block:
                @block.gpsimd
                def _(pool):
                    nc.gpsimd.memset(one16[:], 1.0)
                    with pool.Fori(0, B // 2) as i:
                        for p in range(2):
                            b = 2 * i + p
                            pool.wait_ge(scored, 2 * (b + 1))
                            pool.sem_inc(held, 1)
                            nc.gpsimd.tensor_copy(xs[p][:], xT[:, bass.ds(b * L, L)]).then_inc(staged, 1)
                            nc.gpsimd.tensor_copy(xs16[p][:], xT[:, bass.ds(b * L, L)]).then_inc(staged16, 1)

                @block.tensor
                def _(pe):
                    pe.sem_inc(scored, 4)
                    pe.wait_ge(phid16, 1)
                    with pe.Fori(0, B // 2) as i:
                        for p in range(2):
                            b = 2 * i + p
                            pe.wait_ge(kept, b + 1)
                            pe.wait_ge(staged16, b + 1)
                            nc.tensor.transpose(pt[p][0:L, 0:D], xs[p][:], k["ident"][:]).then_inc(turned, 1)
                            for h in range(2):
                                pe.wait_ge(maxed, 2 * b + h + 1)
                                for w in range(2):
                                    ins = nc.tensor.matmul(pl[h][0:L, w * 512:(w + 1) * 512], xs16[p][:],
                                                           phi16[:, (2 * h + w) * 512:(2 * h + w + 1) * 512], start=True, stop=True)
                                ins.then_inc(scored, 1)
                    pe.wait_ge(kept, B + 2)
                    pe.wait_ge(c, 2)
                    nc.tensor.transpose(pt[0][0:B, 0:L], neg[:], k["ident"][0:L, 0:L]).then_inc(c, 1)

                @block.scalar
                def _(act):
                    nc.scalar.activation(phi16[:], phi[:], ACT.Copy).then_inc(phid16, 1)
                    act.sem_inc(kept, 2)
                    with act.Fori(0, B // 2) as i:
                        for p in range(2):
                            b = 2 * i + p
                            act.wait_ge(turned, b + 1)
                            nc.scalar.activation(xtm[:, bass.ds(b, 1), :].rearrange("t o d -> t (o d)"), pt[p][0:L, 0:D],
                                                 ACT.Copy).then_inc(kept, 1)

                @block.vector
                def _(dve):
                    dve.sem_inc(maxed, 2)
                    with dve.Fori(0, B // 2) as i:
                        for p in range(2):
                            b = 2 * i + p
                            for h in range(2):
                                dve.wait_ge(scored, 2 * b + h + 5)
                                nc.vector.reduce_max(mx[:, h, bass.ds(b, 1)], pl[h][0:L, :], AX).then_inc(maxed, 1)
                    dve.wait_ge(maxed, 2 * B + 2)
                    nc.vector.tensor_tensor(neg[:], mx[:, 0, :], mx[:, 1, :], ALU.max).then_inc(c, 1)
                    dve.wait_ge(c, 1)
                    nc.vector.tensor_scalar(neg[:], neg[:], -1.0, None, ALU.mult).then_inc(c, 1)
                    dve.wait_ge(c, 3)
                    nc.vector.tensor_copy(negr[:], pt[0][0:B, 0:L]).then_inc(c, 1)

                @block.sync
                def _(sp):
                    sp.wait_ge(c, 4)
                    sp.dma_start(nrow[:], negr[:]).then_inc(rowed, 16)
                    sp.wait_ge(rowed, 16)

        acc, LG, W = s.sb("acc", [L, B, D1]), s.sb("LG", [L, B, QS]), s.sb("W", [D, EQ, D])
        M, Z = s.sb("M", [L, QS]), s.sb("Z", [L, QS])
        xt, dn = [s.sb(f"xt{p}", [L, D]) for p in range(2)], [s.sb(f"dn{p}", [L, QS]) for p in range(2)]
        st, y1 = [s.sb(f"st{p}", [D, QS]) for p in range(2)], [s.sb(f"y1{p}", [128, SUB, D1]) for p in range(2)]
        Cs = [s.sb(f"Cs{p}", [128, SUB, L]) for p in range(2)]
        bA, bY, bC, bO = [[s.ps(f"{n}{p}") for p in range(2)] for n in ("bA", "bY", "bC", "bO")]
        z = {n: s.sem(n) for n in ("loadedW", "phied", "staged", "logited", "kept", "maxed", "subbed", "exped", "summed", "inverted",
                                   "zeroed", "dispatched", "slotted", "slotsT", "clogged", "cexped", "yed", "ycopied", "outed", "added",
                                   "ones", "held")}
        main = ExitStack()
        block = main.enter_context(nc.Block())
        NP = B // GB_

        @block.sync
        def _(sp):
            with sp.Fori(0, NQ) as q:
                sp.wait_ge(z["yed"], B * q + pre)
                sp.sem_inc(z["held"], 1)
                for e in range(EQ):
                    sp.dma_start(W[:, e, :], Wd[bass.ds(q * EQ + e, 1)].rearrange("n d e -> d (n e)")).then_inc(z["loadedW"], 16)

        @block.gpsimd
        def _(pool):
            for p in range(2):
                ins = nc.gpsimd.memset(y1[p][:], 1.0)
            ins.then_inc(z["ones"], 1)
            pool.sem_inc(z["dispatched"], pre)
            pool.sem_inc(z["summed"], 1)
            with pool.Fori(0, NQ) as q:
                with pool.Fori(0, B // 2) as i:
                    for p in range(2):
                        pool.wait_ge(z["logited"], B * q + 2 * i + p + 1)
                        pool.sem_inc(z["held"], 1)
                        nc.gpsimd.tensor_copy(xs[p][:], xT[:, bass.ds((2 * i + p) * L, L)]).then_inc(z["staged"], 1)
                pool.wait_ge(z["dispatched"], B * q + pre)
                pool.sem_inc(z["held"], 1)
                nc.gpsimd.memset(Z[:], 0.0).then_inc(z["zeroed"], 1)
                pool.wait_ge(z["zeroed"], q + 1)
                pool.sem_inc(z["held"], 1)
                with pool.Fori(0, NP) as g:
                    pool.wait_ge(z["exped"], NP * q + g + 1)
                    for b in range(GB_):
                        pool.wait_ge(z["summed"], B * q + GB_ * g + b + 1)
                        nc.gpsimd.tensor_tensor(Z[:], Z[:], LG[:, bass.ds(GB_ * g + b, 1), :].rearrange("t o s -> t (o s)"),
                                                ALU.add).then_inc(z["summed"], 1)
                pool.wait_ge(z["inverted"], q + 1)
                pool.sem_inc(z["held"], 1)
                with pool.Fori(0, B // 2) as i:
                    for p in range(2):
                        pool.wait_ge(z["slotted"], B * q + 2 * i + p + 1)
                        pool.sem_inc(z["held"], 1)
                        nc.gpsimd.tensor_copy(xt[p][:], xtm[:, bass.ds(2 * i + p, 1), :].rearrange("t o d -> t (o d)"))
                        nc.gpsimd.tensor_tensor(dn[p][:], LG[:, bass.ds(2 * i + p, 1), :].rearrange("t o s -> t (o s)"), Z[:],
                                                ALU.mult).then_inc(z["dispatched"], 1)

        @block.tensor
        def _(pe):
            for n in ("logited", "slotted", "clogged", "yed", "outed"):
                pe.sem_inc(z[n], pre)
            pe.wait_ge(z["ones"], 1)
            with pe.Fori(0, NQ) as q:
                pe.wait_ge(z["phied"], q + 1)
                pe.wait_ge(z["slotsT"], B * q + pre)
                pe.sem_inc(z["held"], 1)
                with pe.Fori(0, B // 2) as i:
                    for p in range(2):
                        n = B * q + 2 * i + p
                        pe.wait_ge(z["kept"], n + 1)
                        pe.wait_ge(z["staged"], n + 1)
                        nc.tensor.matmul(bA[p][0:L, :], xs[p][:], phiS[:], start=True, stop=True).then_inc(z["logited"], 1)
                pe.wait_ge(z["loadedW"], 16 * EQ * q + 16 * EQ)
                pe.sem_inc(z["held"], 1)
                with pe.Fori(0, B // 2) as i:
                    for p in range(2):
                        b, n = 2 * i + p, B * q + 2 * i + p
                        pe.wait_ge(z["dispatched"], n + 1 + pre)
                        pe.wait_ge(z["slotsT"], n + 1)
                        nc.tensor.matmul(bA[p][:], xt[p][:], dn[p][:], start=True, stop=True).then_inc(z["slotted"], 1)
                        pe.wait_ge(z["cexped"], n + 1)
                        nc.tensor.matmul(bC[p][:, 0:SUB * L], one16[:], nrow[:, bass.ds(b * L, L)].unsqueeze(1).to_broadcast([1, SUB, L]),
                                         start=True, stop=False, skip_group_check=True)
                        for w in range(SUB):
                            ins = nc.tensor.matmul(bC[p][:, w * L:(w + 1) * L], phiS[:, w * 128:(w + 1) * 128],
                                                   xT[:, bass.ds(b * L, L)], start=False, stop=True, skip_group_check=True)
                        ins.then_inc(z["clogged"], 1)
                    for p in range(2):
                        n = B * q + 2 * i + p
                        pe.wait_ge(z["slotsT"], n + 1 + pre)
                        pe.wait_ge(z["ycopied"], n + 1)
                        for w in range(SUB):
                            for e in range(EW):
                                m = w * EW + e
                                ins = nc.tensor.matmul(bY[p][e * PS:(e + 1) * PS, w * D:(w + 1) * D], st[p][:, m * PS:(m + 1) * PS],
                                                       W[:, m, :], start=True, stop=True, tile_position=(0, e * PS))
                        ins.then_inc(z["yed"], 1)
                    for p in range(2):
                        n = B * q + 2 * i + p
                        pe.wait_ge(z["ycopied"], n + 1 + pre)
                        pe.wait_ge(z["cexped"], n + 1 + pre)
                        pe.wait_ge(z["added"], n + 1)
                        for w in range(SUB):
                            ins = nc.tensor.matmul(bO[p][0:L, 0:D1], Cs[p][:, w, :], y1[p][:, w, :], start=(w == 0), stop=(w == SUB - 1))
                        ins.then_inc(z["outed"], 1)

        @block.scalar
        def _(act):
            nc.scalar.preload_act_table_set("natural_log_exp_and_others")
            for n in ("kept", "cexped"):
                act.sem_inc(z[n], pre)
            with act.Fori(0, NQ) as q:
                act.wait_ge(z["clogged"], B * q + pre)
                nc.scalar.activation(phiS[:], phi[:, bass.ds(q * QS, QS)], ACT.Copy).then_inc(z["phied"], 1)
                act.wait_ge(z["dispatched"], B * q + pre)
                act.sem_inc(z["held"], 1)
                with act.Fori(0, B // 2) as i:
                    for p in range(2):
                        act.wait_ge(z["logited"], B * q + 2 * i + p + 1 + pre)
                        nc.scalar.activation(LG[:, bass.ds(2 * i + p, 1), :].rearrange("t o s -> t (o s)"), bA[p][0:L, :],
                                             ACT.Copy).then_inc(z["kept"], 1)
                with act.Fori(0, NP) as g:
                    act.wait_ge(z["subbed"], NP * q + g + 1)
                    piece = LG[:, bass.ds(GB_ * g, GB_), :]
                    nc.scalar.activation(piece, piece, ACT.Exp).then_inc(z["exped"], 1)
                with act.Fori(0, B // 2) as i:
                    for p in range(2):
                        n = B * q + 2 * i + p
                        act.wait_ge(z["outed"], n + 1)
                        act.wait_ge(z["clogged"], n + 1 + pre)
                        nc.scalar.activation(Cs[p][:].rearrange("s w t -> s (w t)"), bC[p][:, 0:SUB * L], ACT.Exp).then_inc(z["cexped"], 1)

        @block.vector
        def _(dve):
            for n in ("slotsT", "ycopied", "added"):
                dve.sem_inc(z[n], pre)
            dve.sem_inc(z["maxed"], 1)
            nc.vector.memset(acc[:], 0.0).then_inc(z["maxed"], 1)
            with dve.Fori(0, NQ) as q:
                dve.wait_ge(z["maxed"], (B + 1) * q + 2)
                nc.vector.memset(M[:], -3.0e38).then_inc(z["maxed"], 1)
                with dve.Fori(0, B // 2) as i:
                    for p in range(2):
                        n = B * q + 2 * i + p
                        dve.wait_ge(z["kept"], n + 1 + pre)
                        dve.wait_ge(z["maxed"], n + q + 3)
                        nc.vector.tensor_tensor(M[:], M[:], LG[:, bass.ds(2 * i + p, 1), :].rearrange("t o s -> t (o s)"),
                                                ALU.max).then_inc(z["maxed"], 1)
                dve.wait_ge(z["maxed"], (B + 1) * q + B + 3)
                dve.sem_inc(z["held"], 1)
                with dve.Fori(0, NP) as g:
                    piece = LG[:, bass.ds(GB_ * g, GB_), :]
                    nc.vector.tensor_tensor(piece, piece, M[:].unsqueeze(1).to_broadcast([L, GB_, QS]), ALU.subtract).then_inc(z["subbed"], 1)
                dve.wait_ge(z["subbed"], NP * q + NP)
                dve.wait_ge(z["summed"], B * q + B + 1)
                nc.vector.reciprocal(Z[:], Z[:]).then_inc(z["inverted"], 1)
                with dve.Fori(0, B // 2) as i:
                    for p in range(2):
                        n = B * q + 2 * i + p
                        dve.wait_ge(z["slotted"], n + 1 + pre)
                        dve.wait_ge(z["yed"], n + 1)
                        nc.vector.tensor_copy(st[p][:], bA[p][:]).then_inc(z["slotsT"], 1)
                    for p in range(2):
                        n = B * q + 2 * i + p
                        dve.wait_ge(z["yed"], n + 1 + pre)
                        dve.wait_ge(z["outed"], n + 1)
                        nc.vector.tensor_tensor(y1[p][:, :, 0:D], bY[p][:].rearrange("s (w d) -> s w d", d=D),
                                                bias[:, bass.ds(q * SUB, SUB), :], ALU.add).then_inc(z["ycopied"], 1)
                    for p in range(2):
                        b, n = 2 * i + p, B * q + 2 * i + p
                        dve.wait_ge(z["outed"], n + 1 + pre)
                        dve.wait_ge(z["added"], n + 1)
                        dst = acc[:, bass.ds(b, 1), :].rearrange("t o d -> t (o d)")
                        nc.vector.tensor_tensor(dst, dst, bO[p][0:L, 0:D1], ALU.add).then_inc(z["added"], 1)

        main.close()
        half = B // 2
        c, rooted, stored = s.sem("c"), s.sem("rooted"), s.sem("stored")
        rec, mean, var = s.sb("rec", [L, B]), s.sb("mean", [L, B]), s.sb("var", [L, B])
        wide = LG[:, :, 0:D]
        block = ctx.enter_context(nc.Block())

        @block.vector
        def _(dve):
            at = [0]

            def link(ins):
                at[0] += 1
                ins.then_inc(c, 1)
                dve.wait_ge(c, at[0])
            wide_b = lambda t: t[:].unsqueeze(2).to_broadcast([L, B, D])
            link(nc.vector.reciprocal(rec[:], acc[:, :, D]))
            link(nc.vector.tensor_tensor(acc[:, :, 0:D], acc[:, :, 0:D], wide_b(rec), ALU.mult))
            link(nc.vector.tensor_tensor(xtm[:], xtm[:], acc[:, :, 0:D], ALU.add))
            link(nc.vector.tensor_reduce(mean[:], xtm[:], AX, ALU.add))
            link(nc.vector.tensor_scalar(mean[:], mean[:], 1.0 / D, None, ALU.mult))
            link(nc.vector.tensor_tensor(xtm[:], xtm[:], wide_b(mean), ALU.subtract))
            link(nc.vector.tensor_tensor(wide, xtm[:], xtm[:], ALU.mult))
            link(nc.vector.tensor_reduce(var[:], wide, AX, ALU.add))
            dve.wait_ge(rooted, 2)
            for h in range(2):
                bs = slice(h * half, (h + 1) * half)
                nc.vector.tensor_tensor(xtm[:, bs], xtm[:, bs], var[:, bs].unsqueeze(2).to_broadcast([L, half, D]), ALU.mult).then_inc(c, 1)

        @block.scalar
        def _(act):
            nc.scalar.preload_act_table_set("natural_log_exp_and_others")
            act.wait_ge(c, 8)
            nc.scalar.activation(var[:], var[:], ACT.Ln, scale=1.0 / D, bias=k["eps"][0:L]).then_inc(rooted, 1)
            act.wait_ge(rooted, 1)
            nc.scalar.activation(var[:], var[:], ACT.Exp, scale=-0.5).then_inc(rooted, 1)

        @block.sync
        def _(sp):
            for h in range(2):
                bs = slice(h * half, (h + 1) * half)
                sp.wait_ge(c, 9 + h)
                sp.dma_start(out[bs].rearrange("b t d -> t b d"), xtm[:, bs]).then_inc(stored, 16)
            sp.wait_ge(stored, 32)


def decoder(nc, a, out):
    with ExitStack() as ctx:
        k = setup(nc, ctx)
        rows = a["x"].rearrange("b t d -> (b t) d")
        load_transposed(nc, k, "x", [(k["xT"][:, n * 128:(n + 1) * 128], rows[n * 128:(n + 1) * 128, :]) for n in range(N // 128)])
        for n, layer in enumerate((l0_attn, l0_xattn, l0_ffn, l1_attn, l1_xattn, l1_ffn, l2_attn, l2_xattn, l2_ffn,
                                   l3_attn, l3_xattn)):
            layer(nc, k, a)
            norm_pass(nc, k, f"norm{n}")
        l3_ffn(nc, k, a, out)


def kernel(**inputs):
    import concourse.bacc as bacc
    from concourse.bass_utils import run_bass_kernel_spmd

    nc = bacc.Bacc("TRN2", target_bir_lowering=False, num_devices=1)
    arrays, a = {}, {}
    for name, value in inputs.items():
        value = np.ascontiguousarray(value)
        arrays[f"in_{name}_dram"] = value
        a[name] = nc.dram_tensor(f"in_{name}_dram", value.shape, mybir.dt.from_np(value.dtype), kind="ExternalInput").ap()
    out = nc.dram_tensor("out_0_dram", (B, L, D), F32, kind="ExternalOutput").ap()
    decoder(nc, a, out)
    return run_bass_kernel_spmd(nc, [arrays], core_ids=[0]).results[0]["out_0_dram"]
```

```python
from contextlib import ExitStack

import numpy as np
import concourse.bass as bass
from concourse import mybir

ALU = mybir.AluOpType
ACT = mybir.ActivationFunctionType
AX = mybir.AxisListType.X
F32 = mybir.dt.float32
BF16 = mybir.dt.bfloat16
I32 = mybir.dt.int32

B, L, D = 32, 100, 128
N = B * L
GB = 4
GT = GB * L
NG = B // GB


def setup(nc, ctx):
    k = {}
    def sb(name, shape, dt=F32):
        k[name] = ctx.enter_context(nc.sbuf_tensor(name, shape, dt))
        return k[name]
    sb("xT", [D, N])
    sb("ident", [128, 128])
    sb("center", [128, 128])
    sb("mean", [128, 128])
    sb("eps", [128, 1])
    made = ctx.enter_context(nc.semaphore("consts_made"))
    with nc.Block() as block:
        @block.gpsimd
        def _(pool):
            nc.gpsimd.memset(k["mean"][:], 1.0 / D)
            nc.gpsimd.memset(k["eps"][:], 1e-5)
            nc.gpsimd.memset(k["ident"][:], 0.0).then_inc(made, 1)
            pool.wait_ge(made, 1)
            nc.gpsimd.affine_select(out=k["ident"][:], in_=k["ident"][:], compare_op=ALU.not_equal, fill=1.0,
                                    base=0, pattern=[[-1, 128]], channel_multiplier=1).then_inc(made, 1)
            pool.wait_ge(made, 2)
            nc.gpsimd.tensor_tensor(k["center"][:], k["ident"][:], k["mean"][:], ALU.subtract).then_inc(made, 1)
    return k


def norm_pass(nc, k, tag):
    xT = k["xT"]
    with ExitStack() as ctx:
        sem = Stage(nc, ctx, tag).sem
        ps_c = [ctx.enter_context(nc.psum_tensor(f"{tag}_c{p}", [128, 512], F32)) for p in range(2)]
        ps_v = [ctx.enter_context(nc.psum_tensor(f"{tag}_v{p}", [128, 512], F32)) for p in range(2)]
        sq = [ctx.enter_context(nc.sbuf_tensor(f"{tag}_sq{p}", [128, GT], F32)) for p in range(2)]
        rs = [ctx.enter_context(nc.sbuf_tensor(f"{tag}_rs{p}", [128, GT], F32)) for p in range(2)]
        centered, squared, summed, logged, rooted, scaled = [[sem(f"{n}{p}") for p in range(2)] for n in
            ("centered", "squared", "summed", "logged", "rooted", "scaled")]
        block = ctx.enter_context(nc.Block())

        @block.tensor
        def _(pe):
            with pe.Fori(0, NG // 2) as i:
                for p in range(2):
                    pe.wait_ge(scaled[p], i + 1)
                    nc.tensor.matmul(ps_c[p][:, 0:GT], k["center"][:], xT[:, bass.ds((2 * i + p) * GT, GT)],
                                     start=True, stop=True).then_inc(centered[p], 1)
                for p in range(2):
                    pe.wait_ge(squared[p], i + 1)
                    nc.tensor.matmul(ps_v[p][:, 0:GT], k["mean"][:], sq[p][:], start=True, stop=True).then_inc(summed[p], 1)

        @block.scalar
        def _(act):
            nc.scalar.preload_act_table_set("natural_log_exp_and_others")
            with act.Fori(0, NG // 2) as i:
                for p in range(2):
                    act.wait_ge(centered[p], i + 1)
                    nc.scalar.activation(sq[p][:], ps_c[p][:, 0:GT], ACT.Square).then_inc(squared[p], 1)
                for p in range(2):
                    act.wait_ge(summed[p], i + 1)
                    act.wait_ge(scaled[p], i + 1)
                    nc.scalar.activation(rs[p][:], ps_v[p][:, 0:GT], ACT.Ln, bias=k["eps"][:]).then_inc(logged[p], 1)
                    act.wait_ge(logged[p], i + 1)
                    nc.scalar.activation(rs[p][:], rs[p][:], ACT.Exp, scale=-0.5).then_inc(rooted[p], 1)

        @block.vector
        def _(dve):
            for p in range(2):
                dve.sem_inc(scaled[p], 1)
            with dve.Fori(0, NG // 2) as i:
                for p in range(2):
                    dve.wait_ge(rooted[p], i + 1)
                    nc.vector.tensor_tensor(xT[:, bass.ds((2 * i + p) * GT, GT)], ps_c[p][:, 0:GT], rs[p][:],
                                            ALU.mult).then_inc(scaled[p], 1)


class Stage:

    def __init__(self, nc, ctx, tag):
        self.nc, self.ctx, self.tag, self.sems = nc, ctx, tag, []
        ctx.callback(self.clear)

    def clear(self):
        self.nc.clear_and_free_semaphores(self.sems)
        self.nc.all_engine_barrier()

    def sb(self, name, shape, dt=F32):
        return self.ctx.enter_context(self.nc.sbuf_tensor(f"{self.tag}_{name}", shape, dt))

    def ps(self, name, shape=(128, 512), dt=F32):
        return self.ctx.enter_context(self.nc.psum_tensor(f"{self.tag}_{name}", list(shape), dt))

    def sem(self, name):
        self.sems.append(self.nc.alloc_semaphore(f"{self.tag}_{name}"))
        return self.sems[-1]


def load(nc, tag, pairs):
    with ExitStack() as ctx:
        loaded = Stage(nc, ctx, tag).sem("loaded")
        with nc.Block() as block:
            @block.sync
            def _(sp):
                for dst, src in pairs[0::2]:
                    sp.dma_start(dst, src, allow_slow_non_contiguous=True).then_inc(loaded, 16)
                sp.wait_ge(loaded, 16 * len(pairs))

            @block.scalar
            def _(act):
                for dst, src in pairs[1::2]:
                    act.dma_start(dst, src, allow_slow_non_contiguous=True).then_inc(loaded, 16)


def load_transposed(nc, k, tag, items, by=None):
    W = 4
    with ExitStack() as ctx:
        s = Stage(nc, ctx, tag)
        nat = s.sb("nat", [128, len(items), 128])
        turned = [s.ps(f"turned{p}") for p in range(2)]
        loaded, transposed, copied = s.sem("loaded"), s.sem("transposed"), s.sem("copied")
        block = ctx.enter_context(nc.Block())

        @block.sync
        def _(sp):
            for n, (dst, src) in enumerate(items):
                sp.dma_start(nat[0:src.shape[0], n, 0:src.shape[1]], src).then_inc(loaded, 16)

        @block.tensor
        def _(pe):
            pe.wait_ge(loaded, 16 * len(items))
            for n, (dst, src) in enumerate(items):
                o, i = src.shape
                if n >= 2 * W and n % W == 0:
                    pe.wait_ge(copied, n - W)
                bank = turned[n // W % 2][0:i, n % W * 128:n % W * 128 + o]
                if by is None:
                    nc.tensor.transpose(bank, nat[0:o, n, 0:i], k["ident"][0:o, 0:o]).then_inc(transposed, 1)
                else:
                    nc.tensor.matmul(bank, nat[0:o, n, 0:i], by[0:o, 0:o], start=True, stop=True).then_inc(transposed, 1)

        @block.vector
        def _(dve):
            for n, (dst, src) in enumerate(items):
                o, i = src.shape
                dve.wait_ge(transposed, min((n // W + 1) * W, len(items)))
                nc.vector.tensor_copy(dst, turned[n // W % 2][0:i, n % W * 128:n % W * 128 + o]).then_inc(copied, 1)


def col(ap):
    return ap.rearrange("(n o) -> n o", o=1)


def l1_ffn(nc, k, a):
    E, F = a["L1_ffn_Wg"].shape[0], a["L1_ffn_Wg"].shape[2]
    C = F // 128
    S = E * C
    xT = k["xT"]
    with ExitStack() as ctx:
        s = Stage(nc, ctx, "l1f")
        wg, wu, wd = s.sb("wg", [D, E, F]), s.sb("wu", [D, E, F]), s.sb("wd", [128, E, C, D])
        load(nc, "l1fw", [(wg[:], a["L1_ffn_Wg"].rearrange("e d f -> d e f")),
                          (wu[:], a["L1_ffn_Wu"].rearrange("e d f -> d e f")),
                          (wd[:], a["L1_ffn_Wd"].rearrange("e (c f) d -> f e c d", f=128))])
        g, u, acc = [s.ps(f"g{p}") for p in range(2)], [s.ps(f"u{p}") for p in range(2)], s.ps("acc")
        sg, h = [s.sb(f"sg{p}", [128, GT]) for p in range(2)], [s.sb(f"h{p}", [128, GT]) for p in range(2)]
        gated, upped, activated, multiplied, downed, added = [s.sem(n) for n in
            ("gated", "upped", "activated", "multiplied", "downed", "added")]
        block = ctx.enter_context(nc.Block())

        @block.tensor
        def _(pe):
            def down(i, n):
                pe.wait_ge(multiplied, i * S + n + 1)
                if n == 0:
                    pe.wait_ge(added, i + 1)
                nc.tensor.matmul(acc[:, 0:GT], wd[:, n // C, n % C, :], h[n % 2][:], start=(n == 0),
                                 stop=(n == S - 1)).then_inc(downed, 1)
            with pe.Fori(0, NG) as i:
                x = xT[:, bass.ds(i * GT, GT)]
                for n in range(S):
                    e, f = n // C, slice(n % C * 128, n % C * 128 + 128)
                    if n >= 2:
                        pe.wait_ge(multiplied, i * S + n - 1)
                    nc.tensor.matmul(g[n % 2][:, 0:GT], wg[:, e, f], x, start=True, stop=True).then_inc(gated, 1)
                    nc.tensor.matmul(u[n % 2][:, 0:GT], wu[:, e, f], x, start=True, stop=True).then_inc(upped, 1)
                    if n >= 1:
                        down(i, n - 1)
                down(i, S - 1)

        @block.scalar
        def _(act):
            with act.Fori(0, NG) as i:
                for n in range(S):
                    act.wait_ge(gated, i * S + n + 1)
                    if n >= 2:
                        act.wait_ge(multiplied, i * S + n - 1)
                    else:
                        act.wait_ge(added, i + 1)
                    nc.scalar.activation(sg[n % 2][:], g[n % 2][:, 0:GT], ACT.Silu).then_inc(activated, 1)

        @block.vector
        def _(dve):
            dve.sem_inc(added, 1)
            with dve.Fori(0, NG) as i:
                for n in range(S):
                    dve.wait_ge(activated, i * S + n + 1)
                    dve.wait_ge(upped, i * S + n + 1)
                    if n >= 2:
                        dve.wait_ge(downed, i * S + n - 1)
                    nc.vector.tensor_tensor(h[n % 2][:], sg[n % 2][:], u[n % 2][:, 0:GT], ALU.mult).then_inc(multiplied, 1)
                dve.wait_ge(downed, i * S + S)
                x = xT[:, bass.ds(i * GT, GT)]
                nc.vector.tensor_tensor(x, x, acc[:, 0:GT], ALU.add).then_inc(added, 1)


def l2_attn(nc, k, a):
    xT = k["xT"]
    DC = 32
    NC = D // DC
    with ExitStack() as ctx:
        s = Stage(nc, ctx, "l2a")
        u, flip = s.sb("u", [D, 2 * L]), s.sb("flip", [L, L])
        flipped = s.sem("flipped")
        with nc.Block() as block:
            @block.gpsimd
            def _(pool):
                nc.gpsimd.memset(flip[:], 0.0).then_inc(flipped, 1)
                pool.wait_ge(flipped, 1)
                nc.gpsimd.affine_select(out=flip[:], in_=flip[:], compare_op=ALU.not_equal, fill=1.0, base=1 - L,
                                        pattern=[[1, L]], channel_multiplier=1)
        t = a["L2_attn_t"]
        load_transposed(nc, k, "l2at", [(u[:, 0:L], t[0:L, :]), (u[:, L:2 * L], t[L:2 * L, :])], by=flip)
        ud = nc.dram_tensor("l2a_ud", [D, 2 * L], F32).ap()
        toe = [s.sb(f"toe{p}", [L, DC, L]) for p in range(2)]
        xs, xtm, ytm = [s.sb(f"xs{p}", [D, GT]) for p in range(2)], s.sb("xtm", [L, D, B]), s.sb("ytm", [L, B, D])
        pt, py = [s.ps(f"pt{p}") for p in range(2)], [s.ps(f"py{p}", (128, 1024)) for p in range(2)]
        wrote, staged, turned, kept = s.sem("wrote"), s.sem("staged"), s.sem("turned"), s.sem("kept")
        filled = [s.sem(f"filled{p}") for p in range(2)]
        convolved, out, back, added = s.sem("convolved"), s.sem("out"), s.sem("back"), s.sem("added")
        block = ctx.enter_context(nc.Block())
        hb = DC // 2

        @block.sync
        def _(sp):
            sp.dma_start(ud, u[:]).then_inc(wrote, 16)
            sp.wait_ge(wrote, 16)
            for c in range(NC):
                if c >= 2:
                    sp.wait_ge(convolved, c - 1)
                src = bass.AP(tensor=ud.tensor, offset=ud.offset + c * DC * 2 * L, ap=[[1, L], [2 * L, DC], [1, L]])
                sp.dma_start(toe[c % 2][:], src).then_inc(filled[c % 2], 16)

        @block.vector
        def _(dve):
            dve.sem_inc(turned, 2)
            with dve.Fori(0, NG // 2) as i:
                for p in range(2):
                    dve.wait_ge(turned, 2 * i + p + 1)
                    nc.vector.tensor_copy(xs[p][:], xT[:, bass.ds((2 * i + p) * GT, GT)]).then_inc(staged, 1)
            for c in range(NC):
                dve.wait_ge(convolved, c + 1)
                for n in range(2):
                    d0 = c * DC + n * hb
                    ins = nc.vector.tensor_copy(ytm[:, :, d0:d0 + hb].rearrange("i b d -> i d b"),
                                                py[c % 2][0:L, n * 512:n * 512 + 512].rearrange("i (d b) -> i d b", b=B))
                ins.then_inc(out, 1)
            for g in range(NG):
                dve.wait_ge(back, g + 1)
                x = xT[:, g * GT:(g + 1) * GT]
                nc.vector.tensor_tensor(x, x, pt[g % 2][:, 0:GT], ALU.add).then_inc(added, 1)

        @block.scalar
        def _(act):
            with act.Fori(0, NG // 2) as i:
                for p in range(2):
                    act.wait_ge(turned, 2 * i + p + 3)
                    nc.scalar.activation(xtm[:, :, bass.ds((2 * i + p) * GB, GB)].rearrange("t d b -> t b d"),
                                         pt[p][0:L, :].rearrange("t (b d) -> t b d", d=D), ACT.Copy).then_inc(kept, 1)

        @block.tensor
        def _(pe):
            pe.sem_inc(kept, 2)
            with pe.Fori(0, NG // 2) as i:
                for p in range(2):
                    pe.wait_ge(staged, 2 * i + p + 1)
                    pe.wait_ge(kept, 2 * i + p + 1)
                    for b in range(GB):
                        ins = nc.tensor.transpose(pt[p][0:L, b * D:(b + 1) * D], xs[p][:, b * L:(b + 1) * L], k["ident"][:])
                    ins.then_inc(turned, 1)
            pe.wait_ge(kept, NG + 2)
            for c in range(NC):
                pe.wait_ge(filled[c % 2], 16 * (c // 2 + 1))
                if c >= 2:
                    pe.wait_ge(out, c - 1)
                for d in range(DC):
                    ins = nc.tensor.matmul(py[c % 2][0:L, d * B:(d + 1) * B], toe[c % 2][:, d, :], xtm[:, c * DC + d, :],
                                           start=True, stop=True)
                ins.then_inc(convolved, 1)
            pe.wait_ge(out, NC)
            for g in range(NG):
                if g >= 2:
                    pe.wait_ge(added, g - 1)
                for b in range(GB):
                    ins = nc.tensor.matmul(pt[g % 2][:, b * L:(b + 1) * L], ytm[:, g * GB + b, :], flip[:], start=True, stop=True)
                ins.then_inc(back, 1)


def l0_attn(nc, k, a):
    xT = k["xT"]
    H, J, W = a["L0_attn_cw1"].shape[0], a["L0_attn_cw1"].shape[1], 7
    DH, PAD, HC = D // H, W // 2, 128 // J
    NC = H // HC
    LP = L + 2 * PAD
    with ExitStack() as ctx:
        s = Stage(nc, ctx, "l0a")
        w = s.sb("w", [D, 4, D])
        cw2T, cw3c, cb = s.sb("cw2T", [128, NC, 128]), s.sb("cw3c", [128, NC, 1]), s.sb("cb", [128, 2, NC])
        cw1c, pos, headof, bo, cb3 = s.sb("cw1c", [128, NC]), s.sb("pos", [128, W]), s.sb("headof", [128, 128]), s.sb("bo", [D, 1]), s.sb("cb3", [D, 1])
        cw2n = s.sb("cw2n", [128, NC, J])
        hid = [s.sb(f"hid{n}", [128, NC, W]) for n in range(3)]
        place, conn, stat = s.sb("place", [128, NC, D]), s.sb("conn", [D, W]), s.sb("stat", [D, 4])
        load_transposed(nc, k, "l0at", [(w[:, n, :], a[f"L0_attn_w{c}"]) for n, c in enumerate("qkvo")])
        flat = lambda name, n: a[name].rearrange("(c h) j -> (h j) c", c=n)
        load(nc, "l0al", [
            (cw1c[:], a["L0_attn_cw1"].rearrange("(c h) j o -> (h j) (c o)", c=NC)),
            (cb[:, 0, :], flat("L0_attn_cb1", NC)), (cb[:, 1, :], flat("L0_attn_cb2", NC)),
            (cw3c[:], a["L0_attn_cw3"].rearrange("(c h) o j -> (h j) c o", c=NC)),
            (bo[:], col(a["L0_attn_bo"])),
            (cw2n[:], a["L0_attn_cw2"].rearrange("(c h) j i -> (h j) c i", c=NC))]
            + [(cb3[h * DH:(h + 1) * DH, :], a["L0_attn_cb3"][h:h + 1, :].to_broadcast([DH, 1])) for h in range(H)])
        m = s.sem("m")
        pc = s.ps("pc")
        cw2d = s.sb("cw2d", [128, NC, 128])
        with nc.Block() as block:
            @block.gpsimd
            def _(pool):
                for j in range(W):
                    nc.gpsimd.memset(pos[:, j:j + 1], float(np.linspace(0.0, 1.0, W, dtype=np.float32)[j]))
                nc.gpsimd.memset(headof[:], 1.0)
                nc.gpsimd.memset(place[:], 1.0)
                nc.gpsimd.memset(cw2d[:], 0.0).then_inc(m, 1)
                pool.wait_ge(m, 1)
                hv = headof[:].rearrange("p (h d) -> p h d", d=DH)
                nc.gpsimd.affine_select(out=hv, in_=hv, compare_op=ALU.is_ge, fill=0.0, base=0,
                                        pattern=[[-DH, H], [0, DH]], channel_multiplier=1).then_inc(m, 1)
                pv = place[:].rearrange("p c (g d) -> p c g d", d=DH)
                for c in range(NC):
                    nc.gpsimd.affine_select(out=pv[:, c], in_=pv[:, c], compare_op=ALU.is_ge, fill=0.0, base=J * HC * c,
                                            pattern=[[-J, H], [0, DH]], channel_multiplier=1)
                pool.wait_ge(m, 2)
                nc.gpsimd.affine_select(out=hv, in_=hv, compare_op=ALU.is_ge, fill=0.0, base=DH - 1,
                                        pattern=[[DH, H], [0, DH]], channel_multiplier=-1).then_inc(m, 1)
                pool.wait_ge(m, 3)
                for c in range(NC):
                    last = nc.gpsimd.affine_select(out=pv[:, c], in_=pv[:, c], compare_op=ALU.is_ge, fill=0.0,
                                                   base=J - 1 - J * HC * c, pattern=[[J, H], [0, DH]], channel_multiplier=-1)
                last.then_inc(m, 1)

            @block.vector
            def _(dve):
                dve.wait_ge(m, 4)
                for c in range(NC):
                    for h in range(HC):
                        r = slice(h * J, h * J + J)
                        nc.vector.tensor_copy(cw2d[r, c, h * J:h * J + J], cw2n[r, c, :])
                    nc.vector.tensor_scalar(hid[0][:, c, :], pos[:], cw1c[:, c:c + 1], cb[:, 0, c:c + 1], ALU.mult, ALU.add)
                    last = nc.vector.tensor_scalar(place[:, c, :], place[:, c, :], cw3c[:, c, :], None, ALU.mult)
                last.then_inc(m, 1)
                dve.wait_ge(m, 6)
                nc.vector.tensor_copy(cw2T[:].rearrange("p c n -> p (c n)"), pc[:]).then_inc(m, 1)
                dve.wait_ge(m, 9)
                for c in range(NC):
                    last = nc.vector.tensor_scalar(hid[2][:, c, :], pc[:, c * W:c * W + W], cb[:, 1, c:c + 1], None, ALU.add)
                last.then_inc(m, 1)
                dve.wait_ge(m, 12)
                nc.vector.tensor_scalar(conn[:], pc[:, 64:64 + W], cb3[:], None, ALU.add).then_inc(m, 1)
                dve.wait_ge(m, 13)
                nc.vector.reduce_max(stat[:, 0:1], conn[:], AX).then_inc(m, 1)
                dve.wait_ge(m, 14)
                nc.vector.tensor_scalar(stat[:, 1:2], stat[:, 0:1], -1.0, None, ALU.mult).then_inc(m, 1)
                dve.wait_ge(m, 16)
                nc.vector.reduce_sum(stat[:, 2:3], conn[:], AX).then_inc(m, 1)
                dve.wait_ge(m, 17)
                nc.vector.reciprocal(stat[:, 3:4], stat[:, 2:3]).then_inc(m, 1)
                dve.wait_ge(m, 18)
                nc.vector.tensor_scalar(conn[:], conn[:], stat[:, 3:4], None, ALU.mult).then_inc(m, 1)

            @block.tensor
            def _(pe):
                pe.wait_ge(m, 5)
                for c in range(NC):
                    last = nc.tensor.transpose(pc[:, c * 128:c * 128 + 128], cw2d[:, c, :], k["ident"][:])
                last.then_inc(m, 1)
                pe.wait_ge(m, 8)
                for c in range(NC):
                    last = nc.tensor.matmul(pc[:, c * W:c * W + W], cw2T[:, c, :], hid[1][:, c, :], start=True, stop=True)
                last.then_inc(m, 1)
                pe.wait_ge(m, 11)
                for c in range(NC):
                    last = nc.tensor.matmul(pc[:, 64:64 + W], place[:, c, :], hid[1][:, c, :], start=(c == 0), stop=(c == NC - 1))
                last.then_inc(m, 1)

            @block.scalar
            def _(act):
                act.wait_ge(m, 7)
                nc.scalar.activation(hid[1][:], hid[0][:], ACT.Gelu).then_inc(m, 1)
                act.wait_ge(m, 10)
                nc.scalar.activation(hid[1][:], hid[2][:], ACT.Gelu).then_inc(m, 1)
                act.wait_ge(m, 15)
                nc.scalar.activation(conn[:], conn[:], ACT.Exp, bias=stat[:, 1:2]).then_inc(m, 1)

        ps = {n: s.ps(f"p{n}") for n in "qkvo"}
        psc = [s.ps(f"sc{p}") for p in range(2)]
        q = s.sb("q", [D, GT])
        kp, vp = s.sb("kp", [D, GB, LP]), s.sb("vp", [D, GB, LP])
        prod = [s.sb(f"prod{p}", [D, GT]) for p in range(2)]
        sc = s.sb("sc", [D, W, GT])
        top, zs, cs, o = s.sb("top", [D, GT]), s.sb("zs", [D, GT]), s.sb("cs", [D, GT]), s.sb("o", [D, GT])
        projected, moved, timesed, headed, scored, shifted, exped, outed, wod, addd = [s.sem(n) for n in
            ("projected", "moved", "timesed", "headed", "scored", "shifted", "exped", "outed", "wod", "addd")]
        chain = s.sem("chain")
        block = ctx.enter_context(nc.Block())
        shape = lambda ap: ap.rearrange("d (b t) -> d b t", t=L)

        @block.tensor
        def _(pe):
            with pe.Fori(0, NG) as i:
                pe.wait_ge(addd, i + 1)
                x = xT[:, bass.ds(i * GT, GT)]
                for n, c in enumerate("qkv"):
                    nc.tensor.matmul(ps[c][:, 0:GT], w[:, n, :], x, start=True, stop=True).then_inc(projected, 1)
                for j in range(W):
                    pe.wait_ge(timesed, i * W + j + 1)
                    if j >= 2:
                        pe.wait_ge(scored, i * W + j - 1)
                    nc.tensor.matmul(psc[j % 2][:, 0:GT], headof[:], prod[j % 2][:], start=True, stop=True).then_inc(headed, 1)
                pe.wait_ge(outed, i + 1)
                nc.tensor.matmul(ps["o"][:, 0:GT], w[:, 3, :], o[:], start=True, stop=True).then_inc(wod, 1)

        @block.scalar
        def _(act):
            nc.scalar.preload_act_table_set("natural_log_exp_and_others")
            with act.Fori(0, NG) as i:
                for n, (c, dst) in enumerate((("q", shape(q[:])), ("k", kp[:, :, PAD:PAD + L]), ("v", vp[:, :, PAD:PAD + L]))):
                    act.wait_ge(projected, 3 * i + n + 1)
                    if c == "q":
                        act.wait_ge(addd, i + 1)
                    nc.scalar.activation(dst, shape(ps[c][:, 0:GT]), ACT.Copy,
                                         scale=float(DH ** -0.5) if c == "q" else 1.0).then_inc(moved, 1)
                act.wait_ge(shifted, i + 1)
                nc.scalar.activation(sc[:], sc[:], ACT.Exp).then_inc(exped, 1)

        @block.vector
        def _(dve):
            nc.vector.memset(kp[:], 0.0).then_inc(chain, 1)
            nc.vector.memset(vp[:], 0.0).then_inc(chain, 1)
            dve.wait_ge(chain, 2)
            dve.sem_inc(addd, 1)
            CH = 2 * W + 6
            with dve.Fori(0, NG) as i:
                at = [0]

                def link(ins):
                    at[0] += 1
                    ins.then_inc(chain, 1)
                    dve.wait_ge(chain, i * CH + 2 + at[0])
                dve.wait_ge(moved, 3 * i + 3)
                for j in range(W + 1):
                    if j < W:
                        if j >= 2:
                            dve.wait_ge(headed, i * W + j - 1)
                        nc.vector.tensor_tensor(shape(prod[j % 2][:]), shape(q[:]), kp[:, :, j:j + L], ALU.mult).then_inc(timesed, 1)
                    if j >= 1:
                        dve.wait_ge(headed, i * W + j)
                        nc.vector.tensor_copy(sc[:, j - 1, :], psc[(j - 1) % 2][:, 0:GT]).then_inc(scored, 1)
                dve.wait_ge(scored, i * W + W)
                link(nc.vector.tensor_reduce(top[:], sc[:].rearrange("d w t -> d t w"), AX, ALU.max))
                nc.vector.tensor_tensor(sc[:], sc[:], top[:].unsqueeze(1).to_broadcast([D, W, GT]), ALU.subtract).then_inc(shifted, 1)
                dve.wait_ge(exped, i + 1)
                link(nc.vector.tensor_reduce(zs[:], sc[:].rearrange("d w t -> d t w"), AX, ALU.add))
                for j in range(W):
                    link(nc.vector.tensor_scalar(sc[:, j, :], sc[:, j, :], conn[:, j:j + 1], None, ALU.mult))
                link(nc.vector.tensor_reduce(cs[:], sc[:].rearrange("d w t -> d t w"), AX, ALU.add))
                link(nc.vector.scalar_tensor_tensor(out=cs[:], in0=zs[:], scalar=1e-9, in1=cs[:], op0=ALU.mult, op1=ALU.add))
                link(nc.vector.reciprocal(cs[:], cs[:]))
                for j in range(W):
                    link(nc.vector.tensor_tensor(shape(sc[:, j, :]), shape(sc[:, j, :]), vp[:, :, j:j + L], ALU.mult))
                link(nc.vector.tensor_reduce(o[:], sc[:].rearrange("d w t -> d t w"), AX, ALU.add))
                nc.vector.tensor_tensor(o[:], o[:], cs[:], ALU.mult).then_inc(outed, 1)
                dve.wait_ge(wod, i + 1)
                x = xT[:, bass.ds(i * GT, GT)]
                nc.vector.scalar_tensor_tensor(out=x, in0=ps["o"][:, 0:GT], scalar=bo[:], in1=x, op0=ALU.add,
                                               op1=ALU.add).then_inc(addd, 1)
                assert at[0] == CH


def l0_xattn(nc, k, a):
    xT, ctxd, lens = k["xT"], a["ctx_2048"], a["mask_BxS2_if0"]
    P = lens.shape[1]
    Q = 4
    PQ = P // Q
    C = ctxd.shape[2]
    DT = float(-np.log(-np.expm1(np.float32(-0.001))))
    BC = float(np.exp(np.float32(-0.001)))
    with ExitStack() as ctx:
        s = Stage(nc, ctx, "l0x")
        winT, cols, decay = s.sb("winT", [D, D]), s.sb("cols", [D, 3]), s.sb("decay", [L, L])
        plug = s.sb("plug", [L, N])
        rowid, ln_bc = s.sb("rowid", [L, 1]), s.sb("ln_bc", [L, 1])
        plug_d = nc.dram_tensor("l0x_plug_d", [B, L], F32).ap()
        m = s.sem("m")
        load_transposed(nc, k, "l0xt", [(winT[:], a["L0_xattn_W_in"])])
        with ExitStack() as own:
            t = Stage(nc, own, "l0xp")
            li, lf, one, cs = t.sb("li", [B * Q, PQ], I32), t.sb("lf", [B * Q, PQ]), t.sb("one", [B * Q, PQ]), t.sb("cs", [B * Q, PQ])
            neg, hit, dump = t.sb("neg", [B * Q, PQ]), t.sb("hit", [B * Q, L]), t.sb("dump", [B * Q, PQ])
            before, same = t.sb("before", [128, 128]), t.sb("same", [128, B])
            carry, bm, cnt = t.sb("carry", [128, 1]), t.sb("bm", [B, L]), t.sb("cnt", [B, L])
            pp = t.ps("pp")
            load(nc, "l0xl", [(li[:], lens.rearrange("b (q s) -> (b q) s", q=Q)), (cols[:, 0:1], col(a["L0_xattn_g_res"])),
                              (cols[:, 1:2], col(a["L0_xattn_b_in"])), (cols[:, 2:3], col(a["L0_xattn_g_init"][0:D]))])
            with nc.Block() as block:
                @block.gpsimd
                def _(pool):
                    nc.gpsimd.memset(before[:], 1.0)
                    nc.gpsimd.memset(same[:], 1.0)
                    nc.gpsimd.memset(one[:], 1.0)
                    nc.gpsimd.memset(ln_bc[:], float(np.log(BC)))
                    nc.gpsimd.iota(rowid[:], pattern=[[0, 1]], base=0, channel_multiplier=1,
                                   allow_small_or_imprecise_dtypes=True)
                    nc.gpsimd.iota(decay[:], pattern=[[-1, L]], base=0, channel_multiplier=1,
                                   allow_small_or_imprecise_dtypes=True).then_inc(m, 1)
                    pool.wait_ge(m, 1)
                    nc.gpsimd.affine_select(out=decay[:], in_=decay[:], compare_op=ALU.is_ge, fill=1e4, base=0,
                                            pattern=[[-1, L]], channel_multiplier=1)
                    bv = before[:].rearrange("p (b q) -> p b q", q=Q)
                    nc.gpsimd.affine_select(out=bv, in_=bv, compare_op=ALU.is_ge, fill=0.0, base=0,
                                            pattern=[[-Q, B], [0, Q]], channel_multiplier=1)
                    nc.gpsimd.affine_select(out=same[:], in_=same[:], compare_op=ALU.is_ge, fill=0.0, base=0,
                                            pattern=[[-Q, B]], channel_multiplier=1).then_inc(m, 1)
                    pool.wait_ge(m, 2)
                    nc.gpsimd.affine_select(out=before[:], in_=before[:], compare_op=ALU.is_gt, fill=0.0, base=0,
                                            pattern=[[1, 128]], channel_multiplier=-1)
                    nc.gpsimd.affine_select(out=same[:], in_=same[:], compare_op=ALU.is_ge, fill=0.0, base=Q - 1,
                                            pattern=[[Q, B]], channel_multiplier=-1).then_inc(m, 1)

                @block.scalar
                def _(act):
                    nc.scalar.preload_act_table_set("natural_log_exp_and_others")
                    act.wait_ge(m, 3)
                    nc.scalar.activation(decay[:], decay[:], ACT.Exp, bias=ln_bc[:], scale=-DT)

                chain = t.sem("chain")

                @block.vector
                def _(dve):
                    at = [0]

                    def link(ins):
                        at[0] += 1
                        ins.then_inc(chain, 1)
                        dve.wait_ge(chain, at[0])
                    dve.wait_ge(m, 3)
                    nc.vector.tensor_scalar(winT[:], winT[:], cols[:, 0:1], None, ALU.mult)
                    link(nc.vector.tensor_copy(lf[:], li[:]))
                    nc.vector.tensor_tensor_scan(cs[:], one[:], lf[:], 0.0, ALU.mult, ALU.add).then_inc(m, 1)
                    dve.wait_ge(m, 5)
                    link(nc.vector.tensor_copy(carry[:], pp[:, 0:1]))
                    link(nc.vector.tensor_scalar(cs[:], cs[:], carry[:], -1.0, ALU.add, ALU.add))
                    link(nc.vector.tensor_scalar(neg[:], cs[:], 0.0, float(L), ALU.is_lt, ALU.mult))
                    link(nc.vector.tensor_tensor(cs[:], cs[:], neg[:], ALU.add))
                    for j in range(L):
                        ins = nc.vector.tensor_scalar(dump[:], cs[:], float(j), 0.0, ALU.is_equal, ALU.max,
                                                      accum_out=hit[:, j:j + 1])
                        link(ins)
                    dve.sem_inc(m, 1)
                    dve.wait_ge(m, 7)
                    link(nc.vector.tensor_scalar(bm[:], pp[0:B, 64:64 + L], 1.0, None, ALU.min))
                    link(nc.vector.tensor_tensor_scan(cnt[:], one[0:B, 0:L], bm[:], 0.0, ALU.mult, ALU.add))
                    nc.vector.tensor_scalar(cnt[:], cnt[:], -1.0, 0.0, ALU.add, ALU.max).then_inc(m, 1)

                @block.tensor
                def _(pe):
                    pe.wait_ge(m, 4)
                    nc.tensor.matmul(pp[:, 0:1], before[:], cs[:, PQ - 1:PQ], start=True, stop=True).then_inc(m, 1)
                    pe.wait_ge(m, 6)
                    nc.tensor.matmul(pp[0:B, 64:64 + L], same[:], hit[:], start=True, stop=True).then_inc(m, 1)

                @block.sync
                def _(sp):
                    sp.wait_ge(m, 8)
                    sp.dma_start(plug_d, cnt[:]).then_inc(m, 16)
                    sp.wait_ge(m, 24)
                    sp.dma_start(plug[:], plug_d.rearrange("b t -> (b t)").unsqueeze(0).to_broadcast([L, N])).then_inc(m, 16)
                    sp.wait_ge(m, 40)

        cx = [s.sb(f"cx{p}", [L, GB, C]) for p in range(2)]
        scr, ss, sel, wt = s.sb("scr", [L, C]), s.sb("ss", [L, GB]), s.sb("sel", [L, GT]), s.sb("wt", [L, GT])
        sq, rs, h = s.sb("sq", [D, GT]), s.sb("rs", [D, GT]), s.sb("h", [D, GT])
        pw, pd, pv, ph = [[s.ps(f"{n}{p}") for p in range(2)] for n in ("pw", "pd", "pv", "ph")]
        loaded = [s.sem(f"loaded{p}") for p in range(2)]
        squared, rooted, selected, spread, weighed, pooled, hsquared, hsummed, hrooted, hscaled, projected, added, chain = [
            s.sem(n) for n in ("squared", "rooted", "selected", "spread", "weighed", "pooled", "hsquared", "hsummed",
                               "hrooted", "hscaled", "projected", "added", "chain")]
        block = ctx.enter_context(nc.Block())
        H = NG // 2

        @block.sync
        def _(sp):
            with sp.Fori(0, H) as i:
                for p in range(2):
                    sp.wait_ge(added, 2 * i + p + 1)
                    sp.dma_start(cx[p][:], ctxd[bass.ds((2 * i + p) * GB, GB), 0:L, :].rearrange("b t c -> t b c")).then_inc(loaded[p], 16)

        @block.scalar
        def _(act):
            nc.scalar.preload_act_table_set("natural_log_exp_and_others")
            with act.Fori(0, H) as i:
                for p in range(2):
                    g = 2 * i + p
                    act.wait_ge(loaded[p], 16 * i + 16)
                    act.wait_ge(added, g + 2)
                    for b in range(GB):
                        nc.scalar.activation(scr[:], cx[p][:, b, :], ACT.Square, accum_out=ss[:, b:b + 1]).then_inc(squared, 1)
                        act.wait_ge(squared, g * GB + b + 1)
                    nc.scalar.activation(ss[:], ss[:], ACT.Ln, bias=k["eps"][0:L], scale=1.0 / C).then_inc(chain, 1)
                    act.wait_ge(chain, g * 2 + 1)
                    nc.scalar.activation(ss[:], ss[:], ACT.Exp, scale=-0.5).then_inc(rooted, 1)
                    nc.scalar.activation(sq[:], xT[:, bass.ds(g * GT, GT)], ACT.Square).then_inc(hsquared, 1)
                    act.wait_ge(hsummed, g + 1)
                    nc.scalar.activation(rs[:], pv[p][:, 0:GT], ACT.Ln, bias=k["eps"][:]).then_inc(chain, 1)
                    act.wait_ge(chain, g * 2 + 2)
                    nc.scalar.activation(rs[:], rs[:], ACT.Exp, scale=-0.5).then_inc(hrooted, 1)

        @block.vector
        def _(dve):
            dve.sem_inc(added, 2)
            with dve.Fori(0, H) as i:
                for p in range(2):
                    g = 2 * i + p
                    nc.vector.tensor_scalar(sel[:], plug[:, bass.ds(g * GT, GT)], rowid[:], None, ALU.is_equal).then_inc(selected, 1)
                    dve.wait_ge(spread, g + 1)
                    dve.wait_ge(rooted, g + 1)
                    v = lambda x: x.rearrange("t (b u) -> t b u", u=L)
                    nc.vector.tensor_tensor(v(wt[:]), v(pw[p][0:L, 0:GT]), ss[:].unsqueeze(2).to_broadcast([L, GB, L]),
                                            ALU.mult).then_inc(weighed, 1)
                    dve.wait_ge(hrooted, g + 1)
                    x = xT[:, bass.ds(g * GT, GT)]
                    nc.vector.tensor_tensor(h[:], x, rs[:], ALU.mult).then_inc(hscaled, 1)
                    dve.wait_ge(projected, g + 1)
                    nc.vector.scalar_tensor_tensor(out=h[:], in0=ph[p][:, 0:GT], scalar=cols[:, 1:2], in1=x, op0=ALU.add,
                                                   op1=ALU.add).then_inc(pooled, 1)
                    dve.wait_ge(pooled, 2 * g + 2)
                    nc.vector.scalar_tensor_tensor(out=x, in0=pd[p][:, 0:GT], scalar=cols[:, 2:3], in1=h[:], op0=ALU.mult,
                                                   op1=ALU.add).then_inc(added, 1)
                    dve.wait_ge(added, g + 3)

        @block.tensor
        def _(pe):
            with pe.Fori(0, H) as i:
                for p in range(2):
                    g = 2 * i + p
                    pe.wait_ge(added, g + 1)
                    pe.wait_ge(selected, g + 1)
                    nc.tensor.matmul(pw[p][0:L, 0:GT], decay[:], sel[:], start=True, stop=True).then_inc(spread, 1)
                    pe.wait_ge(hsquared, g + 1)
                    nc.tensor.matmul(pv[p][:, 0:GT], k["mean"][:], sq[:], start=True, stop=True).then_inc(hsummed, 1)
                    pe.wait_ge(loaded[p], 16 * i + 16)
                    pe.wait_ge(weighed, g + 1)
                    for b in range(GB):
                        ins = nc.tensor.matmul(pd[p][:, b * L:(b + 1) * L], cx[p][:, b, 0:D], wt[:, b * L:(b + 1) * L],
                                               start=True, stop=True)
                    ins.then_inc(pooled, 1)
                    pe.wait_ge(hscaled, g + 1)
                    nc.tensor.matmul(ph[p][:, 0:GT], winT[:], h[:], start=True, stop=True).then_inc(projected, 1)


def l0_ffn(nc, k, a):
    xT, gw = k["xT"], a["L0_ffn_gate_w"]
    E, F = a["L0_ffn_Wg"].shape[0], a["L0_ffn_Wg"].shape[1]
    FC = F // 128
    CAP = int(L * 2.0 / E)
    BT = 128 // E
    TT = BT * L
    SL = BT * CAP
    EH = E // 2
    HS = EH * CAP
    NT = B // BT
    W8 = L + 4
    assert 8 < CAP <= 12
    with ExitStack() as ctx:
        s = Stage(nc, ctx, "l0f")
        gT = s.sb("gT", [D, E])
        wgT, wuT, wdT = s.sb("wgT", [D, E + 1, F]), s.sb("wuT", [D, E + 1, F]), s.sb("wdT", [128, E + 1, FC, D])
        items = [(gT[:], gw)]
        for e in range(E + 1):
            g_, u_, d_ = (a["L0_ffn_Wg"][e], a["L0_ffn_Wu"][e], a["L0_ffn_Wd"][e]) if e < E else (
                a["L0_ffn_Ws_g"], a["L0_ffn_Ws_u"], a["L0_ffn_Ws_d"])
            for c in range(FC):
                f = slice(c * 128, c * 128 + 128)
                items += [(wgT[:, e, f], g_[f, :]), (wuT[:, e, f], u_[f, :]), (wdT[:, e, c, :], d_[:, f])]
        load_transposed(nc, k, "l0ft", items)
        xs, xtm = s.sb("xs", [D, TT]), s.sb("xtm", [L, BT, D])
        sco, st = s.sb("sco", [L, BT, E]), s.sb("st", [L, 4, BT])
        row, rep, rep2, m8, m8b = s.sb("row", [128, W8]), s.sb("rep", [128, W8]), s.sb("rep2", [128, W8]), s.sb("m8", [128, 8]), s.sb("m8b", [128, 8])
        one, pos = s.sb("one", [128, L]), s.sb("pos", [128, L])
        slot = s.sb("slot", [L, E, CAP])
        oh, ohw = s.sb("oh", [L, BT, E, CAP]), s.sb("ohw", [L, BT, E, CAP])
        posT = s.sb("posT", [L, BT, E])
        xg, eog = s.sb("xg", [D, E, BT, CAP]), s.sb("eog", [D, BT, E * CAP])
        act_g, hh = [s.sb(f"ag{p}", [128, FC, TT // 2]) for p in range(2)], [s.sb(f"hh{p}", [128, FC, TT // 2]) for p in range(2)]
        eoS, owS = [s.sb(f"eoS{p}", [HS, 2, D]) for p in range(2)], [s.sb(f"owS{p}", [HS, 2, L]) for p in range(2)]
        pt = [s.ps(f"pt{p}") for p in range(2)]
        pg, pu, pa = [s.ps(f"pg{p}") for p in range(2)], [s.ps(f"pu{p}") for p in range(2)], [s.ps(f"pa{p}") for p in range(2)]
        names = ("staged", "turned", "tcopied", "scored", "smaxed", "exped", "weighted", "rowed", "rowcopied", "posed",
                 "posturned", "hot", "gathered", "gcopied", "gated", "upped", "geluted", "multiplied", "downed", "ecopied",
                 "slotted", "scopied", "scattered", "added")
        q = {n: s.sem(n) for n in names}
        vch, m = s.sem("vch"), s.sem("m")
        steps = [(e, SL) for e in range(E)] + [(E, TT // 2), (E, TT // 2)]
        NS = len(steps)
        block = ctx.enter_context(nc.Block())

        def moving(n):
            return xg[:, n].rearrange("d b c -> d (b c)") if n < E else xs[:, (n - E) * (TT // 2):(n - E + 1) * (TT // 2)]

        @block.gpsimd
        def _(pool):
            nc.gpsimd.memset(one[:], 1.0)
            for j in range(4):
                nc.gpsimd.memset(row[:, L + j:L + j + 1], -2.0 - j)
                nc.gpsimd.memset(m8b[:, 4 + j:5 + j], -2.0 - j)
            nc.gpsimd.iota(slot[:], pattern=[[0, E], [1, CAP]], base=1, channel_multiplier=0,
                           allow_small_or_imprecise_dtypes=True).then_inc(m, 1)

        @block.tensor
        def _(pe):
            with pe.Fori(0, NT) as i:
                pe.wait_ge(q["staged"], i + 1)
                for b in range(BT):
                    n = i * BT + b
                    if b >= 2:
                        pe.wait_ge(q["tcopied"], n - 1)
                    nc.tensor.transpose(pt[b % 2][0:L, 0:D], xs[:, b * L:(b + 1) * L], k["ident"][:]).then_inc(q["turned"], 1)
                pe.wait_ge(q["tcopied"], i * BT + BT)
                for b in range(BT):
                    ins = nc.tensor.matmul(pt[0][0:L, b * E:(b + 1) * E], xs[:, b * L:(b + 1) * L], gT[:], start=True, stop=True)
                ins.then_inc(q["scored"], 1)
                pe.wait_ge(q["weighted"], i + 1)
                nc.tensor.transpose(pt[1][:, 0:L], sco[:].rearrange("t b e -> t (b e)"), k["ident"][0:L, 0:L]).then_inc(q["rowed"], 1)
                pe.wait_ge(q["posed"], i + 1)
                nc.tensor.transpose(pt[0][0:L, 0:128], pos[:], k["ident"][:]).then_inc(q["posturned"], 1)
                pe.wait_ge(q["hot"], i + 1)
                for b in range(BT):
                    n = i * BT + b
                    if b >= 2:
                        pe.wait_ge(q["gcopied"], n - 1)
                    nc.tensor.matmul(pt[b % 2][:, 0:E * CAP], xtm[:, b, :], oh[:, b].rearrange("t e c -> t (e c)"),
                                     start=True, stop=True).then_inc(q["gathered"], 1)
                pe.wait_ge(q["gcopied"], i * BT + BT)

                def down(n):
                    e, w = steps[n]
                    pe.wait_ge(q["multiplied"], i * NS + n + 1)
                    if n >= 2:
                        pe.wait_ge(q["ecopied"], i * E + min(n - 1, E))
                    for c in range(FC):
                        ins = nc.tensor.matmul(pa[n % 2][:, 0:w], wdT[:, e, c, :], hh[n % 2][:, c, 0:w],
                                               start=(c == 0), stop=(c == FC - 1 and n < E), skip_group_check=True)
                    ins.then_inc(q["downed"], 1)
                for n, (e, w) in enumerate(steps):
                    for c in range(FC):
                        o, f = c * (512 // FC), slice(c * 128, c * 128 + 128)
                        if w > 512 // FC:
                            if n > E or c == 0:
                                pe.wait_ge(q["multiplied"], i * NS + n)
                            nc.tensor.matmul(pg[c][:, 0:w], wgT[:, e, f], moving(n), start=True, stop=True).then_inc(q["gated"], 1)
                            nc.tensor.matmul(pu[c][:, 0:w], wuT[:, e, f], moving(n), start=True, stop=True).then_inc(q["upped"], 1)
                        else:
                            if n >= 2 and c == 0:
                                pe.wait_ge(q["multiplied"], i * NS + n - 1)
                            nc.tensor.matmul(pg[n % 2][:, o:o + w], wgT[:, e, f], moving(n), start=True, stop=True).then_inc(q["gated"], 1)
                            nc.tensor.matmul(pu[n % 2][:, o:o + w], wuT[:, e, f], moving(n), start=True, stop=True).then_inc(q["upped"], 1)
                    if n >= 1 and n < E + 1:
                        down(n - 1)
                down(E)
                down(E + 1)
                for b in range(BT):
                    n = i * BT + b
                    if b >= 2:
                        pe.wait_ge(q["scopied"], n - 1)
                    for h in range(2):
                        nc.tensor.transpose(pt[b % 2][0:HS, h * D:(h + 1) * D],
                                            eog[:, b, h * HS:(h + 1) * HS],
                                            k["ident"][:])
                    for h in range(2):
                        ins = nc.tensor.transpose(pt[b % 2][0:HS, 2 * D + h * L:2 * D + (h + 1) * L],
                                                  ohw[:, b, h * EH:(h + 1) * EH].rearrange("t e c -> t (e c)"), k["ident"][0:L, 0:L])
                    ins.then_inc(q["slotted"], 1)
                    pe.wait_ge(q["scopied"], n + 1)
                    dst = pa[b // (BT // 2)][:, b % (BT // 2) * L:(b % (BT // 2) + 1) * L]
                    for h in range(2):
                        ins = nc.tensor.matmul(dst, eoS[b % 2][:, h, :], owS[b % 2][:, h, :], start=False, stop=(h == 1),
                                               skip_group_check=True)
                    ins.then_inc(q["scattered"], 1)

        @block.scalar
        def _(act):
            with act.Fori(0, NT) as i:
                for b in range(BT):
                    n = i * BT + b
                    act.wait_ge(q["turned"], n + 1)
                    nc.scalar.activation(xtm[:, b, :], pt[b % 2][0:L, 0:D], ACT.Copy).then_inc(q["tcopied"], 1)
                act.wait_ge(q["smaxed"], i + 1)
                nc.scalar.activation(sco[:], sco[:], ACT.Exp).then_inc(q["exped"], 1)
                for b in range(BT):
                    n = i * BT + b
                    act.wait_ge(q["gathered"], n + 1)
                    nc.scalar.activation(xg[:, :, b, :], pt[b % 2][:, 0:E * CAP].rearrange("d (e c) -> d e c", c=CAP),
                                         ACT.Copy).then_inc(q["gcopied"], 1)
                for n, (e, w) in enumerate(steps):
                    act.wait_ge(q["gated"], (i * NS + n + 1) * FC)
                    if n >= 2:
                        act.wait_ge(q["multiplied"], i * NS + n - 1)
                    if w > 512 // FC:
                        for c in range(FC):
                            ins = nc.scalar.activation(act_g[n % 2][:, c, 0:w], pg[c][:, 0:w], ACT.Gelu)
                    else:
                        ins = nc.scalar.activation(act_g[n % 2][:, :, 0:w],
                                                   pg[n % 2][:].rearrange("f (c s) -> f c s", c=FC)[:, :, 0:w], ACT.Gelu)
                    ins.then_inc(q["geluted"], 1)
                for b in range(BT):
                    n = i * BT + b
                    act.wait_ge(q["slotted"], n + 1)
                    if b >= 2:
                        act.wait_ge(q["scattered"], n - 1)
                    nc.scalar.activation(eoS[b % 2][:].rearrange("s h d -> s (h d)"), pt[b % 2][0:HS, 0:2 * D], ACT.Copy)
                    nc.scalar.activation(owS[b % 2][:].rearrange("s h t -> s (h t)"), pt[b % 2][0:HS, 2 * D:2 * D + 2 * L],
                                         ACT.Copy).then_inc(q["scopied"], 1)

        held = s.sem("held")

        @block.vector
        def _(dve):
            dve.wait_ge(m, 1)
            CH = 11
            with dve.Fori(0, NT) as i:
                at = [0]

                def link(ins):
                    at[0] += 1
                    ins.then_inc(vch, 1)
                    dve.wait_ge(vch, i * CH + at[0])
                bc = lambda n: st[:, n, :].unsqueeze(2).to_broadcast([L, BT, E])
                logit = pt[0][0:L, 0:128].rearrange("t (b e) -> t b e", e=E)
                nc.vector.tensor_copy(xs[:], xT[:, bass.ds(i * TT, TT)]).then_inc(q["staged"], 1)
                dve.wait_ge(q["scored"], i + 1)
                link(nc.vector.tensor_reduce(st[:, 0, :], logit, AX, ALU.max))
                nc.vector.tensor_tensor(sco[:], logit, bc(0), ALU.subtract).then_inc(q["smaxed"], 1)
                dve.wait_ge(q["exped"], i + 1)
                link(nc.vector.tensor_reduce(st[:, 1, :], sco[:], AX, ALU.add))
                link(nc.vector.reciprocal(st[:, 2, :], st[:, 1, :]))
                nc.vector.tensor_tensor(sco[:], sco[:], bc(2), ALU.mult).then_inc(q["weighted"], 1)
                dve.wait_ge(q["rowed"], i + 1)
                link(nc.vector.tensor_copy(row[:, 0:L], pt[1][:, 0:L]))
                dve.sem_inc(held, 1)
                link(nc.vector.max(m8[:], row[:]))
                dve.sem_inc(held, 1)
                link(nc.vector.match_replace(rep[:], m8[:], row[:], -1.0))
                dve.sem_inc(held, 1)
                link(nc.vector.max(m8[:], rep[:]))
                link(nc.vector.tensor_copy(m8b[:, 0:CAP - 8], m8[:, 0:CAP - 8]))
                dve.sem_inc(held, 1)
                link(nc.vector.match_replace(rep2[:], m8b[:], rep[:], -1.0))
                link(nc.vector.tensor_scalar(rep2[:, 0:L], rep2[:, 0:L], -1.0, None, ALU.is_equal))
                link(nc.vector.tensor_tensor_scan(pos[:], one[:], rep2[:, 0:L], 0.0, ALU.mult, ALU.add))
                nc.vector.tensor_tensor(pos[:], pos[:], rep2[:, 0:L], ALU.mult).then_inc(q["posed"], 1)
                dve.wait_ge(q["posturned"], i + 1)
                nc.vector.tensor_copy(posT[:].rearrange("t b e -> t (b e)"), pt[0][0:L, 0:128]).then_inc(q["rowcopied"], 1)
                dve.wait_ge(q["rowcopied"], i + 1)
                for b in range(BT):
                    ins = nc.vector.tensor_tensor(oh[:, b], posT[:, b, :].unsqueeze(2).to_broadcast([L, E, CAP]), slot[:], ALU.is_equal)
                ins.then_inc(q["hot"], 1)
                dve.wait_ge(q["hot"], i + 1)
                for b in range(BT):
                    nc.vector.tensor_tensor(ohw[:, b], oh[:, b], sco[:, b, :].unsqueeze(2).to_broadcast([L, E, CAP]), ALU.mult)

                def take(n):
                    dve.wait_ge(q["downed"], i * NS + n + 1)
                    dst = eog[:].rearrange("d b (e c) -> d e b c", c=CAP)[:, n]
                    nc.vector.tensor_copy(dst, pa[n % 2][:, 0:SL].rearrange("d (b c) -> d b c", c=CAP)).then_inc(q["ecopied"], 1)
                for n, (e, w) in enumerate(steps):
                    dve.wait_ge(q["geluted"], i * NS + n + 1)
                    dve.wait_ge(q["upped"], (i * NS + n + 1) * FC)
                    if n >= 2:
                        dve.wait_ge(q["downed"], i * NS + n - 1)
                    if w > 512 // FC:
                        for c in range(FC):
                            ins = nc.vector.tensor_tensor(hh[n % 2][:, c, 0:w], act_g[n % 2][:, c, 0:w], pu[c][:, 0:w], ALU.mult)
                    else:
                        ins = nc.vector.tensor_tensor(hh[n % 2][:, :, 0:w], act_g[n % 2][:, :, 0:w],
                                                      pu[n % 2][:].rearrange("f (c s) -> f c s", c=FC)[:, :, 0:w], ALU.mult)
                    ins.then_inc(q["multiplied"], 1)
                    if 1 <= n <= E:
                        take(n - 1)
                dve.wait_ge(q["scattered"], i * BT + BT)
                x = xT[:, bass.ds(i * TT, TT)].rearrange("d (h t) -> d h t", h=2)
                xh = xs[:].rearrange("d (h t) -> d h t", h=2)
                for h in range(2):
                    ins = nc.vector.tensor_tensor(x[:, h], xh[:, h], pa[h][:, 0:TT // 2], ALU.add)
                ins.then_inc(q["added"], 1)
                dve.wait_ge(q["added"], i + 1)
                assert at[0] == CH, at[0]


MAGIC = 1.5 * 2.0 ** 23


def l2_ffn(nc, k, a):
    xT = k["xT"]
    F = a["L2_ffn_w1"].shape[0]
    C = F // 128
    with ExitStack() as ctx:
        s = Stage(nc, ctx, "l2f")
        w1, w2, b1, b2 = s.sb("w1", [128, C, D]), s.sb("w2", [128, C, 128]), s.sb("b1", [128, C]), s.sb("b2", [D, 1])
        load(nc, "l2fl", [(w1[:], a["L2_ffn_w1"].rearrange("(c f) d -> f c d", f=128)),
                          (w2[:], a["L2_ffn_w2"].rearrange("d (c f) -> d c f", f=128)),
                          (b1[:], a["L2_ffn_b1"].rearrange("(c f) -> f c", f=128)), (b2[:], col(a["L2_ffn_b2"]))])
        w1q, w2q = s.sb("w1q", [128, C, D], BF16), s.sb("w2q", [128, C, 128], BF16)
        w1t, w2t = s.sb("w1t", [D, C, 128], BF16), s.sb("w2t", [128, C, D], BF16)
        identb, absw = s.sb("identb", [128, 128], BF16), s.sb("absw", [128, C, 128])
        sw, rsw = s.sb("sw", [128, C + 1]), s.sb("rsw", [128, C + 1])
        top, tall, sx, rsx = s.sb("top", [128, NG + 1]), s.sb("tall", [128, 2]), s.sb("sx", [128, 2]), s.sb("rsx", [128, 2])
        sb1, rb1, bq1 = s.sb("sb1", [128, C]), s.sb("rb1", [128, C]), s.sb("bq1", [128, C])
        sb2, rb2, bq2 = s.sb("sb2", [128, 1]), s.sb("rb2", [128, 1]), s.sb("bq2", [128, 1])
        h = s.sb("h", [128, C, N])
        xr, xq, magic = s.sb("xr", [D, GT]), s.sb("xq", [D, GT], BF16), s.sb("magic", [128, 1])
        hr, hq = [s.sb(f"hr{p}", [128, C, GT]) for p in range(2)], [s.sb(f"hq{p}", [128, C, GT], BF16) for p in range(2)]
        pq = s.ps("pq", (128, 1024), BF16)
        ph = s.ps("ph", (128, 2048))
        po = [s.ps(f"po{p}") for p in range(2)]
        v, weighed, turned, topped, maxed = [s.sem(x) for x in ("v", "weighed", "turned", "topped", "maxed")]
        with nc.Block() as block:
            @block.vector
            def _(dve):
                at = [0]

                def link(ins):
                    at[0] += 1
                    ins.then_inc(v, 1)
                    dve.wait_ge(v, at[0])
                def integers(dst, src, tmp):
                    link(nc.vector.tensor_scalar(tmp, src, MAGIC, MAGIC - 128, ALU.add, ALU.max))
                    link(nc.vector.tensor_scalar(dst, tmp, MAGIC + 127, MAGIC, ALU.min, ALU.subtract))
                nc.vector.memset(magic[:], MAGIC)
                nc.vector.tensor_copy(identb[:], k["ident"][:])
                nc.vector.reduce_max(top[:, 0:1], xT[:], AX).then_inc(topped, 1)
                link(nc.vector.scalar_tensor_tensor(out=absw[:], in0=w1[:], scalar=-1.0, in1=w1[:], op0=ALU.mult, op1=ALU.max))
                link(nc.vector.tensor_reduce(sw[:, 0:C], absw[:], AX, ALU.max))
                link(nc.vector.scalar_tensor_tensor(out=absw[:], in0=w2[:], scalar=-1.0, in1=w2[:], op0=ALU.mult, op1=ALU.max))
                link(nc.vector.reduce_max(sw[:, C:C + 1], absw[:].rearrange("d c f -> d (c f)"), AX))
                link(nc.vector.tensor_scalar(sw[:], sw[:], 1e-8, 1.0 / 127.0, ALU.max, ALU.mult))
                link(nc.vector.reciprocal(rsw[:], sw[:]))
                link(nc.vector.tensor_tensor(absw[:], w1[:], rsw[:, 0:C].unsqueeze(2).to_broadcast([128, C, D]), ALU.mult))
                integers(w1q[:], absw[:], absw[:])
                link(nc.vector.tensor_scalar(absw[:], w2[:], rsw[:, C:C + 1], None, ALU.mult))
                integers(w2q[:], absw[:], absw[:])
                dve.sem_inc(weighed, 1)
                dve.wait_ge(turned, 1)
                dve.wait_ge(maxed, 1)
                pv = pq[:].rearrange("p (n d) -> p n d", d=128)
                nc.vector.tensor_copy(w1t[:], pv[:, 0:C])
                nc.vector.tensor_copy(w2t[:], pv[:, C:2 * C])
                link(nc.vector.tensor_scalar(sx[:, 0:1], tall[:, 0:1], 1e-8, 1.0 / 255.0, ALU.max, ALU.mult))
                link(nc.vector.reciprocal(rsx[:, 0:1], sx[:, 0:1]))
                link(nc.vector.tensor_scalar(sb1[:], sw[:, 0:C], sx[:, 0:1], None, ALU.mult))
                link(nc.vector.reciprocal(rb1[:], sb1[:]))
                link(nc.vector.tensor_tensor(bq1[:], b1[:], rb1[:], ALU.mult))
                link(nc.vector.tensor_scalar(bq1[:], bq1[:], MAGIC, MAGIC, ALU.add, ALU.subtract))
                link(nc.vector.tensor_tensor(bq1[:], bq1[:], sb1[:], ALU.mult))

            @block.tensor
            def _(pe):
                pe.wait_ge(weighed, 1)
                for c in range(C):
                    nc.tensor.transpose(pq[:, c * 128:c * 128 + 128], w1q[:, c, :], identb[:])
                for c in range(C):
                    ins = nc.tensor.transpose(pq[:, (C + c) * 128:(C + c + 1) * 128], w2q[:, c, :], identb[:])
                ins.then_inc(turned, 1)

            @block.gpsimd
            def _(pool):
                pool.wait_ge(topped, 1)
                nc.gpsimd.partition_all_reduce(tall[:, 0:1], top[:, 0:1], 128, bass.bass_isa.ReduceOp.max).then_inc(maxed, 1)

        rounded, clamped, ready, producted, relued = [s.sem(n) for n in ("rounded", "clamped", "ready", "producted", "relued")]
        with nc.Block() as block:
            @block.scalar
            def _(act):
                with act.Fori(0, NG) as i:
                    act.wait_ge(ready, i + 1)
                    nc.scalar.activation(xr[:], xT[:, bass.ds(i * GT, GT)], ACT.Identity, bias=magic[:],
                                         scale=rsx[:, 0:1]).then_inc(rounded, 1)
                    for c in range(C):
                        act.wait_ge(producted, i * C + c + 1)
                        nc.scalar.activation(h[:, c, bass.ds(i * GT, GT)], ph[:, c * 512:c * 512 + GT], ACT.Relu,
                                             bias=bq1[:, c:c + 1], scale=sb1[:, c:c + 1]).then_inc(relued, 1)

            @block.vector
            def _(dve):
                dve.sem_inc(ready, 1)
                with dve.Fori(0, NG) as i:
                    dve.wait_ge(rounded, i + 1)
                    nc.vector.tensor_scalar(xr[:], xr[:], MAGIC, MAGIC + 255, ALU.max, ALU.min).then_inc(clamped, 1)
                    dve.wait_ge(clamped, i + 1)
                    nc.vector.tensor_scalar(xq[:], xr[:], MAGIC, None, ALU.subtract).then_inc(ready, 1)
                    dve.wait_ge(relued, (i + 1) * C)
                    nc.vector.tensor_reduce(top[:, bass.ds(i + 1, 1)], h[:, :, bass.ds(i * GT, GT)], mybir.AxisListType.XY, ALU.max)

            @block.tensor
            def _(pe):
                with pe.Fori(0, NG) as i:
                    pe.wait_ge(ready, i + 2)
                    for c in range(C):
                        nc.tensor.matmul(ph[:, c * 512:c * 512 + GT], w1t[:, c, :], xq[:], start=True,
                                         stop=True).then_inc(producted, 1)

        n = s.sem("n")
        with nc.Block() as block:
            @block.vector
            def _(dve):
                at = [0]

                def link(ins):
                    at[0] += 1
                    ins.then_inc(n, 1)
                    dve.wait_ge(n, at[0])
                link(nc.vector.reduce_max(top[:, 0:1], top[:, 1:NG + 1], AX))
                dve.wait_ge(n, 2)
                at[0] += 1
                link(nc.vector.tensor_scalar(sx[:, 1:2], tall[:, 1:2], 1e-8, 1.0 / 255.0, ALU.max, ALU.mult))
                link(nc.vector.reciprocal(rsx[:, 1:2], sx[:, 1:2]))
                link(nc.vector.tensor_tensor(sb2[:], sw[:, C:C + 1], sx[:, 1:2], ALU.mult))
                link(nc.vector.reciprocal(rb2[:], sb2[:]))
                link(nc.vector.tensor_tensor(bq2[:], b2[:], rb2[:], ALU.mult))
                link(nc.vector.tensor_scalar(bq2[:], bq2[:], MAGIC, MAGIC, ALU.add, ALU.subtract))
                link(nc.vector.tensor_tensor(bq2[:], bq2[:], sb2[:], ALU.mult))

            @block.gpsimd
            def _(pool):
                pool.wait_ge(n, 1)
                nc.gpsimd.partition_all_reduce(tall[:, 1:2], top[:, 0:1], 128, bass.bass_isa.ReduceOp.max).then_inc(n, 1)

        hrounded, hclamped, hready, hproducted, scaled, added = [s.sem(x) for x in
            ("hrounded", "hclamped", "hready", "hproducted", "scaled", "added")]
        block = ctx.enter_context(nc.Block())

        @block.scalar
        def _(act):
            with act.Fori(0, NG // 2) as i:
                for p in range(2):
                    g = 2 * i + p
                    act.wait_ge(hready, g + 1)
                    nc.scalar.activation(hr[p][:], h[:, :, bass.ds(g * GT, GT)], ACT.Identity, bias=magic[:],
                                         scale=rsx[:, 1:2]).then_inc(hrounded, 1)

        @block.vector
        def _(dve):
            dve.sem_inc(hready, 2)
            dve.sem_inc(added, 2)
            with dve.Fori(0, NG // 2) as i:
                for p in range(2):
                    g = 2 * i + p
                    dve.wait_ge(hrounded, g + 1)
                    nc.vector.tensor_scalar(hr[p][:], hr[p][:], MAGIC, MAGIC + 255, ALU.max, ALU.min).then_inc(hclamped, 1)
                    dve.wait_ge(hclamped, g + 1)
                    nc.vector.tensor_scalar(hq[p][:], hr[p][:], MAGIC, None, ALU.subtract).then_inc(hready, 1)
                for p in range(2):
                    g = 2 * i + p
                    dve.wait_ge(hproducted, g + 1)
                    x = xT[:, bass.ds(g * GT, GT)]
                    nc.vector.tensor_scalar(xr[:], po[p][:, 0:GT], sb2[:], bq2[:], ALU.mult, ALU.add).then_inc(scaled, 1)
                    dve.wait_ge(scaled, g + 1)
                    nc.vector.tensor_tensor(x, x, xr[:], ALU.add).then_inc(added, 1)
                    dve.wait_ge(added, g + 3)

        @block.tensor
        def _(pe):
            with pe.Fori(0, NG // 2) as i:
                for p in range(2):
                    g = 2 * i + p
                    pe.wait_ge(hready, g + 3)
                    for c in range(C):
                        ins = nc.tensor.matmul(po[p][:, 0:GT], w2t[:, c, :], hq[p][:, c, :], start=(c == 0), stop=(c == C - 1))
                    ins.then_inc(hproducted, 1)


def l3_attn(nc, k, a):
    xT = k["xT"]
    DI, DS, G = 2 * D, a["L3_attn_A_log"].shape[0], 16
    GS = DI // G
    HB, LAG = 4, 3
    HG = 128 // DS
    F = a["L3_attn_W_ffn1"].shape[0]
    FC = F // 128
    R = 1 + 2 * DS
    with ExitStack() as ctx:
        s = Stage(nc, ctx, "l3a")
        winT, wparT = s.sb("winT", [D, 2 * DI]), s.sb("wparT", [128, 2, 2, 3, 128])
        woutT, wf1T, wf2T = s.sb("woutT", [128, 2, D]), s.sb("wf1T", [D, F]), s.sb("wf2T", [128, FC, D])
        cols, alog, bf1 = s.sb("cols", [D, 4]), s.sb("alog", [128, 4]), s.sb("bf1", [128, FC])
        wp = a["L3_attn_W_param"]
        par = s.sb("par", [128, 2, 3, DI])
        wpg = wp.rearrange("(g r) i -> g r i", r=R)
        pairs = [(par[:, h, 1 + kind, :], wpg[h * HG:(h + 1) * HG, 1 + kind * DS:1 + (kind + 1) * DS, :])
                 for h in range(2) for kind in range(2)]
        pairs += [(par[:, h, 0, :], wpg[h * HG:(h + 1) * HG, 0:1, :].to_broadcast([HG, DS, DI])) for h in range(2)]
        pairs += [(cols[:, 0:1], col(a["L3_attn_g1"])), (cols[:, 1:2], col(a["L3_attn_g2"])), (cols[:, 2:3], col(a["L3_attn_b_ffn2"])),
                  (bf1[:], a["L3_attn_b_ffn1"].rearrange("(c f) -> f c", f=128)),
                  (alog[:, 0:1], a["L3_attn_A_log"].rearrange("(o n x) -> o n x", o=1, x=1).to_broadcast([HG, DS, 1]))]
        load(nc, "l3al", pairs)
        blk = lambda name, o, i: a[name][o * 128:(o + 1) * 128, i * 128:(i + 1) * 128]
        load_transposed(nc, k, "l3at", [(winT[:, c * 128:(c + 1) * 128], blk("L3_attn_W_in", c, 0)) for c in range(4)]
                        + [(woutT[:, c, :], blk("L3_attn_W_out", 0, c)) for c in range(2)]
                        + [(wf1T[:, c * 128:(c + 1) * 128], blk("L3_attn_W_ffn1", c, 0)) for c in range(FC)]
                        + [(wf2T[:, c, :], blk("L3_attn_W_ffn2", 0, c)) for c in range(FC)])
        pick, drop = s.sb("pick", [128, GS, 128]), s.sb("drop", [128, GS, 128])
        eps6 = s.sb("eps6", [128, 1])
        m, mv = s.sem("m"), s.sem("mv")
        pt = s.ps("pt", (128, 1536))
        with nc.Block() as block:
            @block.gpsimd
            def _(pool):
                nc.gpsimd.memset(eps6[:], 1e-6)
                nc.gpsimd.memset(pick[:], 1.0)
                nc.gpsimd.memset(drop[:], 1.0).then_inc(m, 1)
                pool.wait_ge(m, 1)
                dv = drop[:].rearrange("p c (g e) -> p c g e", e=GS)
                for c in range(GS):
                    pv = pick[:, c].rearrange("p (g n) -> p g n", n=DS)
                    nc.gpsimd.affine_select(out=pv, in_=pv, compare_op=ALU.is_equal, fill=0.0, base=-c,
                                            pattern=[[-GS, HG], [0, DS]], channel_multiplier=1)
                    ins = nc.gpsimd.affine_select(out=dv[:, c], in_=dv[:, c], compare_op=ALU.is_ge, fill=0.0, base=0,
                                                  pattern=[[-DS, HG], [0, GS]], channel_multiplier=1)
                ins.then_inc(m, 1)
                pool.wait_ge(m, 2)
                for c in range(GS):
                    ins = nc.gpsimd.affine_select(out=dv[:, c], in_=dv[:, c], compare_op=ALU.is_ge, fill=0.0, base=DS - 1,
                                                  pattern=[[DS, HG], [0, GS]], channel_multiplier=-1)
                ins.then_inc(m, 1)
                pool.wait_ge(m, 3)
                for c in range(GS):
                    ins = nc.gpsimd.affine_select(out=dv[:, c], in_=dv[:, c], compare_op=ALU.is_equal, fill=0.0, base=-c,
                                                  pattern=[[0, HG], [1, GS]], channel_multiplier=0)

            @block.tensor
            def _(pe):
                for n in range(12):
                    j, h, kind = n // 6, n // 3 % 2, n % 3
                    ins = nc.tensor.transpose(pt[:, n * 128:(n + 1) * 128], par[:, h, kind, j * 128:(j + 1) * 128], k["ident"][:])
                ins.then_inc(mv, 1)

            @block.scalar
            def _(act):
                nc.scalar.activation(alog[:, 1:2], alog[:, 0:1], ACT.Exp).then_inc(mv, 1)

            @block.vector
            def _(dve):
                nc.vector.tensor_scalar(winT[:], winT[:], cols[:, 0:1], None, ALU.mult)
                nc.vector.tensor_scalar(wf1T[:], wf1T[:], cols[:, 1:2], None, ALU.mult)
                dve.wait_ge(mv, 2)
                nc.vector.tensor_copy(wparT[:].rearrange("i j h z n -> i (j h z n)"), pt[:])
                nc.vector.tensor_scalar(alog[:, 2:3], alog[:, 1:2], -1.0, None, ALU.mult).then_inc(mv, 1)
                dve.wait_ge(mv, 3)
                nc.vector.tensor_scalar(alog[:, 1:2], alog[:, 2:3], 1e-12, None, ALU.add).then_inc(mv, 1)
                dve.wait_ge(mv, 4)
                nc.vector.reciprocal(alog[:, 3:4], alog[:, 1:2])

        pg, pu, py = [[pt[:, 512 * p:512 * p + GT] for p in range(2)], [s.ps(f"pu{p}") for p in range(2)], [s.ps(f"py{p}") for p in range(2)]]
        pn = pt[:, 1024:1024 + GT]
        pw = s.ps("pw")
        sq, r, z, x1 = [s.sb(n, [D, GT]) for n in ("sq", "r", "z", "x1")]
        xz, prm = s.sb("xz", [128, 4, GT]), s.sb("prm", [128, 3, 2, GT])
        sp_, ea, fr, dl = [s.sb(n, [128, 2, GT]) for n in ("sp", "ea", "fr", "dl")]
        bu = [s.sb(f"bu{p}", [128, GT]) for p in range(2)]
        hs, hc = [[s.sb(f"{n}{p}", [128, GT]) for p in range(HB)] for n in ("hs", "hc")]
        ym, hf = s.sb("ym", [128, 2, GT]), s.sb("hf", [128, FC, GT])
        q = {n: s.sem(n) for n in ("squared", "summed", "logged", "rooted", "normed", "inned", "silued", "parmed", "pcopied",
                                   "absed", "soft1", "soft2", "delta", "clipped", "exped", "ready", "picked", "bued",
                                   "scanned", "used", "dropped", "gated", "outed", "x1ed", "ffed", "ffsilued", "ffouted", "added")}
        ch = s.sem("ch")
        NS = 2 * GS
        block = ctx.enter_context(nc.Block())

        @block.tensor
        def _(pe):
            with pe.Fori(0, NG) as i:
                pe.wait_ge(q["squared"], 2 * i + 1)
                nc.tensor.matmul(pn, k["mean"][:], sq[:], start=True, stop=True).then_inc(q["summed"], 1)
                pe.wait_ge(q["normed"], 2 * i + 1)
                for n in range(4):
                    if n >= 2:
                        pe.wait_ge(q["silued"], 4 * i + n - 1)
                    nc.tensor.matmul(pg[n % 2], winT[:, n * 128:(n + 1) * 128], z[:], start=True, stop=True).then_inc(q["inned"], 1)
                pe.wait_ge(q["silued"], 4 * i + 4)
                for n in range(6):
                    kind, h = n // 2, n % 2
                    if n >= 2:
                        pe.wait_ge(q["pcopied"], 6 * i + n - 1)
                    for j in range(2):
                        ins = nc.tensor.matmul(pg[n % 2], wparT[:, j, h, kind, :], xz[:, j, :], start=(j == 0), stop=(j == 1))
                    ins.then_inc(q["parmed"], 1)

                def drop_(n):
                    pe.wait_ge(q["used"], i * NS + n + 1)
                    nc.tensor.matmul(py[n % 2][:, 0:GT], drop[:, n // 2, :], hc[n % HB][:], start=(n < 2),
                                     stop=(n >= NS - 2)).then_inc(q["dropped"], 1)
                for n in range(NS):
                    if n >= 2:
                        pe.wait_ge(q["bued"], i * NS + n - 1)
                    nc.tensor.matmul(pu[n % 2][:, 0:GT], pick[:, n // 2, :], xz[:, n % 2, :], start=True, stop=True).then_inc(q["picked"], 1)
                    if n >= LAG:
                        drop_(n - LAG)
                for n in range(NS - LAG, NS):
                    drop_(n)
                pe.wait_ge(q["gated"], i + 1)
                for h in range(2):
                    ins = nc.tensor.matmul(pw[:, 0:GT], woutT[:, h, :], ym[:, h, :], start=(h == 0), stop=(h == 1))
                ins.then_inc(q["outed"], 1)
                pe.wait_ge(q["squared"], 2 * i + 2)
                nc.tensor.matmul(pn, k["mean"][:], sq[:], start=True, stop=True).then_inc(q["summed"], 1)
                pe.wait_ge(q["normed"], 2 * i + 2)
                for c in range(FC):
                    if c >= 2:
                        pe.wait_ge(q["ffsilued"], FC * i + c - 1)
                    nc.tensor.matmul(pg[c % 2], wf1T[:, c * 128:(c + 1) * 128], z[:], start=True, stop=True).then_inc(q["ffed"], 1)
                for c in range(FC):
                    pe.wait_ge(q["ffsilued"], FC * i + c + 1)
                    ins = nc.tensor.matmul(pw[:, 0:GT], wf2T[:, c, :], hf[:, c, :], start=(c == 0), stop=(c == FC - 1))
                ins.then_inc(q["ffouted"], 1)

        @block.scalar
        def _(act):
            def root(i, src, n):
                nc.scalar.activation(sq[:], src, ACT.Square).then_inc(q["squared"], 1)
                act.wait_ge(q["summed"], 2 * i + n)
                nc.scalar.activation(r[:], pn, ACT.Ln, bias=eps6[:]).then_inc(q["logged"], 1)
                act.wait_ge(q["logged"], 2 * i + n)
                nc.scalar.activation(r[:], r[:], ACT.Exp, scale=-0.5).then_inc(q["rooted"], 1)
            with act.Fori(0, NG) as i:
                nc.scalar.preload_act_table_set("natural_log_exp_and_others")
                act.wait_ge(q["added"], i + 1)
                root(i, xT[:, bass.ds(i * GT, GT)], 1)
                for n in range(4):
                    act.wait_ge(q["inned"], 4 * i + n + 1)
                    nc.scalar.activation(xz[:, n, :], pg[n % 2], ACT.Silu).then_inc(q["silued"], 1)
                nc.scalar.preload_act_table_set("natural_log_exp_and_others")
                for n in range(6):
                    act.wait_ge(q["parmed"], 6 * i + n + 1)
                    nc.scalar.activation(prm[:, n // 2, n % 2, :], pg[n % 2], ACT.Copy).then_inc(q["pcopied"], 1)
                act.wait_ge(q["pcopied"], 6 * i + 2)
                nc.scalar.activation(sp_[:], prm[:, 0], ACT.Abs).then_inc(q["absed"], 1)
                act.wait_ge(q["absed"], i + 1)
                nc.scalar.activation(sp_[:], sp_[:], ACT.Exp, scale=-1.0).then_inc(q["soft1"], 1)
                act.wait_ge(q["soft1"], i + 1)
                nc.scalar.activation(sp_[:], sp_[:], ACT.Ln, bias=1.0).then_inc(q["soft2"], 1)
                act.wait_ge(q["clipped"], i + 1)
                nc.scalar.activation(ea[:], ea[:], ACT.Exp).then_inc(q["exped"], 1)
                act.wait_ge(q["x1ed"], i + 1)
                root(i, x1[:], 2)
                for c in range(FC):
                    act.wait_ge(q["ffed"], FC * i + c + 1)
                    nc.scalar.activation(hf[:, c, :], pg[c % 2], ACT.Silu, bias=bf1[:, c:c + 1]).then_inc(q["ffsilued"], 1)

        @block.gpsimd
        def _(pool):
            with pool.Fori(0, NG) as i:
                for n in range(NS):
                    pool.wait_ge(q["scanned"], i * NS + n + 1)
                    if n >= HB:
                        pool.wait_ge(q["dropped"], i * NS + n - HB + 1)
                    nc.gpsimd.tensor_tensor(hc[n % HB][:], hs[n % HB][:], prm[:, 2, n % 2, :], ALU.mult).then_inc(q["used"], 1)

        @block.vector
        def _(dve):
            dve.sem_inc(q["added"], 1)
            CH = 9
            with dve.Fori(0, NG) as i:
                at = [0]

                def link(ins):
                    at[0] += 1
                    ins.then_inc(ch, 1)
                    dve.wait_ge(ch, i * CH + at[0])
                x = xT[:, bass.ds(i * GT, GT)]
                dve.wait_ge(q["rooted"], 2 * i + 1)
                nc.vector.tensor_tensor(z[:], x, r[:], ALU.mult).then_inc(q["normed"], 1)
                dve.wait_ge(q["soft2"], i + 1)
                dve.wait_ge(q["pcopied"], 6 * i + 6)
                link(nc.vector.scalar_tensor_tensor(out=dl[:], in0=prm[:, 0], scalar=0.0, in1=sp_[:], op0=ALU.max, op1=ALU.add))
                link(nc.vector.tensor_scalar(ea[:], dl[:], alog[:, 2:3], -10.0, ALU.mult, ALU.max))
                nc.vector.tensor_scalar(sp_[:], ea[:], -1e-4, None, ALU.is_gt).then_inc(q["clipped"], 1)
                dve.wait_ge(q["exped"], i + 1)
                link(nc.vector.tensor_scalar(fr[:], ea[:], -1.0, alog[:, 3:4], ALU.add, ALU.mult))
                link(nc.vector.tensor_tensor(dl[:], dl[:], fr[:], ALU.subtract))
                link(nc.vector.tensor_tensor(dl[:], dl[:], sp_[:], ALU.mult))
                link(nc.vector.tensor_tensor(fr[:], fr[:], dl[:], ALU.add))
                link(nc.vector.memset(ea[:].rearrange("p h (b t) -> p h b t", t=L)[:, :, :, 0], 0.0))
                link(nc.vector.tensor_tensor(fr[:], fr[:], prm[:, 1], ALU.mult))

                def bu_(n):
                    dve.wait_ge(q["picked"], i * NS + n + 1)
                    if n >= 2:
                        dve.wait_ge(q["scanned"], i * NS + n - 1)
                    nc.vector.tensor_tensor(bu[n % 2][:], fr[:, n % 2, :], pu[n % 2][:, 0:GT], ALU.mult).then_inc(q["bued"], 1)
                bu_(0)
                for n in range(NS):
                    if n + 1 < NS:
                        bu_(n + 1)
                    dve.wait_ge(q["bued"], i * NS + n + 1)
                    if n >= HB:
                        dve.wait_ge(q["used"], i * NS + n - HB + 1)
                    nc.vector.tensor_tensor_scan(hs[n % HB][:], ea[:, n % 2, :], bu[n % 2][:], 0.0, ALU.mult, ALU.add).then_inc(q["scanned"], 1)
                dve.wait_ge(q["dropped"], (i + 1) * NS)
                for h in range(2):
                    ins = nc.vector.tensor_tensor(ym[:, h, :], py[h][:, 0:GT], xz[:, 2 + h, :], ALU.mult)
                ins.then_inc(q["gated"], 1)
                dve.wait_ge(q["outed"], i + 1)
                nc.vector.tensor_tensor(x1[:], pw[:, 0:GT], x, ALU.add).then_inc(q["x1ed"], 1)
                dve.wait_ge(q["rooted"], 2 * i + 2)
                nc.vector.tensor_tensor(z[:], x1[:], r[:], ALU.mult).then_inc(q["normed"], 1)
                dve.wait_ge(q["x1ed"], i + 1)
                link(nc.vector.tensor_tensor(x1[:], x1[:], x, ALU.add))
                dve.wait_ge(q["ffouted"], i + 1)
                nc.vector.scalar_tensor_tensor(out=x, in0=pw[:, 0:GT], scalar=cols[:, 2:3], in1=x1[:], op0=ALU.add,
                                               op1=ALU.add).then_inc(q["added"], 1)
                dve.wait_ge(q["added"], i + 2)
                assert at[0] == CH, at[0]


def l1_attn(nc, k, a):
    xT = k["xT"]
    NH = a["L1_attn_Wb"].shape[1]
    DK, DV = a["L1_attn_Wq"].shape[1] // NH, a["L1_attn_Wv"].shape[1] // NH
    assert DV == 128 and DK == 64
    C = 16
    KC = NH * DK // 128
    U = 4
    NU = NH // U
    UT, UV = U * L, U * DV
    R2 = 32
    with ExitStack() as ctx:
        s = Stage(nc, ctx, "l1a")
        wqk, wv, wg, wo = s.sb("wqk", [D, 2, NH * DK]), s.sb("wv", [D, NH, DV]), s.sb("wg", [D, NH, DV]), s.sb("wo", [DV, NH, D])
        taps = s.sb("taps", [128, 2 * KC + NH, 4])
        wgb, hb, gnw = s.sb("wgb", [D, 2, NH]), s.sb("hb", [NH, 4]), s.sb("gnw", [DV, 1])
        load(nc, "l1al", [(wqk[:, 0, :], a["L1_attn_Wq"]), (wqk[:, 1, :], a["L1_attn_Wk"]),
                          (wv[:].rearrange("d h v -> d (h v)"), a["L1_attn_Wv"]), (wg[:].rearrange("d h v -> d (h v)"), a["L1_attn_Wg"]),
                          (wo[:], a["L1_attn_Wo"].rearrange("(h v) d -> v h d", v=DV)),
                          (taps[:, 0:KC, :], a["L1_attn_conv_q"].rearrange("(c p) j -> p c j", p=128)),
                          (taps[:, KC:2 * KC, :], a["L1_attn_conv_k"].rearrange("(c p) j -> p c j", p=128)),
                          (taps[:, 2 * KC:, :], a["L1_attn_conv_v"].rearrange("(c p) j -> p c j", p=128)),
                          (wgb[:, 0, :], a["L1_attn_Wgk"]), (wgb[:, 1, :], a["L1_attn_Wb"]),
                          (hb[:, 0:1], col(a["L1_attn_dt_bias"])), (hb[:, 1:2], col(a["L1_attn_b_b"])),
                          (hb[:, 2:3], col(a["L1_attn_A_log"])), (gnw[:], col(a["L1_attn_g_norm_weight"]))])
        upto, within, below = s.sb("upto", [L, U, L]), s.sb("within", [L, U, L]), s.sb("below", [L, U, L])
        inblk, outblk, eyes = s.sb("inblk", [L, U, L]), s.sb("outblk", [L, U, L]), s.sb("eyes", [L, U, L])
        pair, keep, eps6, lnsc = s.sb("pair", [128, 128]), s.sb("keep", [NH, GB, L]), s.sb("eps6", [128, 1]), s.sb("lnsc", [128, 1])
        ind = s.sb("ind", [NH, NH, L])
        lhsA, lhsL = s.sb("lhsA", [R2 + NH, GT]), s.sb("lhsL", [R2 + NH, GT])
        rhsA, rhsT, rhsL = [s.sb(n, [R2 + NH, NH, L]) for n in ("rhsA", "rhsT", "rhsL")]
        m = s.sem("m")
        FAR = -1e30
        with nc.Block() as block:
            @block.gpsimd
            def _(pool):
                aff = nc.gpsimd.affine_select
                steps = [0]

                def link(ins):
                    steps[0] += 1
                    ins.then_inc(m, 1)
                    pool.wait_ge(m, steps[0])
                for t in (upto, within, below):
                    nc.gpsimd.memset(t[:], 0.0)
                for t in (inblk, pair, keep, ind, lhsA, lhsL, rhsA, rhsT, rhsL):
                    nc.gpsimd.memset(t[:], 1.0)
                nc.gpsimd.memset(eps6[:], 1e-6)
                nc.gpsimd.memset(lnsc[:, :], float(np.log(DK ** -0.5)))
                link(nc.gpsimd.memset(eyes[:], 0.0))
                link(aff(out=upto[:], in_=upto[:], compare_op=ALU.is_ge, fill=FAR, base=0, pattern=[[0, U], [1, L]], channel_multiplier=-1))
                link(aff(out=within[:], in_=within[:], compare_op=ALU.is_gt, fill=FAR, base=0, pattern=[[0, U], [1, L]], channel_multiplier=-1))
                link(aff(out=below[:], in_=below[:], compare_op=ALU.is_gt, fill=FAR, base=0, pattern=[[0, U], [-1, L]], channel_multiplier=1))
                link(aff(out=eyes[:], in_=eyes[:], compare_op=ALU.not_equal, fill=1.0, base=0, pattern=[[0, U], [-1, L]], channel_multiplier=1))
                for c0 in range(0, L, C):
                    w = min(C, L - c0)
                    for t, fill in ((within, FAR), (inblk, 0.0)):
                        v = t[:, :, c0:c0 + w]
                        link(aff(out=v, in_=v, compare_op=ALU.is_ge, fill=fill, base=-c0, pattern=[[0, U], [0, w]], channel_multiplier=1))
                        link(aff(out=v, in_=v, compare_op=ALU.is_ge, fill=fill, base=c0 + w - 1, pattern=[[0, U], [0, w]], channel_multiplier=-1))
                link(nc.gpsimd.tensor_scalar(outblk[:], inblk[:], -1.0, 1.0, ALU.mult, ALU.add))
                pv = pair[:].rearrange("p (g e) -> p g e", e=DK)
                link(aff(out=pv, in_=pv, compare_op=ALU.is_ge, fill=0.0, base=0, pattern=[[-DK, 2], [0, DK]], channel_multiplier=1))
                link(aff(out=pv, in_=pv, compare_op=ALU.is_ge, fill=0.0, base=DK - 1, pattern=[[DK, 2], [0, DK]], channel_multiplier=-1))
                link(nc.gpsimd.memset(keep[:, :, 0:1], 0.0))
                link(aff(out=ind[:], in_=ind[:], compare_op=ALU.is_equal, fill=0.0, base=0, pattern=[[-1, NH], [0, L]], channel_multiplier=1))
                for t in (lhsA, lhsL):
                    link(aff(out=t[0:R2], in_=t[0:R2], compare_op=ALU.is_ge, fill=0.0, base=NH - 1, pattern=[[0, GT]], channel_multiplier=-1))
                for t in (rhsA, rhsT, rhsL):
                    link(aff(out=t[0:R2], in_=t[0:R2], compare_op=ALU.is_equal, fill=0.0, base=0, pattern=[[-1, NH], [0, L]], channel_multiplier=1))

            sc = s.sem("sc")

            @block.scalar
            def _(act):
                nc.scalar.preload_act_table_set("natural_log_exp_and_others")
                nc.scalar.activation(hb[:, 3:4], hb[:, 2:3], ACT.Exp).then_inc(sc, 1)

            @block.vector
            def _(dve):
                dve.wait_ge(sc, 1)
                nc.vector.tensor_scalar(hb[:, 3:4], hb[:, 3:4], -1.0, None, ALU.mult)

        banks = [s.ps(f"bank{n}") for n in range(8)]
        NB = len(banks)
        qk, v = s.sb("qk", [128, 2 * KC, GT]), s.sb("v", [128, NH, GT])
        half = s.sb("half", [128, 2, KC, 2, GT])
        sg = qk
        sq, rt = [s.sb(f"sq{p}", [128, GT]) for p in range(2)], [s.sb(f"rt{p}", [128, GT]) for p in range(2)]
        raw, spl, spt = s.sb("raw", [NH, 2, GT]), s.sb("spl", [NH, 2, GT]), s.sb("spt", [NH, 2, GT])
        G, Gb, beta, betaT = s.sb("G", [NH, GT]), s.sb("Gb", [NH, GT]), s.sb("beta", [NH, GT]), s.sb("betaT", [L, GB, NH])
        buf = [{n: s.sb(f"{n}{u}", [L, UT]) for n in ("AT", "b1", "b2", "b3", "b4", "b5", "R")} for u in range(NU)]
        Z = [s.sb(f"Z{u}", [L, UV]) for u in range(NU)]
        NQ = 2 * KC + NH
        front = {n: s.sem(n) for n in ("projected", "tapped", "convolved", "silued", "squared", "summed", "logged", "rooted",
                                       "normed", "halved", "smalls", "biased", "absed", "soft1", "soft2", "soft", "gked", "summedG",
                                       "betaed", "turned", "ready", "rows", "argued", "gated",
                                       "osquared", "osummed", "ologged", "orooted", "oscaled", "ogated", "projO", "added")}
        PE_ = ["argA", "argT", "argL", "kk", "qk", "vT", "M2T", "M2", "R2", "M4T", "M4", "R3", "M8", "R4", "N", "NT", "Z", "Z1",
               "N2T", "N2", "Z2", "N4T", "Z3", "O"]
        DVE_ = ["minA", "minT", "minL", "MT", "M", "AT", "X", "R1", "R2", "R3", "R4", "Z1", "Z2", "Z3"]
        ACT_ = ["expA", "expT", "expL", "M2T", "M2", "M4T", "M4", "M8", "N", "NT", "Z", "N2T", "N2", "N4T", "O"]
        POOL_ = ["Md", "Mo"]
        reader = {"argA": "minA", "argT": "minT", "argL": "minL", "kk": "M", "qk": "AT", "vT": "X", "R2": "R2", "R3": "R3",
                  "R4": "R4", "Z1": "Z1", "Z2": "Z2", "Z3": "Z3"}
        pe_done, dve_done, act_done, pool_done = [[s.sem(f"{n}{u}") for u in range(NU)] for n in ("pe_done", "dve_done", "act_done", "pool_done")]
        held = s.sem("held")
        block = ctx.enter_context(nc.Block())

        def at(i, b, order, step):
            return (i * GB + b) * len(order) + order.index(step) + 1

        def shape(ap):
            return ap.rearrange("p (b t) -> p b t", t=L)

        @block.tensor
        def _(pe):
            with pe.Fori(0, NG) as i:
                x = xT[:, bass.ds(i * GT, GT)]
                pe.wait_ge(front["added"], i + 1)
                for n in range(NQ):
                    if n >= NB:
                        pe.wait_ge(front["convolved"], i * NQ + n - NB + 1)
                    w = wqk[:, n // KC, n % KC * 128:(n % KC + 1) * 128] if n < 2 * KC else wv[:, n - 2 * KC, :]
                    nc.tensor.matmul(banks[n % NB][:, 0:GT], w, x, start=True, stop=True).then_inc(front["projected"], 1)
                for n in range(2):
                    pe.wait_ge(front["convolved"], i * NQ + NQ - NB + n + 1)
                    pe.sem_inc(held, 1)
                    nc.tensor.matmul(banks[(NQ + n) % NB][0:NH, 0:GT], wgb[:, n, :], x, start=True, stop=True).then_inc(front["smalls"], 1)
                pe.wait_ge(front["convolved"], i * NQ + NQ)
                for n in range(2 * KC):
                    bk = (NQ + 2 + n) % NB
                    pe.wait_ge(front["squared"], i * 2 * KC + n + 1)
                    if n >= NB - 2:
                        pe.wait_ge(front["biased"], i + 1)
                    if n >= NB:
                        pe.wait_ge(front["logged"], i * 2 * KC + n - NB + 1)
                    nc.tensor.matmul(banks[bk][:, 0:GT], pair[:], sq[n % 2][:], start=True, stop=True).then_inc(front["summed"], 1)
                pe.wait_ge(front["betaed"], i + 1)
                pe.wait_ge(front["normed"], (i + 1) * 2 * KC)
                pe.sem_inc(held, 1)
                for b in range(GB):
                    ins = nc.tensor.transpose(banks[0][0:L, b * NH:(b + 1) * NH], beta[:, b * L:(b + 1) * L], k["ident"][0:NH, 0:NH])
                ins.then_inc(front["turned"], 1)
                pe.wait_ge(front["ready"], i + 1)
                for b in range(GB):
                    pe.wait_ge(front["rows"], i * GB + b + 1)
                    for j, step in enumerate(PE_):
                        for u in range(NU):
                            seq = (b * len(PE_) + j) * NU + u
                            bk = banks[seq % NB]
                            if seq >= NB:
                                b0, j0, u0 = (seq - NB) // NU // len(PE_), (seq - NB) // NU % len(PE_), (seq - NB) % NU
                                last = PE_[j0]
                                if last in reader:
                                    pe.wait_ge(dve_done[u0], at(i, b0, DVE_, reader[last]))
                                else:
                                    pe.wait_ge(act_done[u0], at(i, b0, ACT_, last))
                            B = buf[u]
                            dve = lambda what: pe.wait_ge(dve_done[u], at(i, b, DVE_, what))
                            act = lambda what: pe.wait_ge(act_done[u], at(i, b, ACT_, what))
                            pool = lambda what: pe.wait_ge(pool_done[u], at(i, b, POOL_, what))
                            tb = slice(b * L, (b + 1) * L)

                            def heads(lhs, rhs, w=L, width=L, rows=L):
                                for h in range(U):
                                    ins = nc.tensor.matmul(bk[0:rows, h * width:h * width + w], lhs(h), rhs(h), start=True, stop=True)
                                return ins
                            sl = lambda t: (lambda h: t[:, h * L:(h + 1) * L])
                            sv = lambda t: (lambda h: t[:, h * DV:(h + 1) * DV])
                            if step in ("argA", "argT", "argL"):
                                lhs, rhs = {"argA": (lhsA, rhsA), "argT": (lhsA, rhsT), "argL": (lhsL, rhsL)}[step]
                                ins = nc.tensor.matmul(bk[0:L, 0:UT], lhs[:, tb], rhs[:, u * U:(u + 1) * U, :].rearrange("r h t -> r (h t)"),
                                                       start=True, stop=True)
                            elif step in ("kk", "qk"):
                                ins = heads(lambda h: half[:, 1, (u * U + h) // 2, (u * U + h) % 2, tb],
                                            lambda h: half[:, int(step == "kk"), (u * U + h) // 2, (u * U + h) % 2, tb])
                            elif step == "vT":
                                for h in range(U):
                                    ins = nc.tensor.transpose(bk[0:L, h * DV:(h + 1) * DV], v[:, u * U + h, tb], k["ident"][:])
                            elif step == "M2T":
                                dve("MT"), pool("Md")
                                ins = heads(sl(B["b3"]), sl(B["b1"]))
                            elif step == "M2":
                                ins = heads(sl(B["b1"]), sl(B["b3"]))
                            elif step == "R2":
                                dve("R1"), act("M2")
                                ins = heads(sl(B["b5"]), sl(B["R"]))
                            elif step == "M4T":
                                act("M2T")
                                ins = heads(sl(B["b5"]), sl(B["b4"]))
                            elif step == "M4":
                                ins = heads(sl(B["b4"]), sl(B["b5"]))
                            elif step == "R3":
                                dve("R2"), act("M4")
                                ins = heads(sl(B["b3"]), sl(B["R"]))
                            elif step == "M8":
                                act("M4T")
                                ins = heads(sl(B["b1"]), sl(B["b3"]))
                            elif step == "R4":
                                dve("R3"), act("M8")
                                ins = heads(sl(B["b4"]), sl(B["R"]))
                            elif step == "N":
                                dve("R4"), pool("Mo")
                                ins = heads(sl(B["R"]), sl(B["b2"]))
                            elif step == "NT":
                                ins = heads(sl(B["b2"]), sl(B["R"]))
                            elif step == "Z":
                                dve("X")
                                ins = heads(sl(B["R"]), sv(Z[u]), DV, DV)
                            elif step == "Z1":
                                act("Z")
                                ins = heads(sl(B["b1"]), sv(Z[u]), DV, DV)
                            elif step == "N2T":
                                act("N")
                                ins = heads(sl(B["b5"]), sl(B["b1"]))
                            elif step == "N2":
                                ins = heads(sl(B["b1"]), sl(B["b5"]))
                            elif step == "Z2":
                                dve("Z1"), act("N2T")
                                ins = heads(sl(B["b3"]), sv(Z[u]), DV, DV)
                            elif step == "N4T":
                                act("N2")
                                ins = heads(sl(B["b4"]), sl(B["b3"]))
                            elif step == "Z3":
                                dve("Z2"), act("N4T")
                                ins = heads(sl(B["b2"]), sv(Z[u]), DV, DV)
                            elif step == "O":
                                dve("Z3")
                                ins = heads(sv(Z[u]), sl(B["AT"]), rows=DV)
                            ins.then_inc(pe_done[u], 1)
                for u in range(NU):
                    pe.wait_ge(act_done[u], at(i, GB - 1, ACT_, "O"))
                for h in range(NH):
                    if h >= 4:
                        pe.wait_ge(front["gated"], i * NH + h - 3)
                    nc.tensor.matmul(banks[2 + h % 4][:, 0:GT], wg[:, h, :], x, start=True, stop=True).then_inc(front["projected"], 1)
                for h in range(NH + 1):
                    if h < NH:
                        pe.wait_ge(front["osquared"], i * NH + h + 1)
                        nc.tensor.matmul(banks[h % 2][:, 0:GT], k["mean"][:], sq[h % 2][:], start=True, stop=True).then_inc(front["osummed"], 1)
                    if h >= 1:
                        pe.wait_ge(front["ogated"], i * NH + h)
                        nc.tensor.matmul(banks[7][:, 0:GT], wo[:, h - 1, :], sg[:, h - 1, :], start=(h == 1), stop=(h == NH)).then_inc(front["projO"], 1)

        def root(act, i, n):
            act.wait_ge(front["summed"], i * 2 * KC + n + 1)
            if n >= 2:
                act.wait_ge(front["normed"], i * 2 * KC + n - 1)
            r = rt[n % 2]
            nc.scalar.activation(r[:], banks[(NQ + 2 + n) % NB][:, 0:GT], ACT.Ln, bias=eps6[:]).then_inc(front["logged"], 1)
            act.wait_ge(front["logged"], i * 2 * KC + n + 1)
            nc.scalar.activation(r[:], r[:], ACT.Exp, scale=-0.5, bias=lnsc[:] if n < KC else 0.0).then_inc(front["rooted"], 1)

        @block.scalar
        def _(act):
            with act.Fori(0, NG) as i:
                for n in range(NQ + 2):
                    if n < NQ:
                        act.wait_ge(front["projected"], i * (NQ + NH) + n + 1)
                        src = banks[n % NB][:, 0:GT]
                    if n < NQ:
                        dst = qk[:, n, :] if n < 2 * KC else v[:, n - 2 * KC, :]
                        nc.scalar.activation(dst, src, ACT.Copy, scale=taps[:, n, 3:4]).then_inc(front["tapped"], 1)
                    if n >= 2:
                        c = n - 2
                        act.wait_ge(front["convolved"], i * NQ + c + 1)
                        dst = qk[:, c, :] if c < 2 * KC else v[:, c - 2 * KC, :]
                        nc.scalar.activation(dst, dst, ACT.Silu).then_inc(front["silued"], 1)
                nc.scalar.preload_act_table_set("natural_log_exp_and_others")
                for n in range(2 * KC):
                    if n == 0:
                        act.wait_ge(front["silued"], i * NQ + NQ)
                    if n >= 2:
                        act.wait_ge(front["summed"], i * 2 * KC + n - 1)
                    nc.scalar.activation(sq[n % 2][:], qk[:, n, :], ACT.Square).then_inc(front["squared"], 1)
                    if n >= 1:
                        root(act, i, n - 1)
                root(act, i, 2 * KC - 1)
                act.wait_ge(front["biased"], i + 1)
                nc.scalar.activation(spt[:], raw[:], ACT.Abs).then_inc(front["absed"], 1)
                act.wait_ge(front["absed"], i + 1)
                nc.scalar.activation(spt[:], spt[:], ACT.Exp, scale=-1.0).then_inc(front["soft1"], 1)
                act.wait_ge(front["soft1"], i + 1)
                nc.scalar.activation(spt[:], spt[:], ACT.Ln, bias=1.0).then_inc(front["soft2"], 1)
                act.wait_ge(front["soft"], i + 1)
                nc.scalar.activation(beta[:], spl[:, 1, :], ACT.Exp, scale=-1.0).then_inc(front["betaed"], 1)
                for b in range(GB):
                    for j, step in enumerate(ACT_):
                        for u in range(NU):
                            B = buf[u]
                            if step in ("expA", "expT", "expL"):
                                act.wait_ge(dve_done[u], at(i, b, DVE_, "min" + step[3]))
                                t = B[{"A": "AT", "T": "b1", "L": "b2"}[step[3]]]
                                nc.scalar.activation(t[:], t[:], ACT.Exp).then_inc(act_done[u], 1)
                                continue
                            act.wait_ge(pe_done[u], at(i, b, PE_, step))
                            seq = (b * len(PE_) + PE_.index(step)) * NU + u
                            bk = banks[seq % NB]
                            if step == "Z":
                                nc.scalar.activation(Z[u][:], bk[0:L, :], ACT.Copy).then_inc(act_done[u], 1)
                            elif step == "O":
                                nc.scalar.activation(v[:, u * U:(u + 1) * U, b * L:(b + 1) * L],
                                                     bk[:, 0:UT].rearrange("v (h t) -> v h t", t=L), ACT.Copy).then_inc(act_done[u], 1)
                            else:
                                t = B[{"M2T": "b4", "M2": "b5", "M4T": "b1", "M4": "b3", "M8": "b4", "N": "b5", "NT": "b1",
                                       "N2T": "b3", "N2": "b4", "N4T": "b2"}[step]]
                                nc.scalar.activation(t[:], bk[0:L, 0:UT], ACT.Copy).then_inc(act_done[u], 1)
                for u in range(NU):
                    act.wait_ge(act_done[u], at(i, GB - 1, ACT_, "O"))
                for h in range(NH):
                    act.wait_ge(front["projected"], i * (NQ + NH) + NQ + h + 1)
                    nc.scalar.activation(sg[:, h, :], banks[2 + h % 4][:, 0:GT], ACT.Silu).then_inc(front["gated"], 1)
                nc.scalar.preload_act_table_set("natural_log_exp_and_others")
                for h in range(NH + 1):
                    if h < NH:
                        if h >= 2:
                            act.wait_ge(front["osummed"], i * NH + h - 1)
                        nc.scalar.activation(sq[h % 2][:], v[:, h, :], ACT.Square).then_inc(front["osquared"], 1)
                    if h >= 1:
                        act.wait_ge(front["osummed"], i * NH + h)
                        if h >= 3:
                            act.wait_ge(front["oscaled"], i * NH + h - 2)
                        r = rt[(h - 1) % 2]
                        nc.scalar.activation(r[:], banks[(h - 1) % 2][:, 0:GT], ACT.Ln, bias=k["eps"][:]).then_inc(front["ologged"], 1)
                        act.wait_ge(front["ologged"], i * NH + h)
                        nc.scalar.activation(r[:], r[:], ACT.Exp, scale=-0.5).then_inc(front["orooted"], 1)

        @block.gpsimd
        def _(pool):
            nc.gpsimd.memset(half[:], 0.0).then_inc(front["halved"], 1)
            with pool.Fori(0, NG) as i:
                pool.wait_ge(front["ready"], i + 1)
                for b in range(GB):
                    tb = slice(b * L, (b + 1) * L)
                    if b:
                        for u in range(NU):
                            pool.wait_ge(pe_done[u], at(i, b - 1, PE_, "argL"))
                    bc = lambda t: t[:, tb].unsqueeze(1).to_broadcast([NH, NH, L])
                    nc.gpsimd.tensor_tensor(rhsA[R2:R2 + NH], ind[:], bc(G), ALU.mult)
                    nc.gpsimd.tensor_tensor(rhsT[R2:R2 + NH], ind[:], bc(Gb), ALU.mult)
                    nc.gpsimd.tensor_tensor(rhsL[R2:R2 + NH], ind[:], bc(lhsA[0:NH]), ALU.mult).then_inc(front["rows"], 1)
                    pool.wait_ge(front["rows"], i * GB + b + 1)
                    for u in range(NU):
                        B = buf[u]
                        pool.wait_ge(dve_done[u], at(i, b, DVE_, "M"))
                        nc.gpsimd.tensor_tensor(B["b3"][:], B["b2"][:], inblk[:].rearrange("p h t -> p (h t)"), ALU.mult).then_inc(pool_done[u], 1)
                        pool.wait_ge(pool_done[u], at(i, b, POOL_, "Md"))
                        nc.gpsimd.tensor_tensor(B["b2"][:], B["b2"][:], outblk[:].rearrange("p h t -> p (h t)"), ALU.mult).then_inc(pool_done[u], 1)
                    pool.wait_ge(pool_done[NU - 1], at(i, b, POOL_, "Mo"))

        @block.vector
        def _(dve):
            dve.wait_ge(front["halved"], 1)
            dve.sem_inc(front["added"], 1)
            ch = s.sem("ch")
            NC_ = NQ * 2
            with dve.Fori(0, NG) as i:
                for n in range(NQ):
                    dve.wait_ge(front["tapped"], i * NQ + n + 1)
                    dst = shape(qk[:, n, :] if n < 2 * KC else v[:, n - 2 * KC, :])
                    src = shape(banks[n % NB][:, 0:GT])
                    for j in range(1, 4):
                        ins = nc.vector.scalar_tensor_tensor(out=dst[:, :, j:L], in0=src[:, :, 0:L - j], scalar=taps[:, n, 3 - j:4 - j],
                                                             in1=dst[:, :, j:L], op0=ALU.mult, op1=ALU.add)
                        if j < 3:
                            ins.then_inc(ch, 1)
                            dve.wait_ge(ch, i * NC_ + n * 2 + j)
                    ins.then_inc(front["convolved"], 1)
                dve.wait_ge(front["smalls"], 2 * i + 2)
                nc.vector.tensor_scalar(raw[:, 0, :], banks[NQ % NB][0:NH, 0:GT], hb[:, 0:1], None, ALU.add)
                nc.vector.tensor_scalar(raw[:, 1, :], banks[(NQ + 1) % NB][0:NH, 0:GT], hb[:, 1:2], -1.0, ALU.add, ALU.mult).then_inc(front["biased"], 1)
                for n in range(2 * KC):
                    dve.wait_ge(front["rooted"], i * 2 * KC + n + 1)
                    for e in range(2):
                        r = slice(e * DK, (e + 1) * DK)
                        ins = nc.vector.tensor_tensor(half[r, n // KC, n % KC, e, :], qk[r, n, :], rt[n % 2][r, :], ALU.mult)
                    ins.then_inc(front["normed"], 1)
                dve.wait_ge(front["soft2"], i + 1)
                nc.vector.scalar_tensor_tensor(out=spl[:], in0=raw[:], scalar=0.0, in1=spt[:], op0=ALU.max, op1=ALU.add).then_inc(front["soft"], 1)
                dve.wait_ge(front["soft"], i + 1)
                nc.vector.tensor_scalar(spl[:, 0, :], spl[:, 0, :], hb[:, 3:4], None, ALU.mult).then_inc(front["gked"], 1)
                dve.wait_ge(front["gked"], i + 1)
                nc.vector.tensor_tensor_scan(G[:], keep[:].rearrange("h b t -> h (b t)"), spl[:, 0, :], 0.0, ALU.mult, ALU.add).then_inc(front["summedG"], 1)
                dve.wait_ge(front["summedG"], i + 1)
                nc.vector.tensor_tensor(Gb[:], G[:], spl[:, 1, :], ALU.subtract)
                nc.vector.tensor_tensor(lhsL[0:NH, :], G[:], spl[:, 1, :], ALU.subtract)
                nc.vector.tensor_scalar(lhsA[0:NH, :], G[:], -1.0, None, ALU.mult)
                dve.wait_ge(front["turned"], i + 1)
                nc.vector.tensor_copy(betaT[:], banks[0][0:L, 0:GB * NH].rearrange("t (b h) -> t b h", h=NH)).then_inc(front["ready"], 1)
                dve.wait_ge(front["ready"], i + 1)
                for b in range(GB):
                    for j, step in enumerate(DVE_):
                        for u in range(NU):
                            B = buf[u]
                            src = {"minA": "argA", "minT": "argT", "minL": "argL", "MT": "kk", "M": "kk", "AT": "qk", "X": "vT"}.get(step, step)
                            if step != "R1":
                                dve.wait_ge(pe_done[u], at(i, b, PE_, src))
                                seq = (b * len(PE_) + PE_.index(src)) * NU + u
                                bk = banks[seq % NB]
                            wide, nar = (bk[0:L, 0:UT], bk[0:L, :])
                            if step.startswith("min"):
                                mask = {"A": upto, "T": within, "L": below}[step[3]]
                                t = B[{"A": "AT", "T": "b1", "L": "b2"}[step[3]]]
                                ins = nc.vector.tensor_tensor(t[:], wide, mask[:].rearrange("p h t -> p (h t)"), ALU.min)
                            elif step in ("MT", "M", "AT"):
                                dve.wait_ge(act_done[u], at(i, b, ACT_, {"MT": "expT", "M": "expL", "AT": "expA"}[step]))
                                t = B[{"MT": "b1", "M": "b2", "AT": "AT"}[step]]
                                ins = nc.vector.tensor_tensor(t[:], wide, t[:], ALU.mult)
                            elif step == "X":
                                bt = betaT[:, b, u * U:(u + 1) * U].unsqueeze(2).to_broadcast([L, U, DV])
                                ins = nc.vector.tensor_tensor(Z[u][:].rearrange("t (h v) -> t h v", v=DV),
                                                              nar.rearrange("t (h v) -> t h v", v=DV), bt, ALU.mult)
                            elif step == "R1":
                                dve.wait_ge(dve_done[u], at(i, b, DVE_, "MT"))
                                ins = nc.vector.tensor_tensor(B["R"][:], eyes[:].rearrange("p h t -> p (h t)"), B["b1"][:], ALU.subtract)
                            elif step[0] == "R":
                                ins = nc.vector.tensor_tensor(B["R"][:], B["R"][:], wide, ALU.add)
                            elif step == "Z1":
                                ins = nc.vector.tensor_tensor(Z[u][:], Z[u][:], nar, ALU.subtract)
                            else:
                                ins = nc.vector.tensor_tensor(Z[u][:], Z[u][:], nar, ALU.add)
                            ins.then_inc(dve_done[u], 1)
                for h in range(NH):
                    dve.wait_ge(front["orooted"], i * NH + h + 1)
                    nc.vector.tensor_tensor(v[:, h, :], v[:, h, :], rt[h % 2][:], ALU.mult).then_inc(front["oscaled"], 1)
                    dve.wait_ge(front["oscaled"], i * NH + h + 1)
                    nc.vector.scalar_tensor_tensor(out=sg[:, h, :], in0=v[:, h, :], scalar=gnw[:], in1=sg[:, h, :], op0=ALU.mult,
                                                   op1=ALU.mult).then_inc(front["ogated"], 1)
                dve.wait_ge(front["projO"], (i + 1) * NH)
                x = xT[:, bass.ds(i * GT, GT)]
                nc.vector.tensor_tensor(x, x, banks[7][:, 0:GT], ALU.add).then_inc(front["added"], 1)


def split_keys(nc, k, a):
    ctxd = a["ctx_2048"]
    S = ctxd.shape[1]
    FT, TAIL = S // 128, S % 128
    tiles = [128] * FT + [TAIL]
    TG = [range(t, min(t + 4, FT + 1)) for t in range(0, FT + 1, 4)]
    k["kparts"] = nc.dram_tensor("kparts", [B, 3, D, S], BF16).ap()
    with ExitStack() as ctx:
        s = Stage(nc, ctx, "skeys")
        kc = [s.sb(f"kc{p}", [128, FT + 1, D]) for p in range(2)]
        kT, rest = [s.sb(f"kT{p}", [D, S]) for p in range(2)], [s.sb(f"rest{p}", [D, S]) for p in range(2)]
        part = [s.sb(f"part{p}", [D, 3, S], BF16) for p in range(2)]
        bank = [s.ps(f"bank{n}") for n in range(2 * len(TG))]
        loaded = [s.sem(f"loaded{p}") for p in range(2)]
        wrote = [s.sem(f"wrote{p}") for p in range(2)]
        turned, kept, first, second, rest1, rest2 = [s.sem(n) for n in
            ("turned", "kept", "first", "second", "rest1", "rest2")]
        held = s.sem("held")
        block = ctx.enter_context(nc.Block())

        @block.sync
        def _(sp):
            def fetch(b, p):
                    sp.wait_ge(turned, b + 1)
                    sp.sem_inc(held, 1)
                    sp.dma_start(kc[p][:, 0:FT, :], ctxd[bass.ds(b, 1), 0:FT * 128, 0:D].rearrange("o (j p) c -> p (o j) c", p=128)).then_inc(loaded[p], 16)
                    sp.dma_start(kc[p][0:TAIL, FT, :], ctxd[bass.ds(b, 1), FT * 128:S, 0:D].rearrange("o s c -> (o s) c")).then_inc(loaded[p], 16)

            def write(b, p):
                sp.wait_ge(rest2, b + 3)
                sp.sem_inc(held, 1)
                sp.dma_start(k["kparts"][bass.ds(b, 1)].rearrange("o n d s -> d (o n) s"), part[p][:]).then_inc(wrote[p], 16)
            for p in range(2):
                sp.sem_inc(wrote[p], 16)
                fetch(p, p)
            with sp.Fori(0, B // 2 - 1) as i:
                for p in range(2):
                    fetch(2 * i + 2 + p, p)
                    write(2 * i + p, p)
            for p in range(2):
                write(B - 2 + p, p)
            for p in range(2):
                sp.wait_ge(wrote[p], 16 * (B // 2) + 16)

        @block.tensor
        def _(pe):
            pe.sem_inc(turned, 2)
            with pe.Fori(0, B // 2) as i:
                for p in range(2):
                    b = 2 * i + p
                    pe.wait_ge(loaded[p], 32 * i + 32)
                    pe.wait_ge(kept, b + 1)
                    for n, ts in enumerate(TG):
                        for j in ts:
                            r = tiles[j]
                            ins = nc.tensor.transpose(bank[p * len(TG) + n][:, (j - ts[0]) * 128:(j - ts[0]) * 128 + r],
                                                      kc[p][0:r, j, :], k["ident"][0:r, 0:r])
                    ins.then_inc(turned, 1)

        @block.vector
        def _(dve):
            dve.sem_inc(kept, 2)
            dve.sem_inc(rest1, 2)
            with dve.Fori(0, B // 2) as i:
                for p in range(2):
                    b = 2 * i + p
                    dve.wait_ge(turned, b + 3)
                    dve.wait_ge(rest1, b + 1)
                    dve.wait_ge(first, b + 1)
                    for n, ts in enumerate(TG):
                        w = sum(tiles[j] for j in ts)
                        ins = nc.vector.tensor_copy(kT[p][:, ts[0] * 128:ts[0] * 128 + w], bank[p * len(TG) + n][:, 0:w])
                    ins.then_inc(kept, 1)
                    dve.wait_ge(first, b + 3)
                    dve.wait_ge(rest2, b + 1)
                    nc.vector.tensor_tensor(rest[p][:], kT[p][:], part[p][:, 0, :], ALU.subtract).then_inc(rest1, 1)

        @block.scalar
        def _(act):
            for n in (first, second):
                act.sem_inc(n, 2)
            with act.Fori(0, B // 2) as i:
                for p in range(2):
                    b = 2 * i + p
                    act.wait_ge(wrote[p], 16 * i + 16)
                    act.wait_ge(kept, b + 3)
                    nc.scalar.activation(part[p][:, 0, :], kT[p][:], ACT.Copy).then_inc(first, 1)
                    act.wait_ge(rest1, b + 3)
                    nc.scalar.activation(part[p][:, 1, :], rest[p][:], ACT.Copy).then_inc(second, 1)

        @block.gpsimd
        def _(pool):
            pool.sem_inc(rest2, 2)
            with pool.Fori(0, B // 2) as i:
                for p in range(2):
                    b = 2 * i + p
                    pool.wait_ge(second, b + 3)
                    nc.gpsimd.tensor_tensor(part[p][:, 2, :], rest[p][:], part[p][:, 1, :], ALU.subtract).then_inc(rest2, 1)


def cross(nc, k, a, tag, H, own):
    xT, ctxd = k["xT"], a["ctx_2048"]
    S, DH = ctxd.shape[1], D // H
    FT, TAIL = S // 128, S % 128
    tiles = [128] * FT + [TAIL] + ([L] if own else [])
    first = [sum(tiles[:n]) for n in range(len(tiles))]
    NT, KEYS = len(tiles), sum(tiles)
    CK = -(-KEYS // 512)
    KW = -(-KEYS // (2 * CK)) * 2
    assert KW <= 512
    HQ = H * L
    NW = -(-HQ // 128)
    HW = GT
    half = 2 * HW
    HH = half // L
    steps = [(j, c) for j in range(NT) for c in range(HQ // half)]
    SLOTS = [(0, 0), (0, 1), (1, 0), (1, 1), (0, 2), (2, 0)]
    F = 16
    NGR, EH = D // F, F // DH
    KR = len(SLOTS) * F
    V1 = DH + 1
    CT = 4
    HG = H // CT
    scale = float(DH ** -0.5)
    with ExitStack() as ctx:
        s = Stage(nc, ctx, tag)
        headof, one16 = s.sb("headof", [128, H]), s.sb("one16", [1, 128], BF16)
        sumof, outof = s.sb("sumof", [128, 128]), s.sb("outof", [128, HG, D])
        made = s.sem("made")
        with nc.Block() as block:
            @block.gpsimd
            def _(pool):
                count = [0]

                def link(ins):
                    count[0] += 1
                    ins.then_inc(made, 1)
                    pool.wait_ge(made, count[0])
                nc.gpsimd.memset(one16[:], 1.0)
                link(nc.gpsimd.memset(outof[:], 0.0))
                link(nc.gpsimd.memset(sumof[:], -1.0))
                sv = sumof[:].rearrange("p (c r) -> p c r", r=32)
                link(nc.gpsimd.affine_select(out=sv, in_=sv, compare_op=ALU.is_equal, fill=0.0, base=-DH,
                                             pattern=[[-32, CT], [0, 32]], channel_multiplier=1))
                link(nc.gpsimd.memset(headof[:], 1.0))
                link(nc.gpsimd.affine_select(out=headof[:], in_=headof[:], compare_op=ALU.is_ge, fill=0.0, base=0,
                                             pattern=[[-DH, H]], channel_multiplier=1))
                link(nc.gpsimd.affine_select(out=headof[:], in_=headof[:], compare_op=ALU.is_ge, fill=0.0, base=DH - 1,
                                             pattern=[[DH, H]], channel_multiplier=-1))
        qparts = nc.dram_tensor(tag + "_qparts", [3, D, N], BF16).ap()
        bp = s.sb("bp", [D, 1])
        if own:
            kS, vS = s.sb("kS", [D, N]), s.sb("vS", [L, B, D])
            ownparts = nc.dram_tensor(tag + "_ownparts", [3, D, N], BF16).ap()
            w_proj = a[f"{tag}_w_proj"]
        else:
            biasT = s.sb("biasT", [128, FT + 1, B])
        qT = s.sb("qT", [D, N])
        with ExitStack() as mine:
            t = Stage(nc, mine, tag + "p")
            if own:
                wT = t.sb("wT", [D, 4, D])
                pre = a[f"{tag}_w_qkv"]
                load(nc, tag + "l", [(bp[:], col(a[f"{tag}_b_proj"]))])
                load_transposed(nc, k, tag + "t", [(wT[:, n, :], pre[n * D:(n + 1) * D, :]) for n in range(3)]
                                + [(wT[:, 3, :], w_proj)])
                load(nc, tag + "o", [(outof[32 * (h % CT):32 * (h % CT) + DH, h // CT, :], wT[h * DH:(h + 1) * DH, 3, :]) for h in range(H)])
                xs = [t.sb(f"xs{p}", [D, GT]) for p in range(2)]
                pp = [[t.ps(f"pp{n}{p}") for n in range(3)] for p in range(2)]
                held = t.sem("held")
                staged, projected, kept, keptv = t.sem("staged"), t.sem("projected"), t.sem("kept"), t.sem("keptv")
                with nc.Block() as block:
                    @block.gpsimd
                    def _(pool):
                        with pool.Fori(0, NG // 2) as i:
                            for p in range(2):
                                g = 2 * i + p
                                pool.wait_ge(kept, g + 1)
                                pool.wait_ge(keptv, g + 1)
                                pool.sem_inc(held, 1)
                                nc.gpsimd.tensor_copy(xs[p][:], xT[:, bass.ds(g * GT, GT)]).then_inc(staged, 1)

                    @block.tensor
                    def _(pe):
                        with pe.Fori(0, NG // 2) as i:
                            for p in range(2):
                                g = 2 * i + p
                                pe.wait_ge(staged, g + 1)
                                for n in range(2):
                                    nc.tensor.matmul(pp[p][n][:, 0:GT], wT[:, n, :], xs[p][:], start=True, stop=True)
                                for b in range(GB):
                                    ins = nc.tensor.matmul(pp[p][2][0:L, b * D:(b + 1) * D], xs[p][:, b * L:(b + 1) * L], wT[:, 2, :],
                                                           start=True, stop=True)
                                ins.then_inc(projected, 1)

                    @block.scalar
                    def _(act):
                        act.sem_inc(kept, 2)
                        with act.Fori(0, NG // 2) as i:
                            for p in range(2):
                                g = 2 * i + p
                                act.wait_ge(projected, g + 1)
                                nc.scalar.activation(qT[:, bass.ds(g * GT, GT)], pp[p][0][:, 0:GT], ACT.Copy)
                                nc.scalar.activation(kS[:, bass.ds(g * GT, GT)], pp[p][1][:, 0:GT], ACT.Copy).then_inc(kept, 1)

                    @block.vector
                    def _(dve):
                        dve.sem_inc(keptv, 2)
                        with dve.Fori(0, NG // 2) as i:
                            for p in range(2):
                                g = 2 * i + p
                                dve.wait_ge(projected, g + 1)
                                nc.vector.tensor_copy(vS[:, bass.ds(g * GB, GB), :].rearrange("t b d -> t (b d)"),
                                                      pp[p][2][0:L, :]).then_inc(keptv, 1)
            else:
                load(nc, tag + "o", [(outof[32 * (h % CT):32 * (h % CT) + DH, h // CT, :], k["ident"][h * DH:(h + 1) * DH, :]) for h in range(H)])
                mk, mf, live, bb = t.sb("mk", [B, S], I32), t.sb("mf", [B, S]), t.sb("live", [B, 1]), t.sb("bb", [128, 1])
                m16, liveall = t.sb("m16", [B, S], BF16), t.sb("liveall", [128, B])
                bias_d, bias16_d = nc.dram_tensor(tag + "_bias_d", [B, S], F32).ap(), nc.dram_tensor(tag + "_bias16_d", [B, S], BF16).ap()
                live_d = nc.dram_tensor(tag + "_live_d", [B, 1], F32).ap()
                load(nc, tag + "l", [(mk[:], a["mask_BxS2_ik0"]), (bb[:], a["L3_xattn_b"].unsqueeze(0).to_broadcast([128, 1]))])
                c, w = t.sem("c"), t.sem("w")
                with nc.Block() as block:
                    @block.vector
                    def _(dve):
                        nc.vector.memset(bp[:], 0.0)
                        nc.vector.tensor_copy(mf[:], mk[:]).then_inc(c, 1)
                        dve.wait_ge(c, 1)
                        nc.vector.reduce_max(live[:], mf[:], AX).then_inc(c, 1)
                        nc.vector.tensor_scalar(mf[:], mf[:], -1.0, 1e30, ALU.add, ALU.mult).then_inc(c, 1)
                        dve.wait_ge(c, 3)
                        nc.vector.tensor_scalar(mf[:], mf[:], live[:], bb[0:B], ALU.mult, ALU.add).then_inc(c, 1)
                        dve.wait_ge(c, 4)
                        nc.vector.tensor_copy(m16[:], mf[:]).then_inc(c, 1)

                    @block.sync
                    def _(sp):
                        sp.wait_ge(c, 5)
                        sp.dma_start(bias_d, mf[:]).then_inc(w, 16)
                        sp.dma_start(bias16_d, m16[:]).then_inc(w, 16)
                        sp.dma_start(live_d, live[:]).then_inc(w, 16)
                        sp.wait_ge(w, 48)
                        sp.dma_start(liveall[:], live_d.rearrange("b o -> o b").to_broadcast([128, B])).then_inc(w, 16)
                        sp.wait_ge(w, 64)
                load_transposed(nc, k, tag + "b", [(biasT[0:tiles[j], j, :], bias_d[:, j * 128:j * 128 + tiles[j]]) for j in range(FT + 1)])
            qs, qp = t.sb("qs", [D, N]), t.sb("qp", [D, 3, N], BF16)
            cut, out = t.sem("cut"), t.sem("out")
            sources = [(qT, qparts)] + ([(kS, ownparts)] if own else [])
            with nc.Block() as block:
                @block.vector
                def _(dve):
                    at = [0]

                    def link(ins):
                        at[0] += 1
                        ins.then_inc(cut, 1)
                        dve.wait_ge(cut, at[0])
                    link(nc.vector.tensor_scalar(qT[:], qT[:] if own else xT[:], scale, None, ALU.mult))
                    if not own:
                        by = qT[:].rearrange("d (b t) -> d b t", t=L)
                        link(nc.vector.tensor_tensor(by, by, liveall[:].unsqueeze(2).to_broadcast([D, B, L]), ALU.mult))
                    for m, (src, dst) in enumerate(sources):
                        if m:
                            dve.wait_ge(out, 16 * m)
                        for n in range(3):
                            left = qs if n else src
                            link(nc.vector.tensor_copy(qp[:, n, :], left[:]))
                            if n < 2:
                                link(nc.vector.tensor_tensor(qs[:], left[:], qp[:, n, :], ALU.subtract))

                @block.sync
                def _(sp):
                    for m, (src, dst) in enumerate(sources):
                        sp.wait_ge(cut, (1 if own else 2) + 5 * (m + 1))
                        sp.dma_start(dst.rearrange("n d t -> d n t"), qp[:]).then_inc(out, 16)
                        sp.wait_ge(out, 16 * (m + 1))

        kv = [s.sb(f"kv{p}", [128, FT + 1, D]) for p in range(2)]
        KS = [s.sb(f"KS{p}", [KR + 1, NGR, KEYS], BF16) for p in range(2)]
        QSw = [s.sb(f"QS{p}", [KR + 1, NW * 128], BF16) for p in range(2)]
        QS = [q[:, 0:HQ].rearrange("r (g e t) -> r g e t", e=EH, t=L) for q in QSw]
        k16 = [s.sb(f"k16{p}", [D, KEYS], BF16) for p in range(2)]
        v1 = [s.sb(f"v1{p}", [128, NT, H, V1]) for p in range(2)]
        qb16 = [s.sb(f"qb16{p}", [D, H, L], BF16) for p in range(2)]
        mx, top, top16 = s.sb("mx", [128, NW, CK]), s.sb("top", [128, NW]), s.sb("top16", [NW, 128], BF16)
        E = [s.sb(f"E{p}", [128, half]) for p in range(2)]
        U, R, R2 = [s.sb(n, [128, HG * L]) for n in ("U", "R", "R2")]
        br = [s.sb(f"br{p}", [1, S], BF16) for p in range(2)]
        sc, pm = [s.ps(f"sc{p}", (128, 1024)) for p in range(2)], [s.ps(f"pm{p}") for p in range(2)]
        po, px = s.ps("po"), s.ps("px")
        landed_a, landed_b, rowed = [[s.sem(f"{n}{p}") for p in range(2)] for n in ("keys16", "stacked", "rowed")]
        z = {n: s.sem(n) for n in ("queried16", "valued", "scored", "maxed", "topped", "toprow", "toprow16", "ready", "exped",
                                   "pved", "saved", "summed", "logged", "inverted", "refined", "normed", "projected", "done", "held", "filled", "cleared", "zeroed")}
        NS, NM = len(steps), NW * CK
        flat = lambda t: t.rearrange("p h t -> p (h t)")
        PACE = 3 * (NS - 3)
        STEP = 8 if NS > 20 else 6
        MID, END = (12, 24) if NS > 20 else (9, 16)
        NDA = 3 if own else 4
        NDB = len(SLOTS) * (1 + EH + int(own))
        number = lambda bt: 2 * bt[0] + bt[1]
        after = lambda bt: (bt[0], 1) if bt[1] == 0 else (bt[0] + 1, 0)
        before = lambda bt: (bt[0], 0) if bt[1] == 1 else (bt[0] - 1, 1)
        last = B // 2 - 1
        main = ExitStack()
        block = main.enter_context(nc.Block())

        @block.sync
        def _(sp):
            def fetch(bt, fresh=False):
                b, p = number(bt), bt[1]
                if not fresh:
                    sp.wait_ge(z["scored"], (b - 1) * NM)
                    sp.sem_inc(z["held"], 1)
                    sp.wait_ge(z["valued"], b - 1)
                    sp.sem_inc(z["held"], 1)
                sp.dma_start(k16[p][:, 0:S], k["kparts"][bass.ds(b, 1), 0, :, :].rearrange("o d s -> (o d) s")).then_inc(landed_a[p], 16)
                sp.dma_start(kv[p][:, 0:FT, :], ctxd[bass.ds(b, 1), 0:FT * 128, D:2 * D].rearrange("o (j p) c -> p (o j) c", p=128)).then_inc(landed_a[p], 16)
                sp.dma_start(kv[p][0:TAIL, FT, :], ctxd[bass.ds(b, 1), FT * 128:S, D:2 * D].rearrange("o s c -> (o s) c")).then_inc(landed_a[p], 16)

                if not own:
                    sp.dma_start(br[p][:], bias16_d[bass.ds(b, 1), :]).then_inc(landed_a[p], 16)

            def fetch_stack(bt, fresh=False):
                b, p = number(bt), bt[1]
                if not fresh:
                    sp.wait_ge(z["ready"], (b - 1) * NS)
                    sp.sem_inc(z["held"], 1)
                for n, (kp, qp_) in enumerate(SLOTS):
                    rows = slice(n * F, (n + 1) * F)
                    sp.dma_start(KS[p][rows, :, 0:S], k["kparts"][bass.ds(b, 1), kp, :, :].rearrange("o (g r) s -> r (o g) s", r=F)).then_inc(landed_b[p], 16)
                    if own:
                        sp.dma_start(KS[p][rows, :, S:KEYS], ownparts[kp].rearrange("(g r) t -> r g t", r=F)[:, :, bass.ds(b * L, L)]).then_inc(landed_b[p], 16)
                    for e in range(EH):
                        rows = slice(n * F + e * DH, n * F + (e + 1) * DH)
                        src = qparts[qp_].rearrange("(g e r) t -> e r g t", e=EH, r=DH)[e]
                        sp.dma_start(QS[p][rows, :, e, :], src[:, :, bass.ds(b * L, L)]).then_inc(landed_b[p], 16)

            def place(bt):
                b, p = number(bt), bt[1]
                sp.wait_ge(z["toprow16"], b + 1)
                sp.sem_inc(z["held"], 1)
                sp.dma_start(QSw[p][KR:KR + 1, :], top16[:]).then_inc(rowed[p], 16)
            sp.wait_ge(z["cleared"], 1)
            for p in range(2):
                fetch((0, p), fresh=True)
                fetch_stack((0, p), fresh=True)
            place((0, 0))
            with sp.Fori(0, last) as i:
                for p in range(2):
                    fetch((i + 1, p))
                    place(after((i, p)))
                    fetch_stack((i + 1, p))
            place((last, 1))

        @block.gpsimd
        def _(pool):
            for p in range(2):
                ins = nc.gpsimd.memset(QSw[p][0:KR], 0.0)
            ins.then_inc(z["cleared"], 1)
            for p in range(2):
                nc.gpsimd.memset(v1[p][:], 1.0)
            nc.gpsimd.memset(top[:], 0.0).then_inc(z["filled"], 1)
            pool.wait_ge(z["filled"], 1)

            def spread(dst, b):
                return nc.gpsimd.tensor_tensor(dst[:], qT[:, bass.ds(b * L, L)].unsqueeze(1).to_broadcast([D, H, L]),
                                               headof[:].unsqueeze(2).to_broadcast([D, H, L]), ALU.mult)

            def for_maxima(bt, fresh=False):
                b, p = number(bt), bt[1]
                if not fresh:
                    pool.wait_ge(z["scored"], (b - 1) * NM)
                if own:
                    pool.sem_inc(z["held"], 1)
                    nc.gpsimd.tensor_copy(k16[p][:, S:KEYS], kS[:, bass.ds(b * L, L)])
                spread(qb16[p], b).then_inc(z["queried16"], 1)

            def for_scores(bt, fresh=False):
                b, p = number(bt), bt[1]
                if not fresh:
                    pool.wait_ge(z["pved"], (b - 1) * NS)
                pool.wait_ge(landed_a[p], 16 * NDA * bt[0] + 16 * NDA)
                pool.sem_inc(z["held"], 1)
                nc.gpsimd.tensor_copy(v1[p][:, 0:FT, :, 0:DH], kv[p][:, 0:FT, :].rearrange("s j (h d) -> s j h d", d=DH))
                ins = nc.gpsimd.tensor_copy(v1[p][0:TAIL, FT, :, 0:DH], kv[p][0:TAIL, FT, :].rearrange("s (h d) -> s h d", d=DH))
                if own:
                    ins = nc.gpsimd.tensor_copy(v1[p][0:L, FT + 1, :, 0:DH],
                                                vS[:, bass.ds(b, 1), :].rearrange("t o (h d) -> t (o h) d", d=DH))
                ins.then_inc(z["valued"], 1)
            for_maxima((0, 0), fresh=True)
            for_maxima((0, 1), fresh=True)
            for_scores((0, 0), fresh=True)
            for_scores((0, 1), fresh=True)
            for_maxima((1, 0))
            with pool.Fori(1, last) as i:
                for_scores((i, 0))
                for_maxima((i, 1))
                for_scores((i, 1))
                for_maxima((i + 1, 0))
            for_scores((last, 0))
            for_maxima((last, 1))
            for_scores((last, 1))

        @block.tensor
        def _(pe):
            pe.wait_ge(z["filled"], 1)
            pe.wait_ge(z["zeroed"], 1)

            def score(bt, n):
                b, p = number(bt), bt[1]
                w, c = n // CK, n % CK
                if n == 0:
                    pe.wait_ge(landed_a[p], 16 * NDA * bt[0] + 16 * NDA)
                    pe.wait_ge(z["queried16"], b + 1)
                    if not isinstance(b, int) or b:
                        pe.wait_ge(z["maxed"], b * NM)
                if n >= 2:
                    pe.wait_ge(z["maxed"], b * NM + n - 1)
                r = min(128, HQ - w * 128)
                cols = slice(c * KW, min((c + 1) * KW, KEYS))
                dst = pm[n % 2][0:r, 0:cols.stop - cols.start]
                ins = nc.tensor.matmul(dst, flat(qb16[p][:])[:, w * 128:w * 128 + r], k16[p][:, cols], start=True, stop=own)
                if not own:
                    ins = nc.tensor.matmul(dst, one16[0:1, 0:r], br[p][:, cols], start=False, stop=True)
                ins.then_inc(z["scored"], 1)

            def toprow(bt):
                b = number(bt)
                pe.wait_ge(z["topped"], 2 * b + 2)
                nc.tensor.transpose(px[0:NW, 0:128], top[:], k["ident"][:]).then_inc(z["toprow"], 1)

            def attend(bt, more, prior):
                b, p = number(bt), bt[1]
                scores = list(range(NM)) if more else []

                def between(place):
                    while scores and (NM - len(scores)) * PACE < NM * (place + 1):
                        score(after(bt), scores.pop(0))

                def weigh(n):
                    j, c = steps[n]
                    pe.wait_ge(z["exped"], b * NS + n + 1)
                    if n == 0 and prior:
                        pe.wait_ge(z["saved"], b)
                    if tiles[j] <= 64:
                        pe.sem_inc(z["held"], 1)
                    for h in range(HH):
                        hd = c * HH + h
                        at = 32 * (hd % CT)
                        ins = nc.tensor.matmul(po[at:at + V1, hd // CT * L:(hd // CT + 1) * L], v1[p][0:tiles[j], j, hd, :],
                                               E[n % 2][0:tiles[j], h * L:(h + 1) * L], start=(n == 0 and h < CT), stop=(n == NS - 1),
                                               skip_group_check=True, tile_position=(0, at))
                    ins.then_inc(z["pved"], 1)
                pe.wait_ge(landed_b[p], 16 * NDB * bt[0] + 16 * NDB)
                pe.wait_ge(rowed[p], 16 * bt[0] + 16)
                pe.wait_ge(z["valued"], b + 1)
                for n, (j, c) in enumerate(steps):
                    if n >= 2:
                        pe.wait_ge(z["exped"], b * NS + n - 1)
                    r = tiles[j]
                    for e in range(2):
                        GC = EH * L
                        for g in range(c * half // GC + e * (HW // GC), c * half // GC + (e + 1) * (HW // GC)):
                            o = g * GC - c * half - e * HW
                            ins = nc.tensor.matmul(sc[n % 2][0:r, e * 512 + o:e * 512 + o + GC], KS[p][:, g, first[j]:first[j] + r],
                                                   QSw[p][:, g * GC:(g + 1) * GC], start=True, stop=True)
                        if e == 0:
                            between(3 * n)
                    ins.then_inc(z["ready"], 1)
                    between(3 * n + 1)
                    if n >= 1:
                        weigh(n - 1)
                    if prior:
                        finish(before(bt), n)
                    between(3 * n + 2)
                    if more and n == PACE // 3:
                        assert not scores
                        if prior:
                            pe.wait_ge(z["done"], b)
                        toprow(after(bt))
                weigh(NS - 1)

            def finish(bt, n):
                b = number(bt)
                if n == 1:
                    pe.wait_ge(z["saved"], b + 1)
                    if not isinstance(b, int) or b < B - 1:
                        pe.wait_ge(z["toprow16"], b + 2)
                    nc.tensor.matmul(px[:, 0:HG * L], sumof[:], U[:], start=True, stop=True).then_inc(z["summed"], 1)
                if n == STEP:
                    pe.wait_ge(z["normed"], b + 1)
                    for g in range(HG):
                        ins = nc.tensor.matmul(px[:, 0:L], outof[:, g, :], U[:, g * L:(g + 1) * L], start=(g == 0), stop=(g == HG - 1))
                    ins.then_inc(z["projected"], 1)
            for n in range(NM):
                score((0, 0), n)
            toprow((0, 0))
            attend((0, 0), True, False)
            with pe.Fori(0, last) as i:
                attend((i, 1), True, True)
                attend((i + 1, 0), True, True)
            attend((last, 1), False, True)
            for n in (1, STEP):
                finish((last, 1), n)

        @block.scalar
        def _(act):
            nc.scalar.preload_act_table_set("natural_log_exp_and_others")

            def invert(b):
                act.wait_ge(z["summed"], b + 1)
                nc.scalar.activation(R[:], px[:, 0:HG * L], ACT.Ln, scale=-1.0).then_inc(z["logged"], 1)
                act.wait_ge(z["logged"], b + 1)
                nc.scalar.activation(R[:], R[:], ACT.Exp, scale=-1.0).then_inc(z["inverted"], 1)

            def attend(bt, prior):
                b, p = number(bt), bt[1]
                for n, (j, c) in enumerate(steps):
                    act.wait_ge(z["ready"], b * NS + n + 1)
                    if n >= 2:
                        act.wait_ge(z["pved"], b * NS + n - 1)
                    r = tiles[j]
                    src = sc[n % 2][0:r, :].rearrange("s (e w) -> s e w", e=2)[:, :, 0:HW]
                    nc.scalar.activation(E[n % 2][0:r, :].rearrange("s (e w) -> s e w", e=2), src, ACT.Exp,
                                         bias=0.0 if own else biasT[0:r, j, bass.ds(b, 1)]).then_inc(z["exped"], 1)
                    if prior and n == 2:
                        invert(number(before(bt)))
            attend((0, 0), False)
            with act.Fori(0, last) as i:
                attend((i, 1), True)
                attend((i + 1, 0), True)
            attend((last, 1), True)
            invert(B - 1)

        @block.vector
        def _(dve):
            for p in range(2):
                nc.vector.memset(KS[p][KR:KR + 1], 1.0)
            nc.vector.memset(po[:], 0.0).then_inc(z["zeroed"], 1)
            dve.wait_ge(z["filled"], 1)

            def prepare(bt, prior):
                b, p = number(bt), bt[1]
                if prior is not None:
                    save(prior)
                for n in range(NM):
                    if prior is not None and n == MID:
                        divide(prior)
                    if prior is not None and n == END:
                        add(prior)
                    w, c = n // CK, n % CK
                    r = min(128, HQ - w * 128)
                    dve.wait_ge(z["scored"], b * NM + n + 1)
                    nc.vector.reduce_max(mx[0:r, w, c:c + 1], pm[n % 2][0:r, 0:min(KW, KEYS - c * KW)], AX).then_inc(z["maxed"], 1)
                dve.wait_ge(z["maxed"], (b + 1) * NM)
                full = HQ // 128
                ins = nc.vector.tensor_reduce(top[:, 0:full], mx[:, 0:full, :], AX, ALU.max)
                if HQ % 128:
                    ins = nc.vector.tensor_reduce(top[0:HQ % 128, full:NW], mx[0:HQ % 128, full:NW, :], AX, ALU.max)
                ins.then_inc(z["topped"], 1)
                dve.wait_ge(z["topped"], 2 * b + 1)
                nc.vector.tensor_scalar(top[:], top[:], -1.0, None, ALU.mult).then_inc(z["topped"], 1)
                dve.wait_ge(z["toprow"], b + 1)
                nc.vector.tensor_copy(top16[:], px[0:NW, 0:128]).then_inc(z["toprow16"], 1)

            def save(bt):
                dve.wait_ge(z["pved"], (number(bt) + 1) * NS)
                nc.vector.tensor_copy(U[:], po[:, 0:HG * L]).then_inc(z["saved"], 1)

            def divide(bt):
                b = number(bt)
                dve.wait_ge(z["inverted"], b + 1)
                nc.vector.tensor_tensor(R2[:], R[:], px[:, 0:HG * L], ALU.mult).then_inc(z["refined"], 1)
                dve.wait_ge(z["refined"], 2 * b + 1)
                nc.vector.scalar_tensor_tensor(out=R[:], in0=R2[:], scalar=2.0, in1=R[:], op0=ALU.add, op1=ALU.mult).then_inc(z["refined"], 1)
                dve.wait_ge(z["refined"], 2 * b + 2)
                nc.vector.tensor_tensor(U[:], U[:], R[:], ALU.mult).then_inc(z["normed"], 1)

            def add(bt):
                b = number(bt)
                dve.wait_ge(z["projected"], b + 1)
                x = xT[:, bass.ds(b * L, L)]
                nc.vector.scalar_tensor_tensor(out=x, in0=px[:, 0:L], scalar=bp[:], in1=x, op0=ALU.add, op1=ALU.add).then_inc(z["done"], 1)
            prepare((0, 0), None)
            prepare((0, 1), None)
            with dve.Fori(0, last) as i:
                prepare((i + 1, 0), (i, 0))
                prepare((i + 1, 1), (i, 1))
            for p in range(2):
                save((last, p)), divide((last, p)), add((last, p))
        main.close()


def l1_xattn(nc, k, a):
    cross(nc, k, a, "L1_xattn", 16, True)


def l2_xattn(nc, k, a):
    cross(nc, k, a, "L2_xattn", 16, True)


def l3_xattn(nc, k, a):
    cross(nc, k, a, "L3_xattn", 8, False)


def l3_ffn(nc, k, a, out):
    xT, phid, Wd = k["xT"], a["L3_ffn_phi"], a["L3_ffn_W"]
    NE, PS = phid.shape[1], phid.shape[2]
    SLOTS = NE * PS
    QS = 512
    NQ, SUB, EQ = SLOTS // QS, QS // 128, QS // PS
    EW = 128 // PS
    GB_ = 4
    D1 = D + 1
    pre = 2
    with ExitStack() as ctx:
        s = Stage(nc, ctx, "l3f")
        phi, phiS = s.sb("phi", [D, SLOTS]), s.sb("phiS", [D, QS])
        bias, one16, nrow = s.sb("bias", [128, NQ * SUB, D]), s.sb("one16", [1, 128], BF16), s.sb("nrow", [1, N], BF16)
        xtm = s.sb("xtm", [L, B, D])
        xs = [s.sb(f"xs{p}", [D, L]) for p in range(2)]
        bd = a["L3_ffn_b"].rearrange("(w e) d -> e w d", e=EW)
        load(nc, "l3fl", [(phi[:], phid.rearrange("d n p -> d (n p)"))]
             + [(bias[e * PS:(e + 1) * PS], bd[e:e + 1].to_broadcast([PS, NQ * SUB, D])) for e in range(EW)])

        with ExitStack() as first:
            t = Stage(nc, first, "l3m")
            phi16, xs16 = t.sb("phi16", [D, SLOTS], BF16), [t.sb(f"xs16{p}", [D, L], BF16) for p in range(2)]
            mx, neg, negr = t.sb("mx", [L, 2, B]), t.sb("neg", [L, B]), t.sb("negr", [B, L], BF16)
            pl, pt = [t.ps(f"pl{h}", (128, 1024)) for h in range(2)], [t.ps(f"pt{p}") for p in range(2)]
            phid16, staged, staged16, turned, kept, scored, maxed, c, rowed, held = [t.sem(n) for n in
                ("phied", "staged", "staged16", "turned", "kept", "scored", "maxed", "c", "rowed", "held")]
            with nc.Block() as block:
                @block.gpsimd
                def _(pool):
                    nc.gpsimd.memset(one16[:], 1.0)
                    with pool.Fori(0, B // 2) as i:
                        for p in range(2):
                            b = 2 * i + p
                            pool.wait_ge(scored, 2 * (b + 1))
                            pool.sem_inc(held, 1)
                            nc.gpsimd.tensor_copy(xs[p][:], xT[:, bass.ds(b * L, L)]).then_inc(staged, 1)
                            nc.gpsimd.tensor_copy(xs16[p][:], xT[:, bass.ds(b * L, L)]).then_inc(staged16, 1)

                @block.tensor
                def _(pe):
                    pe.sem_inc(scored, 4)
                    pe.wait_ge(phid16, 1)
                    with pe.Fori(0, B // 2) as i:
                        for p in range(2):
                            b = 2 * i + p
                            pe.wait_ge(kept, b + 1)
                            pe.wait_ge(staged16, b + 1)
                            nc.tensor.transpose(pt[p][0:L, 0:D], xs[p][:], k["ident"][:]).then_inc(turned, 1)
                            for h in range(2):
                                pe.wait_ge(maxed, 2 * b + h + 1)
                                for w in range(2):
                                    ins = nc.tensor.matmul(pl[h][0:L, w * 512:(w + 1) * 512], xs16[p][:],
                                                           phi16[:, (2 * h + w) * 512:(2 * h + w + 1) * 512], start=True, stop=True)
                                ins.then_inc(scored, 1)
                    pe.wait_ge(kept, B + 2)
                    pe.wait_ge(c, 2)
                    nc.tensor.transpose(pt[0][0:B, 0:L], neg[:], k["ident"][0:L, 0:L]).then_inc(c, 1)

                @block.scalar
                def _(act):
                    nc.scalar.activation(phi16[:], phi[:], ACT.Copy).then_inc(phid16, 1)
                    act.sem_inc(kept, 2)
                    with act.Fori(0, B // 2) as i:
                        for p in range(2):
                            b = 2 * i + p
                            act.wait_ge(turned, b + 1)
                            nc.scalar.activation(xtm[:, bass.ds(b, 1), :].rearrange("t o d -> t (o d)"), pt[p][0:L, 0:D],
                                                 ACT.Copy).then_inc(kept, 1)

                @block.vector
                def _(dve):
                    dve.sem_inc(maxed, 2)
                    with dve.Fori(0, B // 2) as i:
                        for p in range(2):
                            b = 2 * i + p
                            for h in range(2):
                                dve.wait_ge(scored, 2 * b + h + 5)
                                nc.vector.reduce_max(mx[:, h, bass.ds(b, 1)], pl[h][0:L, :], AX).then_inc(maxed, 1)
                    dve.wait_ge(maxed, 2 * B + 2)
                    nc.vector.tensor_tensor(neg[:], mx[:, 0, :], mx[:, 1, :], ALU.max).then_inc(c, 1)
                    dve.wait_ge(c, 1)
                    nc.vector.tensor_scalar(neg[:], neg[:], -1.0, None, ALU.mult).then_inc(c, 1)
                    dve.wait_ge(c, 3)
                    nc.vector.tensor_copy(negr[:], pt[0][0:B, 0:L]).then_inc(c, 1)

                @block.sync
                def _(sp):
                    sp.wait_ge(c, 4)
                    sp.dma_start(nrow[:], negr[:]).then_inc(rowed, 16)
                    sp.wait_ge(rowed, 16)

        acc, LG, W = s.sb("acc", [L, B, D1]), s.sb("LG", [L, B, QS]), s.sb("W", [D, EQ, D])
        M, Z = s.sb("M", [L, QS]), s.sb("Z", [L, QS])
        xt, dn = [s.sb(f"xt{p}", [L, D]) for p in range(2)], [s.sb(f"dn{p}", [L, QS]) for p in range(2)]
        st, y1 = [s.sb(f"st{p}", [D, QS]) for p in range(2)], [s.sb(f"y1{p}", [128, SUB, D1]) for p in range(2)]
        Cs = [s.sb(f"Cs{p}", [128, SUB, L]) for p in range(2)]
        bA, bY, bC, bO = [[s.ps(f"{n}{p}") for p in range(2)] for n in ("bA", "bY", "bC", "bO")]
        z = {n: s.sem(n) for n in ("loadedW", "phied", "staged", "logited", "kept", "maxed", "subbed", "exped", "summed", "logged", "inverted",
                                   "dispatched", "slotted", "slotsT", "clogged", "cexped", "yed", "ycopied", "outed", "added",
                                   "ones", "held")}
        main = ExitStack()
        block = main.enter_context(nc.Block())
        NP = B // GB_

        @block.sync
        def _(sp):
            with sp.Fori(0, NQ) as q:
                sp.wait_ge(z["yed"], B * q + pre)
                sp.sem_inc(z["held"], 1)
                for e in range(EQ):
                    sp.dma_start(W[:, e, :], Wd[bass.ds(q * EQ + e, 1)].rearrange("n d e -> d (n e)")).then_inc(z["loadedW"], 16)

        @block.gpsimd
        def _(pool):
            for p in range(2):
                ins = nc.gpsimd.memset(y1[p][:], 1.0)
            ins.then_inc(z["ones"], 1)
            pool.sem_inc(z["dispatched"], pre)
            with pool.Fori(0, NQ) as q:
                with pool.Fori(0, B // 2) as i:
                    for p in range(2):
                        pool.wait_ge(z["logited"], B * q + 2 * i + p + 1)
                        pool.sem_inc(z["held"], 1)
                        nc.gpsimd.tensor_copy(xs[p][:], xT[:, bass.ds((2 * i + p) * L, L)]).then_inc(z["staged"], 1)
                pool.wait_ge(z["inverted"], q + 1)
                pool.sem_inc(z["held"], 1)
                with pool.Fori(0, B // 2) as i:
                    for p in range(2):
                        pool.wait_ge(z["slotted"], B * q + 2 * i + p + 1)
                        pool.sem_inc(z["held"], 1)
                        nc.gpsimd.tensor_copy(xt[p][:], xtm[:, bass.ds(2 * i + p, 1), :].rearrange("t o d -> t (o d)"))
                        nc.gpsimd.tensor_tensor(dn[p][:], LG[:, bass.ds(2 * i + p, 1), :].rearrange("t o s -> t (o s)"), Z[:],
                                                ALU.mult).then_inc(z["dispatched"], 1)

        @block.tensor
        def _(pe):
            for n in ("logited", "slotted", "clogged", "yed", "outed"):
                pe.sem_inc(z[n], pre)
            pe.wait_ge(z["ones"], 1)
            with pe.Fori(0, NQ) as q:
                pe.wait_ge(z["phied"], q + 1)
                pe.wait_ge(z["slotsT"], B * q + pre)
                pe.sem_inc(z["held"], 1)
                with pe.Fori(0, B // 2) as i:
                    for p in range(2):
                        n = B * q + 2 * i + p
                        pe.wait_ge(z["kept"], n + 1)
                        pe.wait_ge(z["staged"], n + 1)
                        nc.tensor.matmul(bA[p][0:L, :], xs[p][:], phiS[:], start=True, stop=True).then_inc(z["logited"], 1)
                pe.wait_ge(z["ycopied"], B * q + pre)
                for g in range(NP):
                    pe.wait_ge(z["exped"], NP * q + g + 1)
                    for b in range(g * GB_, (g + 1) * GB_):
                        ins = nc.tensor.matmul(bY[0][0:L, :], k["ident"][0:L, 0:L], LG[:, b, :], start=(b == 0), stop=(b == B - 1))
                ins.then_inc(z["summed"], 1)
                pe.wait_ge(z["loadedW"], 16 * EQ * q + 16 * EQ)
                pe.sem_inc(z["held"], 1)
                with pe.Fori(0, B // 2) as i:
                    for p in range(2):
                        b, n = 2 * i + p, B * q + 2 * i + p
                        pe.wait_ge(z["dispatched"], n + 1 + pre)
                        pe.wait_ge(z["slotsT"], n + 1)
                        nc.tensor.matmul(bA[p][:], xt[p][:], dn[p][:], start=True, stop=True).then_inc(z["slotted"], 1)
                        pe.wait_ge(z["cexped"], n + 1)
                        nc.tensor.matmul(bC[p][:, 0:SUB * L], one16[:], nrow[:, bass.ds(b * L, L)].unsqueeze(1).to_broadcast([1, SUB, L]),
                                         start=True, stop=False, skip_group_check=True)
                        for w in range(SUB):
                            ins = nc.tensor.matmul(bC[p][:, w * L:(w + 1) * L], phiS[:, w * 128:(w + 1) * 128],
                                                   xT[:, bass.ds(b * L, L)], start=False, stop=True, skip_group_check=True)
                        ins.then_inc(z["clogged"], 1)
                    for p in range(2):
                        n = B * q + 2 * i + p
                        pe.wait_ge(z["slotsT"], n + 1 + pre)
                        pe.wait_ge(z["ycopied"], n + 1)
                        for w in range(SUB):
                            for e in range(EW):
                                m = w * EW + e
                                ins = nc.tensor.matmul(bY[p][e * PS:(e + 1) * PS, w * D:(w + 1) * D], st[p][:, m * PS:(m + 1) * PS],
                                                       W[:, m, :], start=True, stop=True, tile_position=(0, e * PS))
                        ins.then_inc(z["yed"], 1)
                    for p in range(2):
                        n = B * q + 2 * i + p
                        pe.wait_ge(z["ycopied"], n + 1 + pre)
                        pe.wait_ge(z["cexped"], n + 1 + pre)
                        pe.wait_ge(z["added"], n + 1)
                        for w in range(SUB):
                            ins = nc.tensor.matmul(bO[p][0:L, 0:D1], Cs[p][:, w, :], y1[p][:, w, :], start=(w == 0), stop=(w == SUB - 1))
                        ins.then_inc(z["outed"], 1)

        @block.scalar
        def _(act):
            nc.scalar.preload_act_table_set("natural_log_exp_and_others")
            for n in ("kept", "cexped"):
                act.sem_inc(z[n], pre)
            with act.Fori(0, NQ) as q:
                act.wait_ge(z["clogged"], B * q + pre)
                nc.scalar.activation(phiS[:], phi[:, bass.ds(q * QS, QS)], ACT.Copy).then_inc(z["phied"], 1)
                act.wait_ge(z["dispatched"], B * q + pre)
                act.sem_inc(z["held"], 1)
                with act.Fori(0, B // 2) as i:
                    for p in range(2):
                        act.wait_ge(z["logited"], B * q + 2 * i + p + 1 + pre)
                        nc.scalar.activation(LG[:, bass.ds(2 * i + p, 1), :].rearrange("t o s -> t (o s)"), bA[p][0:L, :],
                                             ACT.Copy).then_inc(z["kept"], 1)
                with act.Fori(0, NP) as g:
                    act.wait_ge(z["subbed"], NP * q + g + 1)
                    piece = LG[:, bass.ds(GB_ * g, GB_), :]
                    nc.scalar.activation(piece, piece, ACT.Exp).then_inc(z["exped"], 1)
                with act.Fori(0, B // 2) as i:
                    for p in range(2):
                        n = B * q + 2 * i + p
                        act.wait_ge(z["outed"], n + 1)
                        act.wait_ge(z["clogged"], n + 1 + pre)
                        nc.scalar.activation(Cs[p][:].rearrange("s w t -> s (w t)"), bC[p][:, 0:SUB * L], ACT.Exp).then_inc(z["cexped"], 1)

        @block.vector
        def _(dve):
            for n in ("slotsT", "ycopied", "added"):
                dve.sem_inc(z[n], pre)
            dve.sem_inc(z["maxed"], 1)
            nc.vector.memset(acc[:], 0.0).then_inc(z["maxed"], 1)
            with dve.Fori(0, NQ) as q:
                dve.wait_ge(z["maxed"], (B + 1) * q + 2)
                nc.vector.memset(M[:], -3.0e38).then_inc(z["maxed"], 1)
                with dve.Fori(0, B // 2) as i:
                    for p in range(2):
                        n = B * q + 2 * i + p
                        dve.wait_ge(z["kept"], n + 1 + pre)
                        dve.wait_ge(z["maxed"], n + q + 3)
                        nc.vector.tensor_tensor(M[:], M[:], LG[:, bass.ds(2 * i + p, 1), :].rearrange("t o s -> t (o s)"),
                                                ALU.max).then_inc(z["maxed"], 1)
                dve.wait_ge(z["maxed"], (B + 1) * q + B + 3)
                dve.sem_inc(z["held"], 1)
                with dve.Fori(0, NP) as g:
                    piece = LG[:, bass.ds(GB_ * g, GB_), :]
                    nc.vector.tensor_tensor(piece, piece, M[:].unsqueeze(1).to_broadcast([L, GB_, QS]), ALU.subtract).then_inc(z["subbed"], 1)
                dve.wait_ge(z["subbed"], NP * q + NP)
                dve.wait_ge(z["summed"], q + 1)
                dve.wait_ge(z["dispatched"], B * q + pre)
                nc.vector.reciprocal(Z[:], bY[0][0:L, :]).then_inc(z["inverted"], 1)
                with dve.Fori(0, B // 2) as i:
                    for p in range(2):
                        n = B * q + 2 * i + p
                        dve.wait_ge(z["slotted"], n + 1 + pre)
                        dve.wait_ge(z["yed"], n + 1)
                        nc.vector.tensor_copy(st[p][:], bA[p][:]).then_inc(z["slotsT"], 1)
                    for p in range(2):
                        n = B * q + 2 * i + p
                        dve.wait_ge(z["yed"], n + 1 + pre)
                        dve.wait_ge(z["outed"], n + 1)
                        nc.vector.tensor_tensor(y1[p][:, :, 0:D], bY[p][:].rearrange("s (w d) -> s w d", d=D),
                                                bias[:, bass.ds(q * SUB, SUB), :], ALU.add).then_inc(z["ycopied"], 1)
                    for p in range(2):
                        b, n = 2 * i + p, B * q + 2 * i + p
                        dve.wait_ge(z["outed"], n + 1 + pre)
                        dve.wait_ge(z["added"], n + 1)
                        dst = acc[:, bass.ds(b, 1), :].rearrange("t o d -> t (o d)")
                        nc.vector.tensor_tensor(dst, dst, bO[p][0:L, 0:D1], ALU.add).then_inc(z["added"], 1)

        main.close()
        half = B // 2
        c, rooted, stored = s.sem("c"), s.sem("rooted"), s.sem("stored")
        rec, mean, var = s.sb("rec", [L, B]), s.sb("mean", [L, B]), s.sb("var", [L, B])
        wide = LG[:, :, 0:D]
        block = ctx.enter_context(nc.Block())

        @block.vector
        def _(dve):
            at = [0]

            def link(ins):
                at[0] += 1
                ins.then_inc(c, 1)
                dve.wait_ge(c, at[0])
            wide_b = lambda t: t[:].unsqueeze(2).to_broadcast([L, B, D])
            link(nc.vector.reciprocal(rec[:], acc[:, :, D]))
            link(nc.vector.tensor_tensor(acc[:, :, 0:D], acc[:, :, 0:D], wide_b(rec), ALU.mult))
            link(nc.vector.tensor_tensor(xtm[:], xtm[:], acc[:, :, 0:D], ALU.add))
            link(nc.vector.tensor_reduce(mean[:], xtm[:], AX, ALU.add))
            link(nc.vector.tensor_scalar(mean[:], mean[:], 1.0 / D, None, ALU.mult))
            link(nc.vector.tensor_tensor(xtm[:], xtm[:], wide_b(mean), ALU.subtract))
            link(nc.vector.tensor_tensor(wide, xtm[:], xtm[:], ALU.mult))
            link(nc.vector.tensor_reduce(var[:], wide, AX, ALU.add))
            dve.wait_ge(rooted, 2)
            for h in range(2):
                bs = slice(h * half, (h + 1) * half)
                nc.vector.tensor_tensor(xtm[:, bs], xtm[:, bs], var[:, bs].unsqueeze(2).to_broadcast([L, half, D]), ALU.mult).then_inc(c, 1)

        @block.scalar
        def _(act):
            nc.scalar.preload_act_table_set("natural_log_exp_and_others")
            act.wait_ge(c, 8)
            nc.scalar.activation(var[:], var[:], ACT.Ln, scale=1.0 / D, bias=k["eps"][0:L]).then_inc(rooted, 1)
            act.wait_ge(rooted, 1)
            nc.scalar.activation(var[:], var[:], ACT.Exp, scale=-0.5).then_inc(rooted, 1)

        @block.sync
        def _(sp):
            for h in range(2):
                bs = slice(h * half, (h + 1) * half)
                sp.wait_ge(c, 9 + h)
                sp.dma_start(out[bs].rearrange("b t d -> t b d"), xtm[:, bs]).then_inc(stored, 16)
            sp.wait_ge(stored, 32)


def decoder(nc, a, out):
    with ExitStack() as ctx:
        k = setup(nc, ctx)
        rows = a["x"].rearrange("b t d -> (b t) d")
        load_transposed(nc, k, "x", [(k["xT"][:, n * 128:(n + 1) * 128], rows[n * 128:(n + 1) * 128, :]) for n in range(N // 128)])
        for n, layer in enumerate((l0_attn, l0_xattn, l0_ffn, l1_attn, l1_xattn, l1_ffn, l2_attn, l2_xattn, l2_ffn,
                                   l3_attn, l3_xattn)):
            if layer is l1_xattn:
                split_keys(nc, k, a)
            layer(nc, k, a)
            norm_pass(nc, k, f"norm{n}")
        l3_ffn(nc, k, a, out)


def kernel(**inputs):
    import concourse.bacc as bacc
    from concourse.bass_utils import run_bass_kernel_spmd

    nc = bacc.Bacc("TRN2", target_bir_lowering=False, num_devices=1)
    arrays, a = {}, {}
    for name, value in inputs.items():
        value = np.ascontiguousarray(value)
        arrays[f"in_{name}_dram"] = value
        a[name] = nc.dram_tensor(f"in_{name}_dram", value.shape, mybir.dt.from_np(value.dtype), kind="ExternalInput").ap()
    out = nc.dram_tensor("out_0_dram", (B, L, D), F32, kind="ExternalOutput").ap()
    decoder(nc, a, out)
    return run_bass_kernel_spmd(nc, [arrays], core_ids=[0]).results[0]["out_0_dram"]
```
